# Optimizing a Trainium2 kernel written in Bass

```python
import numpy as np
import jax
import jax.numpy as jnp

def _softmax(x, axis=-1):
    return jax.nn.softmax(x, axis=axis)

def _gelu(x):
    return jax.nn.gelu(x, approximate=True)

def _silu(x):
    return jax.nn.silu(x)

def _sigmoid(x):
    return jax.nn.sigmoid(x)

def _layernorm(x, axis=-1, eps=1e-05):
    m = jnp.mean(x, axis=axis, keepdims=True)
    v = jnp.var(x, axis=axis, keepdims=True)
    return (x - m) / jnp.sqrt(v + eps)

def _scatter_add(tgt, idx, src, axis=0):
    return tgt.at[idx].add(src)

def _segment_sum(src, seg, n):
    return jax.ops.segment_sum(src, seg, n)
kernel_name = 'mk_gnn_preln_d4_gnn_r16_18b6f2'

def setup_inputs(seed: int=0):
    np.random.seed(seed)
    _w = jnp.asarray

    def _rec_inputs():
        import jax
        import jax.numpy as jnp
        _gk = jax.random.key(seed)
        x = -0.000202 + 1 * jax.random.normal(jax.random.fold_in(_gk, 1), (3125, 128), jnp.float32)
        src = jax.random.randint(jax.random.fold_in(_gk, 2), (100000,), 0, 3125, jnp.int32)
        dst = jnp.minimum((3125 * jax.random.uniform(jax.random.fold_in(_gk, 3), (100000,)) ** 2.0).astype(jnp.int32), 49999)
        _o = jnp.argsort(dst, stable=True)
        src = src[_o]
        dst = dst[_o]
        edge_attr_16 = 0.00028786 + 0.999816 * jax.random.normal(jax.random.fold_in(_gk, 12), (100000, 16), jnp.float32)
        edge_type_8 = jax.random.randint(jax.random.fold_in(_gk, 14), (100000,), 0, 8, jnp.int32)
        edge_weight = jax.random.uniform(jax.random.fold_in(_gk, 15), (100000,), jnp.float32, 0.0, 0.999998)
        return (x, src, dst, edge_attr_16, edge_type_8, edge_weight)
    x, src, dst, edge_attr_16, edge_type_8, edge_weight = _rec_inputs()

    def _L0_gnn_setup():
        import jax, jax.numpy as jnp
        import numpy as np
        N_NODES = 3125
        N_EDGES = 100000
        IN_DIM = 128
        HEADS = 8
        OUT_C = 16
        NEG_SLOPE = 0.2
        BN_EPS = 1e-05
        key = jax.random.key(seed)
        ks = jax.random.split(key, 8)
        x = jax.random.normal(ks[0], (N_NODES, IN_DIM), dtype=jnp.float32)
        edge_index = jax.random.randint(ks[1], (2, N_EDGES), 0, N_NODES, dtype=jnp.int64)
        W = jax.random.normal(ks[2], (IN_DIM, HEADS * OUT_C), dtype=jnp.float32) / np.sqrt(IN_DIM)
        att_src = jax.random.normal(ks[3], (HEADS, OUT_C), dtype=jnp.float32) / np.sqrt(OUT_C)
        att_dst = jax.random.normal(ks[4], (HEADS, OUT_C), dtype=jnp.float32) / np.sqrt(OUT_C)
        bias = jnp.zeros((HEADS * OUT_C,), dtype=jnp.float32)
        gamma = jnp.ones((HEADS * OUT_C,), dtype=jnp.float32)
        beta = jnp.zeros((HEADS * OUT_C,), dtype=jnp.float32)
        return {'x': x, 'edge_index': edge_index, 'W': W, 'att_src': att_src, 'att_dst': att_dst, 'bias': bias, 'gamma': gamma, 'beta': beta}
    _L0_gnn_all = _L0_gnn_setup()
    _L0_gnn_in = {k: v for k, v in _L0_gnn_all.items() if k in ('W', 'att_src', 'att_dst', 'bias', 'gamma', 'beta')}
    del _L0_gnn_all

    def _L1_gnn_setup():
        import jax, jax.numpy as jnp
        import numpy as np
        N_NODES = 3125
        N_EDGES = 50000
        IN_DIM = 128
        H_DIM = 128
        NUM_RELS = 8

        def _rel_graph_conv(x, src, dst, etypes, norm, comp, V, bias):
            W = jnp.einsum('rb,bio->rio', comp, V)
            H = jnp.einsum('ni,rio->nro', x, W)
            m = H[src, etypes] * norm
            agg = jax.ops.segment_sum(m, dst, num_segments=x.shape[0])
            return agg + bias
        key = jax.random.key(seed)
        ks = jax.random.split(key, 10)
        s_in = 1.0 / np.sqrt(IN_DIM)
        s_h = 1.0 / np.sqrt(H_DIM)
        return {'features': jax.random.normal(ks[0], (N_NODES, IN_DIM), jnp.float32), 'etypes': jax.random.randint(ks[1], (N_EDGES,), 0, NUM_RELS), 'edge_weight': jax.random.uniform(ks[2], (N_EDGES,), jnp.float32), 'src': jax.random.randint(ks[3], (N_EDGES,), 0, N_NODES), 'dst': jax.random.randint(ks[4], (N_EDGES,), 0, N_NODES), 'comp1': jax.random.normal(ks[5], (NUM_RELS, NUM_RELS), jnp.float32) * (1.0 / NUM_RELS), 'V1': jax.random.normal(ks[6], (NUM_RELS, IN_DIM, H_DIM), jnp.float32) * s_in, 'bias1': jnp.zeros((H_DIM,), jnp.float32), 'comp2': jax.random.normal(ks[7], (NUM_RELS, NUM_RELS), jnp.float32) * (1.0 / NUM_RELS), 'V2': jax.random.normal(ks[8], (NUM_RELS, H_DIM, H_DIM), jnp.float32) * s_h, 'bias2': jnp.zeros((H_DIM,), jnp.float32)}
    _L1_gnn_all = _L1_gnn_setup()
    _L1_gnn_in = {k: v for k, v in _L1_gnn_all.items() if k in ('comp1', 'V1', 'bias1', 'comp2', 'V2', 'bias2')}
    del _L1_gnn_all

    def _L2_gnn_setup():
        import jax, jax.numpy as jnp
        import numpy as np
        N = 625
        E = 10000
        D = 128
        H = 4
        C = 128
        HC = H * C
        EPS_SOFTMAX = 1e-16
        EPS_NORM = 1e-05
        key = jax.random.key(seed)
        ks = jax.random.split(key, 12)
        s = 1.0 / np.sqrt(D)
        sb = 1.0 / np.sqrt(3 * D)
        return {'x': jax.random.normal(ks[0], (N, D), jnp.float32), 'edge_index': jax.random.randint(ks[1], (2, E), 0, N, dtype=jnp.int64), 'Wq': jax.random.normal(ks[2], (D, HC), jnp.float32) * s, 'bq': jnp.zeros((HC,), jnp.float32), 'Wk': jax.random.normal(ks[3], (D, HC), jnp.float32) * s, 'bk': jnp.zeros((HC,), jnp.float32), 'Wv': jax.random.normal(ks[4], (D, HC), jnp.float32) * s, 'bv': jnp.zeros((HC,), jnp.float32), 'Wskip': jax.random.normal(ks[5], (D, D), jnp.float32) * s, 'bskip': jnp.zeros((D,), jnp.float32), 'Wbeta': jax.random.normal(ks[6], (3 * D,), jnp.float32) * sb, 'gn_weight': jnp.ones((D,), jnp.float32), 'gn_bias': jnp.zeros((D,), jnp.float32), 'gn_mean_scale': jnp.ones((D,), jnp.float32)}
    _L2_gnn_all = _L2_gnn_setup()
    _L2_gnn_in = {k: v for k, v in _L2_gnn_all.items() if k in ('Wq', 'bq', 'Wk', 'bk', 'Wv', 'bv', 'Wskip', 'bskip', 'Wbeta', 'gn_weight', 'gn_bias', 'gn_mean_scale')}
    del _L2_gnn_all

    def _L3_gnn_setup():
        import jax, jax.numpy as jnp
        import numpy as np
        BN_EPS = 1e-05

        def _bn(x, gamma, beta):
            m = jnp.mean(x, axis=0)
            v = jnp.var(x, axis=0)
            return (x - m) * jax.lax.rsqrt(v + BN_EPS) * gamma + beta
        key = jax.random.key(seed)
        ks = jax.random.split(key, 12)
        N, E, D, ED = (3125, 37500, 128, 16)
        s = lambda k, sh: jax.random.normal(k, sh, dtype=jnp.float32) * 0.05
        return {'h': jax.random.normal(ks[0], (N, D), dtype=jnp.float32), 'edge_index': jax.random.randint(ks[1], (2, E), 0, N, dtype=jnp.int64), 'edge_attr': jax.random.normal(ks[2], (E, ED), dtype=jnp.float32), 'ee_w1': s(ks[3], (ED, D)), 'ee_b1': jnp.zeros((D,), jnp.float32), 'ee_g1': jnp.ones((D,), jnp.float32), 'ee_bb1': jnp.zeros((D,), jnp.float32), 'ee_w2': s(ks[4], (D, D)), 'ee_b2': jnp.zeros((D,), jnp.float32), 'mlp_w1': s(ks[5], (D, D)), 'mlp_b1': jnp.zeros((D,), jnp.float32), 'mlp_g1': jnp.ones((D,), jnp.float32), 'mlp_bb1': jnp.zeros((D,), jnp.float32), 'mlp_w2': s(ks[6], (D, D)), 'mlp_b2': jnp.zeros((D,), jnp.float32), 'mlp_g2': jnp.ones((D,), jnp.float32), 'mlp_bb2': jnp.zeros((D,), jnp.float32)}
    _L3_gnn_all = _L3_gnn_setup()
    _L3_gnn_in = {k: v for k, v in _L3_gnn_all.items() if k in ('ee_w1', 'ee_b1', 'ee_g1', 'ee_bb1', 'ee_w2', 'ee_b2', 'mlp_w1', 'mlp_b1', 'mlp_g1', 'mlp_bb1', 'mlp_w2', 'mlp_b2', 'mlp_g2', 'mlp_bb2')}
    del _L3_gnn_all
    return {'x': x, 'src': src, 'dst': dst, 'edge_attr_16': edge_attr_16, 'edge_type_8': edge_type_8, 'edge_weight': edge_weight, 'L0_gnn_W': _L0_gnn_in['W'], 'L0_gnn_att_src': _L0_gnn_in['att_src'], 'L0_gnn_att_dst': _L0_gnn_in['att_dst'], 'L0_gnn_bias': _L0_gnn_in['bias'], 'L0_gnn_gamma': _L0_gnn_in['gamma'], 'L0_gnn_beta': _L0_gnn_in['beta'], 'L1_gnn_comp1': _L1_gnn_in['comp1'], 'L1_gnn_V1': _L1_gnn_in['V1'], 'L1_gnn_bias1': _L1_gnn_in['bias1'], 'L1_gnn_comp2': _L1_gnn_in['comp2'], 'L1_gnn_V2': _L1_gnn_in['V2'], 'L1_gnn_bias2': _L1_gnn_in['bias2'], 'L2_gnn_Wq': _L2_gnn_in['Wq'], 'L2_gnn_bq': _L2_gnn_in['bq'], 'L2_gnn_Wk': _L2_gnn_in['Wk'], 'L2_gnn_bk': _L2_gnn_in['bk'], 'L2_gnn_Wv': _L2_gnn_in['Wv'], 'L2_gnn_bv': _L2_gnn_in['bv'], 'L2_gnn_Wskip': _L2_gnn_in['Wskip'], 'L2_gnn_bskip': _L2_gnn_in['bskip'], 'L2_gnn_Wbeta': _L2_gnn_in['Wbeta'], 'L2_gnn_gn_weight': _L2_gnn_in['gn_weight'], 'L2_gnn_gn_bias': _L2_gnn_in['gn_bias'], 'L2_gnn_gn_mean_scale': _L2_gnn_in['gn_mean_scale'], 'L3_gnn_ee_w1': _L3_gnn_in['ee_w1'], 'L3_gnn_ee_b1': _L3_gnn_in['ee_b1'], 'L3_gnn_ee_g1': _L3_gnn_in['ee_g1'], 'L3_gnn_ee_bb1': _L3_gnn_in['ee_bb1'], 'L3_gnn_ee_w2': _L3_gnn_in['ee_w2'], 'L3_gnn_ee_b2': _L3_gnn_in['ee_b2'], 'L3_gnn_mlp_w1': _L3_gnn_in['mlp_w1'], 'L3_gnn_mlp_b1': _L3_gnn_in['mlp_b1'], 'L3_gnn_mlp_g1': _L3_gnn_in['mlp_g1'], 'L3_gnn_mlp_bb1': _L3_gnn_in['mlp_bb1'], 'L3_gnn_mlp_w2': _L3_gnn_in['mlp_w2'], 'L3_gnn_mlp_b2': _L3_gnn_in['mlp_b2'], 'L3_gnn_mlp_g2': _L3_gnn_in['mlp_g2'], 'L3_gnn_mlp_bb2': _L3_gnn_in['mlp_bb2']}

def reference(x, src, dst, edge_attr_16, edge_type_8, edge_weight, L0_gnn_W, L0_gnn_att_src, L0_gnn_att_dst, L0_gnn_bias, L0_gnn_gamma, L0_gnn_beta, L1_gnn_comp1, L1_gnn_V1, L1_gnn_bias1, L1_gnn_comp2, L1_gnn_V2, L1_gnn_bias2, L2_gnn_Wq, L2_gnn_bq, L2_gnn_Wk, L2_gnn_bk, L2_gnn_Wv, L2_gnn_bv, L2_gnn_Wskip, L2_gnn_bskip, L2_gnn_Wbeta, L2_gnn_gn_weight, L2_gnn_gn_bias, L2_gnn_gn_mean_scale, L3_gnn_ee_w1, L3_gnn_ee_b1, L3_gnn_ee_g1, L3_gnn_ee_bb1, L3_gnn_ee_w2, L3_gnn_ee_b2, L3_gnn_mlp_w1, L3_gnn_mlp_b1, L3_gnn_mlp_g1, L3_gnn_mlp_bb1, L3_gnn_mlp_w2, L3_gnn_mlp_b2, L3_gnn_mlp_g2, L3_gnn_mlp_bb2):
    import jax
    import jax.numpy as jnp

    def _L0_gnn_ref(x, edge_index, W, att_src, att_dst, bias, gamma, beta):
        import jax, jax.numpy as jnp
        import numpy as np
        N_NODES = 3125
        N_EDGES = 100000
        IN_DIM = 128
        HEADS = 8
        OUT_C = 16
        NEG_SLOPE = 0.2
        BN_EPS = 1e-05
        N = x.shape[0]
        H, C = att_src.shape
        src, dst = (edge_index[0], edge_index[1])
        xl = (x @ W).reshape(N, H, C)
        a_src = jnp.sum(xl * att_src[None], axis=-1)
        a_dst = jnp.sum(xl * att_dst[None], axis=-1)
        e = jax.nn.leaky_relu(a_src[src] + a_dst[dst], NEG_SLOPE)
        m = jax.ops.segment_max(e, dst, num_segments=N)
        m = jnp.where(jnp.isfinite(m), m, 0.0)
        ex = jnp.exp(e - m[dst])
        denom = jax.ops.segment_sum(ex, dst, num_segments=N)
        alpha = ex / (denom[dst] + 1e-16)
        out = jax.ops.segment_sum(alpha[:, :, None] * xl[src], dst, num_segments=N)
        h = out.reshape(N, H * C) + bias
        mean = jnp.mean(h, axis=0)
        var = jnp.mean((h - mean) ** 2, axis=0)
        h = (h - mean) * jax.lax.rsqrt(var + BN_EPS) * gamma + beta
        h = jax.nn.relu(h)
        return x + h

    def _L1_gnn_ref(features, etypes, edge_weight, src, dst, comp1, V1, bias1, comp2, V2, bias2):
        import jax, jax.numpy as jnp
        import numpy as np
        N_NODES = 3125
        N_EDGES = 50000
        IN_DIM = 128
        H_DIM = 128
        NUM_RELS = 8

        def _rel_graph_conv(x, src, dst, etypes, norm, comp, V, bias):
            W = jnp.einsum('rb,bio->rio', comp, V)
            H = jnp.einsum('ni,rio->nro', x, W)
            m = H[src, etypes] * norm
            agg = jax.ops.segment_sum(m, dst, num_segments=x.shape[0])
            return agg + bias
        norm = edge_weight[:, None]
        h = _rel_graph_conv(features, src, dst, etypes, norm, comp1, V1, bias1)
        h = jax.nn.relu(h)
        h = _rel_graph_conv(h, src, dst, etypes, norm, comp2, V2, bias2)
        return h

    def _L2_gnn_ref(x, edge_index, Wq, bq, Wk, bk, Wv, bv, Wskip, bskip, Wbeta, gn_weight, gn_bias, gn_mean_scale):
        import jax, jax.numpy as jnp
        import numpy as np
        N = 625
        E = 10000
        D = 128
        H = 4
        C = 128
        HC = H * C
        EPS_SOFTMAX = 1e-16
        EPS_NORM = 1e-05
        n = x.shape[0]
        src, dst = (edge_index[0], edge_index[1])
        q = (x @ Wq + bq).reshape(n, H, C)
        k = (x @ Wk + bk).reshape(n, H, C)
        v = (x @ Wv + bv).reshape(n, H, C)
        alpha = jnp.einsum('ehc,ehc->eh', q[dst], k[src]) / jnp.sqrt(jnp.float32(C))
        amax = jax.ops.segment_max(alpha, dst, num_segments=n)
        amax = jnp.where(jnp.isfinite(amax), amax, 0.0)
        ex = jnp.exp(alpha - amax[dst])
        denom = jax.ops.segment_sum(ex, dst, num_segments=n)
        attn = ex / (denom[dst] + EPS_SOFTMAX)
        msgs = attn[:, :, None] * v[src]
        out = jax.ops.segment_sum(msgs, dst, num_segments=n)
        out = out.mean(axis=1)
        skip = x @ Wskip + bskip
        beta = jax.nn.sigmoid(jnp.concatenate([out, skip, out - skip], axis=-1) @ Wbeta)
        beta = beta[:, None]
        out = beta * skip + (1.0 - beta) * out
        mean = out.mean(axis=0)
        centered = out - gn_mean_scale * mean
        var = (centered * centered).mean(axis=0)
        out = gn_weight * centered / jnp.sqrt(var + EPS_NORM) + gn_bias
        out = jax.nn.gelu(out, approximate=False)
        return out + x

    def _L3_gnn_ref(h, edge_index, edge_attr, ee_w1, ee_b1, ee_g1, ee_bb1, ee_w2, ee_b2, mlp_w1, mlp_b1, mlp_g1, mlp_bb1, mlp_w2, mlp_b2, mlp_g2, mlp_bb2):
        import jax, jax.numpy as jnp
        import numpy as np
        BN_EPS = 1e-05

        def _bn(x, gamma, beta):
            m = jnp.mean(x, axis=0)
            v = jnp.var(x, axis=0)
            return (x - m) * jax.lax.rsqrt(v + BN_EPS) * gamma + beta
        N = h.shape[0]
        src, dst = (edge_index[0], edge_index[1])
        e = jax.nn.relu(_bn(edge_attr @ ee_w1 + ee_b1, ee_g1, ee_bb1)) @ ee_w2 + ee_b2
        agg_edge = jax.ops.segment_sum(e, dst, num_segments=N)
        h = h + agg_edge
        neigh = jax.ops.segment_sum(h[src], dst, num_segments=N)
        z = h + neigh
        z = jax.nn.relu(_bn(z @ mlp_w1 + mlp_b1, mlp_g1, mlp_bb1))
        z = jax.nn.relu(_bn(z @ mlp_w2 + mlp_b2, mlp_g2, mlp_bb2))
        return z
    edge_index = jnp.stack([src, dst])
    h = jnp.maximum(_layernorm(x, axis=-1), 0.0)
    x = x + _L0_gnn_ref(h, edge_index, L0_gnn_W, L0_gnn_att_src, L0_gnn_att_dst, L0_gnn_bias, L0_gnn_gamma, L0_gnn_beta)
    h = jnp.maximum(_layernorm(x, axis=-1), 0.0)
    x = x + _L1_gnn_ref(h, edge_type_8, edge_weight, src, dst, L1_gnn_comp1, L1_gnn_V1, L1_gnn_bias1, L1_gnn_comp2, L1_gnn_V2, L1_gnn_bias2)
    h = jnp.maximum(_layernorm(x, axis=-1), 0.0)
    x = x + _L2_gnn_ref(h, edge_index, L2_gnn_Wq, L2_gnn_bq, L2_gnn_Wk, L2_gnn_bk, L2_gnn_Wv, L2_gnn_bv, L2_gnn_Wskip, L2_gnn_bskip, L2_gnn_Wbeta, L2_gnn_gn_weight, L2_gnn_gn_bias, L2_gnn_gn_mean_scale)
    h = jnp.maximum(_layernorm(x, axis=-1), 0.0)
    x = x + _L3_gnn_ref(h, edge_index, edge_attr_16, L3_gnn_ee_w1, L3_gnn_ee_b1, L3_gnn_ee_g1, L3_gnn_ee_bb1, L3_gnn_ee_w2, L3_gnn_ee_b2, L3_gnn_mlp_w1, L3_gnn_mlp_b1, L3_gnn_mlp_g1, L3_gnn_mlp_bb1, L3_gnn_mlp_w2, L3_gnn_mlp_b2, L3_gnn_mlp_g2, L3_gnn_mlp_bb2)
    return x

_drawn_inputs = setup_inputs


def setup_inputs(seed=0):
    import zlib

    import numpy as np

    out = dict(_drawn_inputs(seed))
    spreads = {'L0_gnn_bias': (0.0, 0.8),
     'L0_gnn_gamma': (1.0, 0.2),
     'L0_gnn_beta': (0.0, 0.1),
     'L1_gnn_bias1': (0.0, 0.1),
     'L1_gnn_bias2': (0.0, 0.1),
     'L2_gnn_bq': (0.0, 0.8),
     'L2_gnn_bk': (0.0, 0.8),
     'L2_gnn_bv': (0.0, 0.8),
     'L2_gnn_bskip': (0.0, 0.8),
     'L2_gnn_gn_weight': (1.0, 0.2),
     'L2_gnn_gn_bias': (0.0, 0.487),
     'L2_gnn_gn_mean_scale': (1.0, 0.2),
     'L3_gnn_ee_b1': (0.0, 0.8),
     'L3_gnn_ee_g1': (1.0, 0.2),
     'L3_gnn_ee_bb1': (0.0, 0.1),
     'L3_gnn_ee_b2': (0.0, 0.1),
     'L3_gnn_mlp_b1': (0.0, 0.8),
     'L3_gnn_mlp_g1': (1.0, 0.2),
     'L3_gnn_mlp_bb1': (0.0, 0.309),
     'L3_gnn_mlp_b2': (0.0, 0.8),
     'L3_gnn_mlp_g2': (1.0, 0.2),
     'L3_gnn_mlp_bb2': (0.0, 0.445)}
    factors = {'L2_gnn_Wq': 3.47, 'L2_gnn_Wk': 3.464}
    for name, (base, spread) in spreads.items():
        noise = np.random.default_rng([zlib.crc32(name.encode()), seed]).standard_normal(out[name].shape)
        drawn = base * np.exp(spread * noise) if base else spread * noise
        out[name] = jnp.asarray(drawn.astype(out[name].dtype))
    for name, factor in factors.items():
        out[name] = (out[name] * factor).astype(out[name].dtype)
    return out
```

```python
from contextlib import ExitStack

import concourse.bass as bass
from concourse import mybir

F32 = mybir.dt.float32
I32 = mybir.dt.int32
ALU = mybir.AluOpType
ACT = mybir.ActivationFunctionType
AX_X = mybir.AxisListType.X

P = 128
N = 3125
E = 100000
D = 128
NT = -(-N // P)
NLAST = N - (NT - 1) * P
NP = NT * P
SUPER = 2 * P
ST = -(-E // SUPER)
SS = 416
K = 2 * SS
SETS = K // 8
NQ = 4
JB = 104
assert ST + NT - 1 <= SS and SS == 4 * JB and SETS % NQ == 0
BIG = 1.0e30
LN_EPS = 1e-5
CR = 16
R_REL = 8
NW = NT * D
ARENA = 30720


def build(nc, t, out):
    ctx = ExitStack()
    with ctx:
        def sb(name, shape, dt=F32):
            return ctx.enter_context(nc.sbuf_tensor(name, shape, dt))

        stage_sems = []

        def sem(name):
            stage_sems.append(nc.alloc_semaphore(name=name))
            return stage_sems[-1]

        def end_stage():
            nc.clear_and_free_semaphores(stage_sems)
            stage_sems.clear()
            nc.all_engine_barrier()

        def dram(name, shape, dt=F32):
            return nc.dram_tensor(name, shape, dt, kind="Internal").ap()

        X = sb("X", [P, NW])
        H = sb("H", [P, NW])
        HT = sb("HT", [P, NP])
        idx_src = sb("idx_src", [P, K], I32)
        idx_rel = sb("idx_rel", [P, K], I32)
        drel = sb("drel", [P, K])
        wgt = sb("wgt", [P, K])
        pen = sb("pen", [P, K])
        ntile = sb("ntile", [1, SS], I32)
        estep = sb("estep", [1, SS], I32)
        att = sb("att", [P, K * 8])
        ident = sb("ident", [P, P])
        ones = sb("ones", [P, P])
        lastmask = sb("lastmask", [P, P])
        iota_row = sb("iota_row", [P, P])
        pidx = sb("pidx", [P, 1])
        small = sb("small", [P, 192])
        A = sb("arena", [P, ARENA])
        PS = ctx.enter_context(nc.psum_tensor("PS", [P, 4096], F32))

        drel_rows = dram("drel_rows", [SS, SUPER])
        key_rows = dram("key_rows", [SS, SUPER])
        n_rows = dram("n_rows", [4, JB], I32)
        e_rows = dram("e_rows", [4, JB], I32)
        tab0 = dram("tab0", [NP, 136])
        tab_rel = dram("tab_rel", [NP * R_REL, D])
        tab_x = dram("tab_x", [NP, D])
        tab_h = dram("tab_h", [NP, D])
        spill0 = dram("spill0", [SETS, P, 8 * 136])
        spill2 = dram("spill2", [SETS, P, 8 * 129])
        score_rows = dram("score_rows", [8, K, P])
        prob_rows = dram("prob_rows", [8, K, P])
        carry_a = dram("carry_a", [P, 4])
        edge_sum = dram("edge_sum", [P, NW])
        carry_b = dram("carry_b", [P, 2])

        def v3(ap, n=D):
            return ap.rearrange("p (t f) -> p t f", f=n)

        def bc_in(ap, n):
            return ap.unsqueeze(len(ap.shape)).to_broadcast(list(ap.shape) + [n])

        def bc_mid(ap, n):
            return ap.unsqueeze(1).to_broadcast([ap.shape[0], n, ap.shape[1]])

        def bcast_load(eng, dst, src):
            return eng.dma_start(dst, src.partition_broadcast(P))

        def load_tiles(eng, row, at, top):
            _, values = nc.values_load_multi_w_load_instructions(row[0:1, bass.ds(at, 4)], engines=[eng], min_val=0,
                                                                 max_val=top)
            return values

        class Chain:

            def __init__(self, name, eng):
                self.sem, self.n, self.eng = sem(name), 0, eng

            def __call__(self, ins):
                self.n += 1
                ins.then_inc(self.sem, 1)
                self.eng.wait_ge(self.sem, self.n)

        def node_view(dram_ap, full):
            if full:
                return dram_ap[0:(NT - 1) * P, :].rearrange("(t p) f -> p t f", p=P)
            return dram_ap[(NT - 1) * P:N, :]

        def stage_setup():
            s_x, s_row, s_zero = sem("s_x"), sem("s_row"), sem("s_zero")
            s_iota, s_const, s_key, s_keyb = sem("s_iota"), sem("s_const"), sem("s_key"), sem("s_keyb")
            s_step, s_gath, s_slot, s_tp, s_nw, s_rows, s_nt = (sem("s_step"), sem("s_gath"), sem("s_slot"), sem("s_tp"),
                                                          sem("s_nw"), sem("s_rows"), sem("s_nt"))
            iota_i = A[:, 0:P].bitcast(I32)
            pidx_i = A[:, P:P + 1].bitcast(I32)
            j_i = A[:, 132:136].bitcast(I32)
            s_i = A[0:1, 144:144 + ST].bitcast(I32)
            last_i = A[0:1, 544:544 + ST].bitcast(I32)
            key = A[0:1, 944:944 + ST]
            keyb = A[:, 1344:1344 + ST]
            junk = A[:, 1744:1744 + ST]
            jf, ej, nf, base, oob = (A[:, 2144 + 4 * i:2148 + 4 * i] for i in range(5))
            e_i, n_i = A[:, 2176:2180].bitcast(I32), A[:, 2180:2184].bitcast(I32)
            tile_i, sidx_f = A[0:1, 2200:2200 + ST].bitcast(I32), A[0:1, 2600:2600 + ST]
            tmp = A[:, 3072:3072 + K]
            raw = [A[:, 4096 + 1024 * i:4096 + 1024 * (i + 1)] for i in range(4)]
            sl = [A[:, 8192 + 1024 * i:8192 + 1024 * (i + 1)] for i in range(4)]
            with nc.Block() as block:
                @block.sync
                def _(sp):
                    sp.dma_start(last_i, t["dst"][:, SUPER - 1:SUPER].rearrange("s o -> o s"),
                                 allow_slow_non_contiguous=True).then_inc(s_row, 16)
                    sp.wait_ge(s_zero, 1)
                    sp.dma_start(v3(X[:, 0:(NT - 1) * D]), node_view(t["x"], True)).then_inc(s_x, 16)
                    sp.dma_start(X[0:NLAST, (NT - 1) * D:NW], node_view(t["x"], False)).then_inc(s_x, 16)
                    sp.wait_ge(s_step, 1)
                    sp.dma_start(n_rows.rearrange("b p -> p b"), n_i[0:JB, :],
                                 allow_slow_non_contiguous=True).then_inc(s_nw, 16)
                    sp.dma_start(e_rows.rearrange("b p -> p b"), e_i[0:JB, :],
                                 allow_slow_non_contiguous=True).then_inc(s_nw, 16)
                    sp.wait_ge(s_nw, 32)
                    sp.dma_start(estep[:], e_rows.rearrange("b p -> (b p)").unsqueeze(0)).then_inc(s_nt, 16)
                    sp.dma_start(ntile[:], n_rows.rearrange("b p -> (b p)").unsqueeze(0)).then_inc(s_nt, 16)
                    sp.wait_ge(s_slot, 1)
                    sp.dma_start(drel_rows.rearrange("(b p) e -> p b e", p=JB),
                                 sl[0][0:JB, :].rearrange("p (b e) -> p b e", b=4)).then_inc(s_rows, 16)
                    sp.dma_start(key_rows.rearrange("(b p) e -> p b e", p=JB),
                                 sl[3][0:JB, :].rearrange("p (b e) -> p b e", b=4)).then_inc(s_rows, 16)
                    sp.wait_ge(s_rows, 32)
                    sp.wait_ge(s_nt, 32)
                    sp.wait_ge(s_x, 32)

                @block.gpsimd
                def _(pool):
                    nc.gpsimd.iota(iota_i, [[1, P]], base=0, channel_multiplier=0)
                    nc.gpsimd.iota(pidx_i, [[1, 1]], base=0, channel_multiplier=1)
                    nc.gpsimd.iota(s_i, [[1, ST]], base=0, channel_multiplier=0)
                    nc.gpsimd.iota(j_i, [[JB, 4]], base=0, channel_multiplier=1).then_inc(s_iota, 1)
                    pool.wait_ge(s_const, 1)
                    nc.gpsimd.affine_select(out=ident[:], in_=ones[:], compare_op=ALU.is_equal, fill=0.0, base=0,
                                            pattern=[[-1, P]], channel_multiplier=1)
                    nc.gpsimd.affine_select(out=lastmask[:], in_=ones[:], compare_op=ALU.is_ge, fill=0.0,
                                            base=NLAST - 1, pattern=[[0, P]], channel_multiplier=-1).then_inc(s_const, 1)
                    pool.wait_ge(s_step, 1)
                    for n, name in enumerate(("dst", "src", "etype", "weight")):
                        for b in range(4):
                            o = raw[n][0:JB, b * SUPER:(b + 1) * SUPER]
                            pool.indirect_dma_start(
                                out=o if name == "weight" else o.bitcast(I32), out_offset=None, in_=t[name],
                                in_offset=bass.IndirectOffsetOnAxis(ap=e_i[0:JB, b:b + 1], axis=0)).then_inc(s_gath, 16)

                @block.vector
                def _(dve):
                    ch = Chain("c_setup", dve)
                    dve.memset(X[:, (NT - 1) * D:NW], 0.0).then_inc(s_zero, 1)
                    dve.memset(ones[:], 1.0).then_inc(s_const, 1)
                    dve.wait_ge(s_iota, 1)
                    dve.tensor_copy(iota_row[:], iota_i)
                    dve.tensor_copy(jf, j_i)
                    dve.tensor_copy(sidx_f, s_i)
                    ch(dve.tensor_copy(pidx[:], pidx_i))
                    dve.wait_ge(s_row, 16)
                    ch(dve.tensor_scalar(tile_i, last_i, 7, None, ALU.arith_shift_right))
                    ch(dve.tensor_copy(key, tile_i))
                    ch(dve.tensor_scalar(key, key, float(NT - 1), None, ALU.min))
                    dve.tensor_tensor(key, key, sidx_f, ALU.add).then_inc(s_key, 1)
                    dve.wait_ge(s_keyb, 1)
                    ch(dve.tensor_copy(keyb, PS[:, 0:ST]))
                    for b in range(4):
                        ch(dve.tensor_scalar(junk, keyb, jf[:, b:b + 1], None, ALU.is_lt, ALU.add,
                                             accum_out=ej[:, b:b + 1]))
                    ch(dve.tensor_tensor(nf, jf, ej, ALU.subtract))
                    ch(dve.tensor_scalar(nf, nf, float(NT - 1), None, ALU.min))
                    ch(dve.tensor_scalar(oob, ej, float(ST), 1.0e6, ALU.is_ge, ALU.mult))
                    ch(dve.tensor_scalar(ej, ej, float(ST - 1), None, ALU.min))
                    dve.tensor_copy(e_i, ej)
                    ch(dve.scalar_tensor_tensor(base, nf, float(P), oob, ALU.mult, ALU.add))
                    dve.tensor_copy(n_i, nf).then_inc(s_step, 1)
                    dve.wait_ge(s_gath, 256)
                    dve.tensor_copy(sl[3][0:JB, :], raw[0][0:JB, :].bitcast(I32))
                    dve.tensor_copy(sl[1][0:JB, :], raw[1][0:JB, :].bitcast(I32))
                    ch(dve.scalar_tensor_tensor(sl[2][0:JB, :], raw[1][0:JB, :].bitcast(I32), float(R_REL),
                                                raw[2][0:JB, :].bitcast(I32), ALU.mult, ALU.add))
                    for b in range(4):
                        c = slice(b * SUPER, (b + 1) * SUPER)
                        ins = dve.tensor_scalar(sl[0][0:JB, c], sl[3][0:JB, c], base[0:JB, b:b + 1], None,
                                                ALU.subtract)
                    ins.then_inc(s_slot, 1)
                    for i, dst in enumerate((drel, idx_src, idx_rel, wgt)):
                        for g in range(2):
                            dve.wait_ge(s_tp, 2 * i + g + 1)
                            bank = (2 * i + g) * 512
                            o = dst[:].rearrange("p (j g) -> p g j", g=2)[:, g, :]
                            ch(dve.tensor_copy(o, PS[:, bank:bank + SS]))
                    ch(dve.tensor_scalar(tmp, drel[:], 0.0, None, ALU.is_ge))
                    ch(dve.scalar_tensor_tensor(pen[:], drel[:], float(P), tmp, ALU.is_lt, ALU.mult))
                    ch(dve.tensor_scalar(pen[:], pen[:], -1.0, BIG, ALU.add, ALU.mult))

                @block.tensor
                def _(pe):
                    pe.wait_ge(s_key, 1)
                    pe.wait_ge(s_const, 2)
                    nc.tensor.matmul(PS[:, 0:ST], ones[0:1, :], key, start=True, stop=True).then_inc(s_keyb, 1)
                    pe.wait_ge(s_slot, 1)
                    for i, src in enumerate((sl[0], sl[1], sl[2], raw[3])):
                        for g in range(2):
                            for b in range(4):
                                o = (2 * i + g) * 512 + b * JB
                                ins = nc.tensor.transpose(PS[:, o:o + JB],
                                                          src[0:JB, b * SUPER + g * P:b * SUPER + (g + 1) * P],
                                                          ident[0:JB, 0:JB])
                            ins.then_inc(s_tp, 1)

        def stage_norm(name):
            s_var, s_std, s_h, s_t = sem(name + "_var"), sem(name + "_std"), sem(name + "_h"), sem(name + "_t")
            mu, var, std = A[:, 0:NT], A[:, 32:32 + NT], A[:, 64:64 + NT]
            sq = A[:, 128:128 + NW]
            with nc.Block() as block:
                @block.vector
                def _(dve):
                    ch = Chain(name + "_c", dve)
                    ch(dve.tensor_reduce(mu, v3(X[:]), AX_X, ALU.add))
                    ch(dve.tensor_scalar(mu, mu, 1.0 / D, None, ALU.mult))
                    ch(dve.tensor_tensor(v3(H[:]), v3(X[:]), bc_in(mu, D), ALU.subtract))
                    ch(dve.tensor_tensor(sq, H[:], H[:], ALU.mult))
                    ch(dve.tensor_reduce(var, v3(sq), AX_X, ALU.add))
                    dve.tensor_scalar(var, var, 1.0 / D, LN_EPS, ALU.mult, ALU.add).then_inc(s_var, 1)
                    dve.wait_ge(s_std, 1)
                    ch(dve.reciprocal(std, std))
                    for g in range(7):
                        a, b = 4 * g, min(4 * g + 4, NT)
                        ch(dve.tensor_tensor(v3(H[:, a * D:b * D]), v3(H[:, a * D:b * D]), bc_in(std[:, a:b], D),
                                             ALU.mult))
                        dve.tensor_scalar(H[:, a * D:b * D], H[:, a * D:b * D], 0.0, None, ALU.max).then_inc(s_h, 1)

                @block.scalar
                def _(act):
                    act.wait_ge(s_var, 1)
                    nc.scalar.activation(std, var, ACT.Sqrt).then_inc(s_std, 1)
                    for g in range(7):
                        a, b = 512 * g, min(512 * g + 512, NP)
                        act.wait_ge(s_t, g + 1)
                        nc.scalar.copy(HT[:, a:b], PS[:, a:b])

                @block.tensor
                def _(pe):
                    transpose_tiles(pe, H, s_h, s_t)

        def transpose_tiles(pe, src, s_in, s_out):
            for g in range(7):
                pe.wait_ge(s_in, g + 1)
                for a in range(4 * g, min(4 * g + 4, NT)):
                    ins = nc.tensor.transpose(PS[:, a * P:(a + 1) * P], src[:, a * D:(a + 1) * D], ident[:])
                ins.then_inc(s_out, 1)

        def project_tiles(pe, srcT, w, s_out):
            for g in range(7):
                for a in range(4 * g, min(4 * g + 4, NT)):
                    ins = nc.tensor.matmul(PS[:, a * P:(a + 1) * P], srcT[:, a * P:(a + 1) * P], w,
                                           start=True, stop=True)
                ins.then_inc(s_out, 1)

        def node_sum(pe, src, dst, s_in, v, s_out):
            pe.wait_ge(s_in, v)
            for a in range(NT):
                ins = nc.tensor.matmul(dst, (lastmask if a == NT - 1 else ones)[:], src[:, a * D:(a + 1) * D],
                                       start=(a == 0), stop=(a == NT - 1))
            ins.then_inc(s_out, 1)

        def gather_sets(pool, name, table, idx, G, width, idx_now, full, frees):
            row = table.shape[1]
            s_ix, s_dummy = sem(name + "_ix"), sem(name + "_pd")
            with pool.Fori(0, SETS // NQ) as i:
                for q in range(NQ):
                    for f, per in frees:
                        pool.wait_ge(f, i * (NQ * per) + ((q + 1 - NQ) * per + CR))
                        pool.sem_inc(s_dummy, 1)
                    nc.gpsimd.tensor_copy(idx_now[:, 8 * q:8 * q + 8],
                                          idx[:, bass.ds(i * (8 * NQ) + 8 * q, 8)]).then_inc(s_ix, 1)
                    pool.wait_ge(s_ix, i * NQ + q + 1)
                    pool.sem_inc(s_dummy, 1)
                    for k in range(8):
                        o = (q * 8 + k) * width
                        pool.indirect_dma_start(
                            out=G[:, o:o + row], out_offset=None, in_=table,
                            in_offset=bass.IndirectOffsetOnAxis(ap=idx_now[:, 8 * q + k:8 * q + k + 1], axis=0)
                        ).then_inc(full[q], 16)

        def each_set(eng, step):
            with eng.Fori(0, SETS // NQ - 1) as i:
                for q in range(NQ):
                    step(i, q, i * NQ + q, NQ)
            i = SETS // NQ - 1
            for q in range(NQ):
                step(i, q, i * NQ + q, NQ - 1 - q)

        def after(i, q, n=1):
            return i + (q + n) // NQ, (q + n) % NQ, i * NQ + (q + n)

        def stage_scores(name, heads, table, width, node_tab, node_w, spill):
            o_g = NT * node_w if heads == 4 else 256
            o_db = o_g + NQ * 8 * width
            G = A[:, o_g:o_db]
            DB = [A[:, o_db + 1024 * i:o_db + 1024 * (i + 1)] for i in range(2)]
            MT = [A[:, o_db + 2048 + 1024 * i:o_db + 3072 + 1024 * i] for i in range(2)]
            o_t = o_db + 4096
            t1, t2 = A[:, o_t:o_t + 64], A[:, o_t + 64:o_t + 128]
            prod = [A[:, o_t + 128 + 516 * i:o_t + 644 + 516 * i] for i in range(4)]
            idx_now = A[:, o_t + 2400:o_t + 2400 + 8 * NQ].bitcast(I32)
            assert o_t + 2400 + 8 * NQ <= ARENA
            full = [sem(f"{name}_g{q}") for q in range(NQ)]
            db_full = [sem(f"{name}_db{q}") for q in range(2)]
            mt_done, mm_done, read_done, spilled, spill_free = (sem(name + x) for x in
                                                                ("_mt", "_mm", "_rd", "_sp", "_sf"))
            mul_done, act_red = sem(name + "_mul"), sem(name + "_ar")
            s_c, s_vd, s_pd = sem(name + "_c"), sem(name + "_vd"), sem(name + "_ed")
            rows = drel_rows.rearrange("j e -> (j e)").unsqueeze(0)
            with nc.Block() as block:
                @block.gpsimd
                def _(pool):
                    gather_sets(pool, name, table, idx_src, G, width, idx_now, full,
                                [(read_done, 1), (spill_free, 1)])

                if heads == 4:
                    @block.scalar
                    def _(act):
                        act.sem_inc(act_red, CR)
                        with act.Fori(0, SETS // NQ) as i:
                            for q in range(NQ):
                                act.wait_ge(read_done, i * NQ + (q + 1 - 2 + CR))
                                for k in range(8):
                                    act.wait_ge(mul_done, i * (8 * NQ) + (q * 8 + k + 1 + CR))
                                    for h in (2, 3):
                                        o = 32 * (q % 2) + 4 * k + h
                                        pr = prod[k % 4][:, h * width:(h + 1) * width]
                                        ins = nc.scalar.activation(pr, pr, ACT.Copy, accum_out=t1[:, o:o + 1])
                                    ins.then_inc(act_red, 1)

                @block.sync
                def _(sp):
                    sp.sem_inc(spill_free, CR)

                    def load_dst(i, q, s):
                        sp.dma_start(DB[q % 2], rows[0:1, bass.ds(s * 1024, 1024)].to_broadcast([P, 1024])
                                     ).then_inc(db_full[q % 2], 16)

                    def step(i, q, s, more):
                        sp.wait_ge(full[q], i * 128 + 128)
                        sp.dma_start(spill[bass.ds(s, 1), :, :].rearrange("o p f -> (o p) f"),
                                     G[:, q * 8 * width:(q + 1) * 8 * width]).then_inc(spilled, 16)
                        if more >= 2:
                            sp.wait_ge(mt_done, s + (1 + CR))
                            load_dst(*after(i, q, 2))
                        sp.wait_ge(spilled, s * 16 + 16)
                        sp.sem_inc(spill_free, 1)

                    load_dst(0, 0, 0)
                    load_dst(0, 1, 1)
                    each_set(sp, step)

                @block.tensor
                def _(pe):
                    pe.sem_inc(mm_done, CR)
                    with pe.Fori(0, SETS // NQ) as i:
                        for q in range(NQ):
                            s = i * NQ + q
                            tiles = load_tiles(mybir.EngineType.PE, ntile, s * 4, NT - 1)
                            pe.wait_ge(mt_done, s + 1 + CR)
                            if heads == 8:
                                pe.wait_ge(read_done, s + (1 - 2 + CR))
                            for k in range(8):
                                n = tiles[k // 2]
                                lhsT = MT[q % 2][:, k * P:(k + 1) * P]
                                if heads == 8:
                                    ins = nc.tensor.matmul(PS[:, (q % 2) * 512 + k * 8:(q % 2) * 512 + k * 8 + 8], lhsT,
                                                           node_tab[:, bass.ds(n * 8, 8)], start=True, stop=True)
                                else:
                                    pe.wait_ge(mul_done, s * 8 + (k + 1 - 4 + CR))
                                    for c in range(2):
                                        b = ((k % 4) * 2 + c) * 512
                                        ins = nc.tensor.matmul(PS[:, b:b + 258], lhsT,
                                                               node_tab[:, bass.ds(n * 516 + 258 * c, 258)],
                                                               start=True, stop=True)
                                    ins.then_inc(s_pd, 1)
                            if heads == 8:
                                ins.then_inc(mm_done, 1)

                @block.vector
                def _(dve):
                    if heads == 4:
                        ch = Chain(name + "_c0", dve)
                        ch(dve.memset(G, 1.0))
                        dve.sem_inc(mul_done, CR)
                    dve.sem_inc(mt_done, CR)
                    dve.sem_inc(read_done, CR)

                    def onehots(i, q, s):
                        dve.wait_ge(db_full[q % 2], i * (8 * NQ) + (16 * (q // 2) + 16))
                        if heads == 8:
                            dve.wait_ge(mm_done, s + (1 - 2 + CR))
                        else:
                            dve.wait_ge(mul_done, s * 8 + (8 - 16 + CR))
                        nc.vector.tensor_scalar(MT[q % 2], DB[q % 2], pidx[:, 0:1], None,
                                                ALU.is_equal).then_inc(mt_done, 1)

                    def step(i, q, s, more):
                            if more:
                                onehots(*after(i, q))
                            g3 = G[:, q * 8 * width:(q + 1) * 8 * width].rearrange("p (k f) -> p k f", f=width)
                            dve.wait_ge(full[q], i * 128 + 128)
                            pen_b = bc_in(pen[:, bass.ds(s * 8, 8)], heads)
                            o = att[:, bass.ds(s * (8 * heads), 8 * heads)].rearrange("p (k h) -> p k h", h=heads)
                            if heads == 8:
                                dve.wait_ge(mm_done, s + 1 + CR)
                                p3 = PS[:, (q % 2) * 512:(q % 2) * 512 + 64].rearrange("p (k h) -> p k h", h=8)
                                a3 = t1.rearrange("p (k h) -> p k h", h=8)
                                nc.vector.tensor_tensor(a3, p3, g3[:, :, 128:136], ALU.add).then_inc(read_done, 1)
                                dve.wait_ge(read_done, s + 1 + CR)
                                nc.vector.scalar_tensor_tensor(t2, t1, 0.2, t1, ALU.mult, ALU.max).then_inc(s_c, 1)
                                dve.wait_ge(s_c, s + 1)
                                nc.vector.tensor_tensor(o, t2.rearrange("p (k h) -> p k h", h=8), pen_b,
                                                        ALU.add).then_inc(s_vd, 1)
                            else:
                                def reduce_slot(k):
                                    return nc.vector.tensor_reduce(
                                        t1[:, 32 * (q % 2) + 4 * k:32 * (q % 2) + 4 * k + 2],
                                        prod[k % 4][:, 0:258].rearrange("p (h f) -> p h f", h=2), AX_X,
                                        ALU.add).then_inc(s_vd, 1)

                                for k in range(8):
                                    c = s * 8 + k
                                    dve.wait_ge(s_pd, c + 1)
                                    dve.wait_ge(act_red, c + (1 - 4 + CR))
                                    b = (k % 4) * 1024
                                    p4 = PS[:, b:b + 1024].rearrange("p (b f) -> p b f", b=2)
                                    xs = g3[:, k, :].unsqueeze(1).unsqueeze(1).to_broadcast([P, 2, 2, width])
                                    nc.vector.tensor_tensor(
                                        prod[k % 4].rearrange("p (b h f) -> p b h f", b=2, h=2),
                                        p4[:, :, 0:258].rearrange("p b (h f) -> p b h f", h=2), xs,
                                        ALU.mult).then_inc(mul_done, 1)
                                    if k:
                                        dve.wait_ge(mul_done, c + CR)
                                        reduce_slot(k - 1)
                                dve.wait_ge(mul_done, s * 8 + 8 + CR)
                                reduce_slot(7)
                                dve.wait_ge(s_vd, s * 8 + 8)
                                dve.wait_ge(act_red, s * 8 + 8 + CR)
                                nc.vector.tensor_tensor(
                                    o, t1[:, 32 * (q % 2):32 * (q % 2) + 32].rearrange("p (k h) -> p k h", h=4), pen_b,
                                    ALU.add).then_inc(read_done, 1)

                    onehots(0, 0, 0)
                    each_set(dve, step)

        def stage_softmax(name, heads):
            C = P // heads
            L = K * P // C
            XS, KEY, RST, SC = (A[:, i * 6656:i * 6656 + L] for i in range(4))
            stage = [A[0:JB, 26624 + 512 * i:27136 + 512 * i] for i in range(4)]
            f4, c4, c2 = A[:, 28672:28676], A[0:heads, 28704:28704 + 4 * C], A[0:heads, 28832:28832 + 2 * C]
            w = [A[0:heads, 28960 + 32 * i:28960 + 32 * i + C] for i in range(6)]
            pq = A[:, 29216:29218]
            a3 = att[:, 0:K * heads].rearrange("p (k h) -> p k h", h=heads)
            HG = heads // 4
            s_tp, s_ev, s_st, s_ld, s_key, s_f4, s_c4, s_c2, s_pq, s_exp, s_pr, s_lp, s_t2, s_sub = (
                sem(name + f"_{i}") for i in range(14))
            s_lo = [sem(f"{name}_lo{i}") for i in range(4)]
            s_lq = [sem(f"{name}_lq{i}") for i in range(4)]
            JOBS = 8 * HG

            def rows_of(d, j):
                b, g = j // HG, j % HG
                return d[4 * g:4 * g + 4, b * JB:(b + 1) * JB, :].rearrange("h k e -> k h e")
            with nc.Block() as block:
                @block.tensor
                def _(pe):
                    for j in range(JOBS):
                        if j >= 8:
                            pe.wait_ge(s_ev, j - 7)
                        for h in range(4):
                            o = (j % 8) * 512 + h * P
                            ins = nc.tensor.transpose(PS[0:JB, o:o + P],
                                                      a3[:, (j // HG) * JB:(j // HG + 1) * JB, 4 * (j % HG) + h],
                                                      ident[:])
                        ins.then_inc(s_tp, 1)
                    for j in range(JOBS):
                        pe.wait_ge(s_lo[j % 4], 16 * (j // 4 + 1))
                        if j < 8:
                            pe.wait_ge(s_ev, JOBS)
                        else:
                            pe.wait_ge(s_t2, j - 7)
                        for h in range(4):
                            o = (j % 8) * 512 + h * JB
                            ins = nc.tensor.transpose(PS[:, o:o + JB], stage[j % 4][:, h * P:(h + 1) * P],
                                                      ident[0:JB, 0:JB])
                        ins.then_inc(s_lp, 1)

                @block.scalar
                def _(act):
                    for j in range(JOBS):
                        act.wait_ge(s_tp, j + 1)
                        if j >= 4:
                            act.wait_ge(s_lq[j % 4], 16 * (j // 4))
                        nc.scalar.copy(stage[j % 4], PS[0:JB, (j % 8) * 512:(j % 8) * 512 + 512]).then_inc(s_ev, 1)
                    act.wait_ge(s_sub, 1)
                    nc.scalar.activation(XS, XS, ACT.Exp).then_inc(s_exp, 1)

                @block.sync
                def _(sp):
                    for h in range(heads):
                        sp.dma_start(KEY[h * C:(h + 1) * C, :],
                                     key_rows.rearrange("j e -> (j e)").rearrange("(c l) -> c l", c=C)
                                     ).then_inc(s_key, 16)
                    for j in range(JOBS):
                        sp.wait_ge(s_ev, j + 1)
                        sp.dma_start(rows_of(score_rows, j), stage[j % 4].rearrange("k (h e) -> k h e", h=4)
                                     ).then_inc(s_lq[j % 4], 16)
                    for i in range(4):
                        sp.wait_ge(s_lq[i], 16 * (JOBS // 4))
                    sp.dma_start(XS, score_rows[0:heads].rearrange("h k e -> (h k e)").rearrange("(q l) -> q l", q=P)
                                 ).then_inc(s_ld, 16)
                    sp.wait_ge(s_f4, 1)
                    sp.dma_start(carry_a, f4).then_inc(s_c4, 16)
                    sp.wait_ge(s_c4, 16)
                    sp.dma_start(c4, carry_a.rearrange("(h c) v -> h (c v)", h=heads)).then_inc(s_c4, 16)
                    sp.wait_ge(s_c2, 1)
                    sp.dma_start(carry_b.rearrange("(h c) v -> h (c v)", h=heads), c2).then_inc(s_pq, 16)
                    sp.wait_ge(s_pq, 16)
                    sp.dma_start(pq, carry_b).then_inc(s_pq, 16)
                    sp.wait_ge(s_exp, 1)
                    sp.dma_start(prob_rows[0:heads].rearrange("h k e -> (h k e)").rearrange("(q l) -> q l", q=P), XS
                                 ).then_inc(s_pr, 16)
                    sp.wait_ge(s_pr, 16)
                    for j in range(JOBS):
                        if j >= 4:
                            sp.wait_ge(s_lp, j - 3)
                        sp.dma_start(stage[j % 4].rearrange("k (h e) -> k h e", h=4), rows_of(prob_rows, j)
                                     ).then_inc(s_lo[j % 4], 16)

                @block.vector
                def _(dve):
                    ch = Chain(name + "_cv", dve)
                    dve.wait_ge(s_key, 16 * heads)
                    ch(dve.tensor_tensor(RST[:, 1:L], KEY[:, 1:L], KEY[:, 0:L - 1], ALU.is_equal))
                    ch(dve.tensor_scalar(RST[:, 1:L], RST[:, 1:L], -1.0, BIG, ALU.add, ALU.mult))
                    ch(dve.memset(RST[:, 0:1], -BIG))
                    dve.wait_ge(s_ld, 16)
                    ch(dve.tensor_tensor_scan(SC, RST, XS, -BIG, ALU.add, ALU.max))
                    ch(dve.tensor_tensor_scan(SC[:, 0:L - 1][:, ::-1], RST[:, 1:L][:, ::-1], SC[:, 0:L - 1][:, ::-1],
                                              SC[:, L - 1:L], ALU.add, ALU.max))
                    dve.tensor_copy(f4[:, 0:1], SC[:, 0:1])
                    dve.tensor_copy(f4[:, 1:2], SC[:, L - 1:L])
                    dve.tensor_copy(f4[:, 2:3], KEY[:, 0:1])
                    dve.tensor_copy(f4[:, 3:4], KEY[:, L - 1:L]).then_inc(s_f4, 1)
                    dve.wait_ge(s_c4, 32)
                    c43 = c4.rearrange("h (c v) -> h c v", v=4)
                    F, T, KF, KL = (c43[:, :, v] for v in range(4))
                    cont, single, link, run, tmpw, zero = w
                    ch(dve.memset(cont[:, 0:1], -BIG))
                    ch(dve.tensor_tensor(cont[:, 1:C], KF[:, 1:C], KL[:, 0:C - 1], ALU.is_equal))
                    ch(dve.tensor_scalar(cont[:, 1:C], cont[:, 1:C], -1.0, BIG, ALU.add, ALU.mult))
                    ch(dve.tensor_tensor(single, KF, KL, ALU.is_equal))
                    ch(dve.tensor_scalar(single, single, -1.0, BIG, ALU.add, ALU.mult))
                    c23 = c2.rearrange("h (c v) -> h c v", v=2)
                    ch(dve.memset(c2, -BIG))
                    ch(dve.tensor_tensor(link, cont, single, ALU.add))
                    ch(dve.tensor_tensor_scan(run, link, T, -BIG, ALU.add, ALU.max))
                    ch(dve.tensor_tensor(c23[:, 1:C, 0], run[:, 0:C - 1], cont[:, 1:C], ALU.add))
                    ch(dve.tensor_tensor(link[:, 0:C - 1], cont[:, 1:C], single[:, 0:C - 1], ALU.add))
                    ch(dve.memset(link[:, C - 1:C], -BIG))
                    ch(dve.tensor_tensor_scan(run[:, ::-1], link[:, ::-1], F[:, ::-1], -BIG, ALU.add, ALU.max))
                    dve.tensor_tensor(c23[:, 0:C - 1, 1], run[:, 1:C], cont[:, 1:C], ALU.add).then_inc(s_c2, 1)
                    dve.wait_ge(s_pq, 32)
                    for v, at in ((0, 0), (1, L - 1)):
                        ch(dve.tensor_scalar(RST, KEY, KEY[:, at:at + 1], None, ALU.is_equal))
                        ch(dve.tensor_scalar(RST, RST, -1.0, BIG, ALU.add, ALU.mult))
                        ch(dve.scalar_tensor_tensor(SC, RST, pq[:, v:v + 1], SC, ALU.add, ALU.max))
                    dve.tensor_tensor(XS, XS, SC, ALU.subtract).then_inc(s_sub, 1)
                    for j in range(JOBS):
                        dve.wait_ge(s_lp, j + 1)
                        b, g = j // HG, j % HG
                        o = a3[:, b * JB:(b + 1) * JB, 4 * g:4 * g + 4].rearrange("p k h -> p h k")
                        dve.tensor_copy(o, PS[:, (j % 8) * 512:(j % 8) * 512 + 4 * JB]
                                        .rearrange("p (h k) -> p h k", h=4)).then_inc(s_t2, 1)

        def stage_aggregate(name, acc, chunks, heads=0, spill=None, width=D, table=None, idx=None, weighted=False,
                            edge_w=None):
            W = sum(chunks)
            o = acc[1]
            ACC = A[:, acc[0]:acc[0] + NT * W]
            G = A[:, o:o + NQ * 8 * width]
            o += NQ * 8 * width
            M = [A[:, o + 1024 * i:o + 1024 * (i + 1)] for i in range(2)]
            o += 2048
            Y = [A[:, o + 8 * W * i:o + 8 * W * (i + 1)] for i in range(2)] if heads or edge_w is not None else None
            o += 16 * W if Y else 0
            if edge_w is not None:
                GE = A[:, o:o + NQ * 1024]
                o += NQ * 1024
            dcol = A[:, o:o + 8 * NQ]
            wcol = A[:, o + 32:o + 32 + 8 * NQ]
            idx_now = A[:, o + 64:o + 64 + 8 * NQ].bitcast(I32)
            assert o + 96 <= ARENA, (name, o)
            RG = 4 if len(chunks) == 2 or edge_w is not None else 8
            full = [sem(f"{name}_g{q}") for q in range(NQ)]
            attr_full = [sem(f"{name}_at{q}") for q in range(NQ)]
            m_done, y_done, sum_done, add_done, z_done, r_done = (sem(name + x) for x in
                                                                  ("_m", "_y", "_s", "_a", "_z", "_r"))
            s_v, s_dd, s_ones = sem(name + "_v"), sem(name + "_dd"), sem(name + "_one")
            ya_done = sem(name + "_ya")
            lead = len(chunks)

            def region(ss, c):
                return ((ss % RG) * lead + c) * 512
            with nc.Block() as block:
                @block.sync
                def _(sp):
                    if spill is not None:
                        with sp.Fori(0, SETS // NQ) as i:
                            for q in range(NQ):
                                sp.wait_ge(y_done, i * NQ + (q + 1 - NQ + CR))
                                if heads == 4:
                                    sp.wait_ge(ya_done, i * NQ + (q + 1 - NQ + CR))
                                sp.dma_start(G[:, q * 8 * width:(q + 1) * 8 * width],
                                             spill[bass.ds(i * NQ + q, 1), :, :].rearrange("o p f -> (o p) f")
                                             ).then_inc(full[q], 16)
                    if edge_w is not None:
                        sp.wait_ge(s_ones, 1)
                        with sp.Fori(0, SETS // NQ) as i:
                            for q in range(NQ):
                                s = i * NQ + q
                                sp.wait_ge(z_done, s + (1 - NQ + CR))
                                for u in range(4):
                                    e = sp.value_load(estep[0:1, bass.ds(s * 4 + u, 1)], min_val=0, max_val=ST - 1)
                                    sp.dma_start(GE[0:16, (q * 4 + u) * 256:(q * 4 + u + 1) * 256]
                                                 .rearrange("f (g e) -> f g e", g=2),
                                                 t["attr_t"][bass.ds(e * 2, 2), :, :].rearrange("g f e -> f g e")
                                                 ).then_inc(attr_full[q], 16)

                if heads:
                    @block.gpsimd
                    def _(pool):
                        pool.sem_inc(y_done, CR)
                        with pool.Fori(0, SETS // NQ) as i:
                            for q in range(NQ):
                                s = i * NQ + q
                                pool.wait_ge(sum_done, s * 4 + (4 - 8 + CR))
                                pool.wait_ge(full[q], i * 16 + 16)
                                y3 = Y[q % 2].rearrange("p (k f) -> p k f", f=W)
                                g3 = G[:, q * 8 * width:(q + 1) * 8 * width].rearrange("p (k f) -> p k f", f=width)
                                p3 = att[:, bass.ds(s * (8 * heads), 8 * heads)].rearrange("p (k h) -> p k h", h=heads)
                                if heads == 8:
                                    nc.gpsimd.tensor_copy(y3[:, :, D:D + 8], p3)
                                    nc.gpsimd.tensor_tensor(y3[:, :, 0:D].rearrange("p k (h c) -> p k h c", h=8),
                                                            g3[:, :, 0:D].rearrange("p k (h c) -> p k h c", h=8),
                                                            bc_in(p3, 16), ALU.mult).then_inc(y_done, 1)
                                else:
                                    for c in range(2):
                                        nc.gpsimd.tensor_copy(y3[:, :, c * 258 + 256:c * 258 + 258],
                                                              p3[:, :, 2 * c:2 * c + 2])
                                    for h in range(2):
                                        ins = nc.gpsimd.tensor_tensor(y3[:, :, h * D:(h + 1) * D], g3[:, :, 0:D],
                                                                      bc_in(p3[:, :, h], D), ALU.mult)
                                    ins.then_inc(y_done, 1)

                if table is not None:
                    @block.gpsimd
                    def _(pool):
                        gather_sets(pool, name, table, idx, G, width, idx_now, full,
                                    [(sum_done, 4) if edge_w is None else (r_done, 1)])

                @block.scalar
                def _(act):
                    if heads == 4:
                        act.sem_inc(ya_done, CR)
                        with act.Fori(0, SETS // NQ) as i:
                            for q in range(NQ):
                                s = i * NQ + q
                                act.wait_ge(full[q], i * 16 + 16)
                                act.wait_ge(sum_done, s * 4 + (4 - 8 + CR))
                                act.sem_inc(s_ones, 1)
                                y3 = Y[q % 2].rearrange("p (k f) -> p k f", f=W)
                                for k in range(8):
                                    for h in (2, 3):
                                        o = 258 + (h - 2) * D
                                        ins = nc.scalar.activation(
                                            y3[:, k, o:o + D], G[:, (q * 8 + k) * width:(q * 8 + k) * width + D],
                                            ACT.Copy, scale=att[:, bass.ds(s * 32 + (k * 4 + h), 1)])
                                ins.then_inc(ya_done, 1)
                    if edge_w is not None:
                        act.sem_inc(r_done, CR)
                        with act.Fori(0, SETS // NQ) as i:
                            for q in range(NQ):
                                s = i * NQ + q
                                act.wait_ge(sum_done, s * 4 + (4 - 8 + CR))
                                act.wait_ge(full[q], i * 128 + 128)
                                act.sem_inc(s_dd, 1)
                                y3 = Y[q % 2].rearrange("p (k f) -> p k f", f=W)
                                for k in range(8):
                                    nc.scalar.activation(y3[:, k, 0:D], G[:, (q * 8 + k) * D:(q * 8 + k + 1) * D],
                                                         ACT.Copy, scale=wgt[:, bass.ds(s * 8 + k, 1)])
                                act.wait_ge(z_done, s + 1 + CR)
                                for v in range(2):
                                    b = 2048 + (q % 2) * 1024 + v * 512
                                    ins = nc.scalar.activation(
                                        y3[:, 4 * v:4 * v + 4, D:2 * D],
                                        PS[:, b:b + 512].rearrange("p (k f) -> p k f", f=D), ACT.Relu)
                                ins.then_inc(r_done, 1)

                @block.tensor
                def _(pe):
                    pe.sem_inc(sum_done, CR)
                    if edge_w is not None:
                        pe.sem_inc(z_done, CR)
                    def features(i, q, s):
                        pe.wait_ge(attr_full[q], i * 64 + 64)
                        pe.wait_ge(r_done, s + (1 - 2 + CR))
                        for k in range(8):
                            b = 2048 + (q % 2) * 1024 + k * P
                            ins = nc.tensor.matmul(PS[:, b:b + P], GE[0:17, (q * 8 + k) * P:(q * 8 + k + 1) * P],
                                                   edge_w, start=True, stop=True)
                        ins.then_inc(z_done, 1)

                    def step(i, q, s, more):
                            if edge_w is not None:
                                if more:
                                    features(*after(i, q))
                                pe.wait_ge(r_done, s + 1 + CR)
                            elif table is not None:
                                pe.wait_ge(full[q], i * 128 + 128)
                            if heads:
                                pe.wait_ge(y_done, s + 1 + CR)
                            if heads == 4:
                                pe.wait_ge(ya_done, s + 1 + CR)
                            pe.wait_ge(m_done, s + 1)
                            for u in range(4):
                                ss = s * 4 + u
                                pe.wait_ge(add_done, ss * 2 + (2 - 2 * RG + CR))
                                for c, wc in enumerate(chunks):
                                    b, at = region(q * 4 + u, c), sum(chunks[:c])
                                    for g in range(2):
                                        k = 2 * u + g
                                        rhs = (Y[q % 2][:, k * W + at:k * W + at + wc] if Y else
                                               G[:, (q * 8 + k) * width:(q * 8 + k) * width + wc])
                                        ins = nc.tensor.matmul(PS[:, b:b + wc], M[q % 2][:, k * P:(k + 1) * P], rhs,
                                                               start=(g == 0), stop=(g == 1))
                                ins.then_inc(sum_done, 1)

                    if edge_w is not None:
                        pe.wait_ge(s_ones, 1)
                        features(0, 0, 0)
                    each_set(pe, step)

                @block.vector
                def _(dve):
                    ch = Chain(name + "_c0", dve)
                    ch(dve.memset(ACC, 0.0))
                    if edge_w is not None:
                        ch(dve.memset(GE[0:32, :], 1.0))
                        for y in Y:
                            ch(dve.memset(y.rearrange("p (k f) -> p k f", f=W)[:, :, 2 * D:2 * D + 1], 1.0))
                        dve.sem_inc(s_ones, 1)
                    dve.sem_inc(add_done, CR)

                    def prepare(i, q, s, load=lambda: None):
                        dve.wait_ge(sum_done, s * 4 + (4 - 8 + CR))
                        nc.vector.tensor_scalar(dcol[:, 8 * q:8 * q + 8], drel[:, bass.ds(s * 8, 8)], 1.0, None,
                                                ALU.mult).then_inc(s_v, 1)
                        if weighted:
                            nc.vector.tensor_scalar(wcol[:, 8 * q:8 * q + 8], wgt[:, bass.ds(s * 8, 8)], 1.0, None,
                                                    ALU.mult).then_inc(s_v, 1)
                        dve.wait_ge(s_v, s * 2 + 2 if weighted else s + 1)
                        for k in range(8):
                            c = 8 * q + k
                            if weighted:
                                ins = nc.vector.tensor_scalar(M[q % 2][:, k * P:(k + 1) * P], iota_row[:],
                                                              dcol[:, c:c + 1], wcol[:, c:c + 1], ALU.is_equal, ALU.mult)
                            else:
                                ins = nc.vector.tensor_scalar(M[q % 2][:, k * P:(k + 1) * P], iota_row[:],
                                                              dcol[:, c:c + 1], None, ALU.is_equal)
                        ins.then_inc(m_done, 1)
                        tiles = load()
                        return tiles

                    def add_up(q, s, tiles):
                        for u, n in enumerate(tiles):
                            ss = s * 4 + u
                            dve.wait_ge(sum_done, ss + 1 + CR)
                            for v in range(2):
                                dve.wait_ge(add_done, ss * 2 + (v - 1 + CR))
                                lo, hi = ((0, W // 2), (W // 2, W))[v]
                                b = region(q * 4 + u, v if lead == 2 else 0) + (0 if lead == 2 else lo)
                                a = ACC[:, bass.ds(n * W + lo, hi - lo)]
                                nc.vector.tensor_tensor(a, a, PS[:, b:b + hi - lo], ALU.add).then_inc(add_done, 1)

                    def tiles_of(s):
                        return load_tiles(mybir.EngineType.DVE, ntile, s * 4, NT - 1)

                    def step(i, q, s, more):
                        if more:
                            tiles = prepare(*after(i, q), lambda: tiles_of(s))
                        else:
                            tiles = tiles_of(s)
                        add_up(q, s, tiles)

                    prepare(0, 0, 0)
                    each_set(dve, step)
            return ACC

        def bn_vector(dve, ch, name, Z, SQ, gamma, beta, v, mean_scale=None):
            mean, var, std = v[0:3]
            s_z, s_sum, s_var, s_std = v[3]
            ch(dve.tensor_copy(mean, mean))
            s_z_sem = s_z
            dve.sem_inc(s_z_sem, 1)
            dve.wait_ge(s_sum, 1)
            ch(dve.tensor_scalar(mean, PS[:, 3584:3584 + D], 1.0 / N, None, ALU.mult))
            if mean_scale is not None:
                ch(dve.tensor_tensor(mean, mean, mean_scale, ALU.mult))
            ch(dve.tensor_tensor(v3(Z), v3(Z), bc_mid(mean, NT), ALU.subtract))
            dve.tensor_tensor(SQ, Z, Z, ALU.mult).then_inc(s_z, 1)
            dve.wait_ge(s_sum, 2)
            dve.tensor_scalar(var, PS[:, 3584:3584 + D], 1.0 / N, LN_EPS, ALU.mult, ALU.add).then_inc(s_var, 1)
            dve.wait_ge(s_std, 1)
            ch(dve.reciprocal(std, std))
            ch(dve.tensor_tensor(std, std, gamma, ALU.mult))
            ch(dve.tensor_tensor(v3(Z), v3(Z), bc_mid(std, NT), ALU.mult))
            ch(dve.tensor_tensor(v3(Z), v3(Z), bc_mid(beta, NT), ALU.add))

        def bn_sems(name):
            return tuple(sem(f"{name}_bn{x}") for x in ("z", "sum", "var", "std"))

        def bn_tensor(pe, Z, SQ, sems):
            s_z, s_sum, _, _ = sems
            node_sum(pe, Z, PS[:, 3584:3584 + D], s_z, 1, s_sum)
            node_sum(pe, SQ, PS[:, 3584:3584 + D], s_z, 2, s_sum)

        def bn_scalar(act, var, std, sems):
            act.wait_ge(sems[2], 1)
            nc.scalar.activation(std, var, ACT.Sqrt).then_inc(sems[3], 1)

        def stage_gat_table():
            s_w, s_mm, s_ev, s_st, s_tab = sem("g0_w"), sem("g0_mm"), sem("g0_ev"), sem("g0_st"), sem("g0_tab")
            ad = A[:, 0:NT * 8]
            tab = A[:, 256:256 + NT * 136].rearrange("p (t f) -> p t f", f=136)
            w, asb, adb = A[:, 4096:4224], A[:, 4224:4352], A[:, 4352:4480]
            tmp = A[:, 4608:4608 + NW]
            with nc.Block() as block:
                @block.sync
                def _(sp):
                    sp.dma_start(w, t["L0_gnn_W"]).then_inc(s_w, 16)
                    bcast_load(sp, asb, t["L0_gnn_att_src"].rearrange("h c -> (h c)")).then_inc(s_w, 16)
                    bcast_load(sp, adb, t["L0_gnn_att_dst"].rearrange("h c -> (h c)")).then_inc(s_w, 16)
                    sp.wait_ge(s_st, 1)
                    sp.dma_start(tab0.rearrange("(t p) f -> p t f", p=P), tab).then_inc(s_tab, 16)
                    sp.wait_ge(s_tab, 16)

                @block.tensor
                def _(pe):
                    pe.wait_ge(s_w, 48)
                    project_tiles(pe, HT, w, s_mm)

                @block.scalar
                def _(act):
                    for g in range(7):
                        a, b = 4 * g, min(4 * g + 4, NT)
                        act.wait_ge(s_mm, g + 1)
                        nc.scalar.copy(tab[:, a:b, 0:D], v3(PS[:, a * D:b * D])).then_inc(s_ev, 1)

                @block.vector
                def _(dve):
                    ch = Chain("g0_c", dve)
                    dve.wait_ge(s_w, 48)
                    dve.wait_ge(s_ev, 7)
                    ch(dve.tensor_tensor(v3(tmp), tab[:, :, 0:D], bc_mid(adb, NT), ALU.mult))
                    ch(dve.tensor_reduce(ad.rearrange("p (t h) -> p t h", h=8),
                                         tmp.rearrange("p (t h c) -> p t h c", t=NT, c=16), AX_X, ALU.add))
                    ch(dve.tensor_tensor(v3(tmp), tab[:, :, 0:D], bc_mid(asb, NT), ALU.mult))
                    dve.tensor_reduce(tab[:, :, D:D + 8], tmp.rearrange("p (t h c) -> p t h c", t=NT, c=16), AX_X,
                                      ALU.add).then_inc(s_st, 1)
            return ad

        def stage_gat_end(ACC):
            s_w = sem("g1_w")
            bn = bn_sems("g1")
            base = NT * 136
            Z, SQ = A[:, base:base + NW], A[:, base + NW:base + 2 * NW]
            rd = A[:, base + 2 * NW:base + 2 * NW + NT * 8]
            o = base + 2 * NW + 256
            bias, gam, bet, mean, var, std = (A[:, o + D * i:o + D * (i + 1)] for i in range(6))
            a3 = ACC.rearrange("p (t f) -> p t f", f=136)
            with nc.Block() as block:
                @block.sync
                def _(sp):
                    bcast_load(sp, bias, t["L0_gnn_bias"]).then_inc(s_w, 16)
                    bcast_load(sp, gam, t["L0_gnn_gamma"]).then_inc(s_w, 16)
                    bcast_load(sp, bet, t["L0_gnn_beta"]).then_inc(s_w, 16)

                @block.vector
                def _(dve):
                    ch = Chain("g1_c", dve)
                    ch(dve.memset(mean, 0.0))
                    r3 = rd.rearrange("p (t h) -> p t h", h=8)
                    ch(dve.tensor_scalar(r3, a3[:, :, D:D + 8], 1e-16, None, ALU.add))
                    ch(dve.reciprocal(rd, rd))
                    ch(dve.tensor_tensor(Z.rearrange("p (t h c) -> p t h c", t=NT, c=16),
                                         a3[:, :, 0:D].rearrange("p t (h c) -> p t h c", c=16), bc_in(r3, 16),
                                         ALU.mult))
                    dve.wait_ge(s_w, 48)
                    ch(dve.tensor_tensor(v3(Z), v3(Z), bc_mid(bias, NT), ALU.add))
                    bn_vector(dve, ch, "g1", Z, SQ, gam, bet, (mean, var, std, bn))
                    ch(dve.tensor_scalar(Z, Z, 0.0, None, ALU.max))
                    ch(dve.tensor_tensor(Z, Z, H[:], ALU.add))
                    ch(dve.tensor_tensor(X[:], X[:], Z, ALU.add))

                @block.tensor
                def _(pe):
                    bn_tensor(pe, Z, SQ, bn)

                @block.scalar
                def _(act):
                    bn_scalar(act, var, std, bn)

        def stage_rel_table(name, comp, V):
            s_w, s_wr, s_mm, s_ea, s_ev, = (sem(name + x) for x in ("_w", "_wr", "_mm", "_ea", "_ev"))
            s_out = [sem(f"{name}_o{i}") for i in range(4)]
            v_sb, wr, cb = A[:, 0:1024], A[:, 1024:2048], A[:, 2048:2112]
            tb = [A[:, 4096 + 1024 * i:5120 + 1024 * i] for i in range(4)]
            tab3 = tab_rel.rearrange("(t p r) o -> t p (r o)", p=P, r=R_REL)
            with nc.Block() as block:
                @block.sync
                def _(sp):
                    sp.dma_start(v_sb.rearrange("i (b o) -> i b o", b=R_REL), V.rearrange("b i o -> i b o")
                                 ).then_inc(s_w, 16)
                    bcast_load(sp, cb, comp.rearrange("r b -> (r b)")).then_inc(s_w, 16)
                    for a in range(NT):
                        sp.wait_ge(s_ea, a + 1)
                        sp.wait_ge(s_ev, a + 1)
                        sp.dma_start(tab3[a], tb[a % 4]).then_inc(s_out[a % 4], 16)
                    for i in range(4):
                        sp.wait_ge(s_out[i], 16 * len(range(i, NT, 4)))

                @block.vector
                def _(dve):
                    ch = Chain(name + "_c", dve)
                    dve.wait_ge(s_w, 32)
                    for b in range(R_REL):
                        for r in range(R_REL):
                            o, src = wr[:, r * D:(r + 1) * D], v_sb[:, b * D:(b + 1) * D]
                            c = cb[:, r * R_REL + b:r * R_REL + b + 1]
                            if b == 0:
                                ins = dve.tensor_scalar(o, src, c, None, ALU.mult)
                            else:
                                ins = dve.scalar_tensor_tensor(o, src, c, o, ALU.mult, ALU.add)
                        if b < R_REL - 1:
                            ch(ins)
                    ins.then_inc(s_wr, 1)
                    for a in range(NT):
                        dve.wait_ge(s_mm, a + 1)
                        if a >= 4:
                            dve.wait_ge(s_out[a % 4], 16 * (a // 4))
                        b = (a % 4) * 1024
                        dve.tensor_copy(tb[a % 4][:, 0:512], PS[:, b:b + 512]).then_inc(s_ev, 1)

                @block.scalar
                def _(act):
                    for a in range(NT):
                        act.wait_ge(s_mm, a + 1)
                        if a >= 4:
                            act.wait_ge(s_out[a % 4], 16 * (a // 4))
                        b = (a % 4) * 1024 + 512
                        nc.scalar.copy(tb[a % 4][:, 512:1024], PS[:, b:b + 512]).then_inc(s_ea, 1)

                @block.tensor
                def _(pe):
                    pe.wait_ge(s_wr, 1)
                    for a in range(NT):
                        if a >= 4:
                            pe.wait_ge(s_ev, a - 3)
                            pe.wait_ge(s_ea, a - 3)
                        for c in range(2):
                            b = (a % 4) * 1024 + 512 * c
                            ins = nc.tensor.matmul(PS[:, b:b + 512], HT[:, a * P:(a + 1) * P],
                                                   wr[:, 512 * c:512 * (c + 1)], start=True, stop=True)
                        ins.then_inc(s_mm, 1)

        def stage_rel_end(name, ACC, bias_ap, first):
            s_w, s_h, s_t = sem(name + "_w"), sem(name + "_h"), sem(name + "_t")
            bias = A[:, ARENA - D:ARENA]
            with nc.Block() as block:
                @block.sync
                def _(sp):
                    bcast_load(sp, bias, bias_ap).then_inc(s_w, 16)

                @block.vector
                def _(dve):
                    ch = Chain(name + "_c", dve)
                    dve.wait_ge(s_w, 16)
                    a3 = ACC.rearrange("p (t f) -> p t f", t=NT)[:, :, 0:D]
                    ch(dve.tensor_tensor(a3, a3, bc_mid(bias, NT), ALU.add))
                    if first:
                        dve.tensor_scalar(v3(H[:]), a3, 0.0, None, ALU.max).then_inc(s_h, 7)
                    else:
                        ch(dve.tensor_tensor(X[:], X[:], ACC, ALU.add))
                if first:
                    @block.tensor
                    def _(pe):
                        transpose_tiles(pe, H, s_h, s_t)

                    @block.scalar
                    def _(act):
                        for g in range(7):
                            a, b = 512 * g, min(512 * g + 512, NP)
                            act.wait_ge(s_t, g + 1)
                            nc.scalar.copy(HT[:, a:b], PS[:, a:b])

        def stage_queries():
            s_w, s_tab, s_q, s_qe, s_u, s_ue = (sem("q_" + x) for x in ("w", "tab", "q", "qe", "u", "ue"))
            U = A[:, 0:NT * 516]
            o = NT * 516
            wq, wkt = A[:, o:o + 512], A[:, o + 512:o + 1024]
            bq, bk = A[:, o + 1024:o + 1028], A[:, o + 1028:o + 1032]
            qt = [A[:, o + 1040 + 512 * i:o + 1552 + 512 * i] for i in range(2)]
            with nc.Block() as block:
                @block.sync
                def _(sp):
                    sp.dma_start(wq, t["L2_gnn_Wq"]).then_inc(s_w, 16)
                    sp.dma_start(wkt.rearrange("c (h f) -> c h f", h=4), t["wk_t"].rearrange("(h c) f -> c h f", h=4)
                                 ).then_inc(s_w, 16)
                    sp.dma_start(bq, t["bq_t"]).then_inc(s_w, 16)
                    sp.dma_start(bk, t["bk_t"]).then_inc(s_w, 16)
                    sp.dma_start(tab_x.rearrange("(t p) f -> p t f", p=P), v3(H[:])).then_inc(s_tab, 16)
                    sp.wait_ge(s_tab, 16)

                @block.tensor
                def _(pe):
                    pe.wait_ge(s_w, 64)
                    for a in range(NT + 1):
                        if a < NT:
                            if a >= 2:
                                pe.wait_ge(s_qe, a - 1)
                            for h in range(4):
                                o = (a % 2) * 512 + h * P
                                ins = nc.tensor.matmul(PS[:, o:o + P], wq[:, h * P:(h + 1) * P],
                                                       HT[:, a * P:(a + 1) * P], start=True, stop=True)
                            ins.then_inc(s_q, 1)
                        if a > 0:
                            b = a - 1
                            pe.wait_ge(s_qe, b + 1)
                            if b >= 2:
                                pe.wait_ge(s_ue, b - 1)
                            for h in range(4):
                                o = 1024 + (b % 2) * 1024 + (h // 2) * 512
                                lhsT = qt[b % 2][:, h * P:(h + 1) * P]
                                nc.tensor.matmul(PS[:, o + (h % 2) * 129:o + (h % 2) * 129 + D], lhsT,
                                                 wkt[:, h * D:(h + 1) * D], start=True, stop=True)
                                ins = nc.tensor.matmul(PS[:, o + (h % 2) * 129 + D:o + (h % 2) * 129 + 129], lhsT, bk[:, h:h + 1],
                                                       start=True, stop=True)
                            ins.then_inc(s_u, 1)

                @block.vector
                def _(dve):
                    dve.wait_ge(s_w, 64)
                    for a in range(NT):
                        dve.wait_ge(s_q, a + 1)
                        if a >= 2:
                            dve.wait_ge(s_u, a - 1)
                        dve.tensor_tensor(qt[a % 2].rearrange("c (h n) -> c h n", h=4),
                                          PS[:, (a % 2) * 512:(a % 2) * 512 + 512].rearrange("c (h n) -> c h n", h=4),
                                          bc_in(bq, P), ALU.add).then_inc(s_qe, 1)

                @block.scalar
                def _(act):
                    for a in range(NT):
                        act.wait_ge(s_u, a + 1)
                        o = 1024 + (a % 2) * 1024
                        nc.scalar.activation(U[:, a * 516:(a + 1) * 516].rearrange("p (c f) -> p c f", c=2),
                                             PS[:, o:o + 1024].rearrange("p (c f) -> p c f", c=2)[:, :, 0:258],
                                             ACT.Copy, scale=float(D) ** -0.5).then_inc(s_ue, 1)
            return U

        def stage_transformer_end(ACC):
            names = ("w", "zn", "zt", "ze", "at", "ae", "o", "oe", "sk", "ske", "gate", "sig", "gelu", "g")
            s_w, s_zn, s_zt, s_ze, s_at, s_ae, s_o, s_oe, s_sk, s_ske, s_gate, s_sig, s_gin, s_gelu = (
                sem("t_" + x) for x in names)
            bn = bn_sems("t")
            o = NT * 516
            OUT, SK, T1 = (A[:, o + NW * i:o + NW * (i + 1)] for i in range(3))
            o += 3 * NW
            wv, wsk = A[:, o:o + 512], A[:, o + 512:o + 640]
            bv = A[0:4, o + 640:o + 768]
            vec = [A[:, o + 768 + D * i:o + 896 + D * i] for i in range(10)]
            bsk, wb1, wb2, wb3, gw, gb, gm, mean, var, std = vec
            o += 768 + 1280
            rd, ra = A[:, o:o + 100], A[:, o + 100:o + 200]
            gt, sg = A[:, o + 200:o + 225], A[:, o + 232:o + 257]
            zt = [A[:, o + 260 + 512 * i:o + 772 + 512 * i] for i in range(2)]
            aT = [A[0:4, o + 1284 + P * i:o + 1412 + P * i] for i in range(2)]
            assert o + 1540 <= ARENA
            a4 = ACC.rearrange("p (t c f) -> p t c f", c=2, f=258)
            r4 = rd.rearrange("p (t c h) -> p t c h", c=2, h=2)
            T2 = A[:, 0:NW]
            with nc.Block() as block:
                @block.sync
                def _(sp):
                    sp.dma_start(wv, t["L2_gnn_Wv"]).then_inc(s_w, 16)
                    sp.dma_start(wsk, t["L2_gnn_Wskip"]).then_inc(s_w, 16)
                    sp.dma_start(bv, t["L2_gnn_bv"].rearrange("(h c) -> h c", h=4)).then_inc(s_w, 16)
                    bcast_load(sp, bsk, t["L2_gnn_bskip"]).then_inc(s_w, 16)
                    for i, w in enumerate((wb1, wb2, wb3)):
                        bcast_load(sp, w, t["L2_gnn_Wbeta"][i * D:(i + 1) * D]).then_inc(s_w, 16)
                    bcast_load(sp, gw, t["L2_gnn_gn_weight"]).then_inc(s_w, 16)
                    bcast_load(sp, gb, t["L2_gnn_gn_bias"]).then_inc(s_w, 16)
                    bcast_load(sp, gm, t["L2_gnn_gn_mean_scale"]).then_inc(s_w, 16)

                @block.tensor
                def _(pe):
                    pe.wait_ge(s_w, 160)
                    pe.wait_ge(s_zn, 1)
                    for a in range(NT + 1):
                        if a < NT:
                            if a >= 2:
                                pe.wait_ge(s_ze, a - 1)
                                pe.wait_ge(s_ae, a - 1)
                            for h in range(4):
                                b = (a % 2) * 512 + h * P
                                nc.tensor.transpose(PS[:, b:b + P],
                                                    a4[:, a, h // 2, (h % 2) * D:(h % 2) * D + D], ident[:]
                                                    ).then_inc(s_zt, 1)
                            b = 1024 + (a % 2) * 512
                            nc.tensor.transpose(PS[0:4, b:b + P], ra[:, 4 * a:4 * a + 4], ident[:]).then_inc(s_at, 1)
                        if a > 0:
                            c = a - 1
                            b = 2048 + (c % 2) * 512
                            pe.wait_ge(s_ze, c + 1)
                            pe.wait_ge(s_ae, c + 1)
                            if c >= 2:
                                pe.wait_ge(s_oe, c - 1)
                            for h in range(4):
                                nc.tensor.matmul(PS[:, b:b + D], zt[c % 2][:, h * P:(h + 1) * P],
                                                 wv[:, h * D:(h + 1) * D], start=(h == 0), stop=False)
                            nc.tensor.matmul(PS[:, b:b + D], aT[c % 2], bv, start=False, stop=True).then_inc(s_o, 1)
                    pe.wait_ge(s_oe, NT)
                    project_tiles(pe, HT, wsk, s_sk)
                    pe.wait_ge(s_ske, 1)
                    bn_tensor(pe, OUT, T1, bn)

                @block.scalar
                def _(act):
                    for a in range(NT):
                        act.wait_ge(s_zt, 4 * a + 4)
                        if a >= 2:
                            act.wait_ge(s_o, a - 1)
                        nc.scalar.copy(zt[a % 2], PS[:, (a % 2) * 512:(a % 2) * 512 + 512]).then_inc(s_ze, 1)
                    act.wait_ge(s_gate, 1)
                    nc.scalar.activation(sg, gt, ACT.Sigmoid).then_inc(s_sig, 1)
                    bn_scalar(act, var, std, bn)
                    act.wait_ge(s_gin, 1)
                    nc.scalar.activation(T1, OUT, ACT.Gelu).then_inc(s_gelu, 1)

                @block.vector
                def _(dve):
                    ch = Chain("t_c", dve)
                    ch(dve.memset(mean, 0.0))
                    den = a4[:, :, :, 256:258]
                    ch(dve.tensor_scalar(r4, den, 1e-16, None, ALU.add))
                    ch(dve.reciprocal(rd, rd))
                    ch(dve.tensor_scalar(rd, rd, 0.25, None, ALU.mult))
                    dve.tensor_tensor(ra.rearrange("p (t c h) -> p t c h", c=2, h=2), den, r4, ALU.mult)
                    for c in range(2):
                        z = a4[:, :, c, 0:256].rearrange("p t (h f) -> p t h f", h=2)
                        ins = dve.tensor_tensor(z, z, bc_in(r4[:, :, c, :], D), ALU.mult)
                    ins.then_inc(s_zn, 1)
                    for a in range(NT):
                        dve.wait_ge(s_at, a + 1)
                        if a >= 2:
                            dve.wait_ge(s_o, a - 1)
                        dve.tensor_copy(aT[a % 2], PS[0:4, 1024 + (a % 2) * 512:1024 + (a % 2) * 512 + P]
                                        ).then_inc(s_ae, 1)
                        if a >= 1:
                            c = a - 1
                            dve.wait_ge(s_o, c + 1)
                            b = 2048 + (c % 2) * 512
                            dve.tensor_copy(OUT[:, c * D:(c + 1) * D], PS[:, b:b + D]).then_inc(s_oe, 1)
                    c = NT - 1
                    dve.wait_ge(s_o, NT)
                    b = 2048 + (c % 2) * 512
                    dve.tensor_copy(OUT[:, c * D:(c + 1) * D], PS[:, b:b + D]).then_inc(s_oe, 1)
                    dve.wait_ge(s_oe, NT)
                    dve.wait_ge(s_sk, 7)
                    ch(dve.tensor_tensor(v3(SK), v3(PS[:, 0:NW]), bc_mid(bsk, NT), ALU.add))
                    ch(dve.tensor_tensor(v3(T1), v3(OUT), bc_mid(wb1, NT), ALU.mult))
                    ch(dve.tensor_tensor(v3(T2), v3(SK), bc_mid(wb2, NT), ALU.mult))
                    ch(dve.tensor_tensor(T1, T1, T2, ALU.add))
                    ch(dve.tensor_tensor(T2, OUT, SK, ALU.subtract))
                    ch(dve.tensor_tensor(v3(T2), v3(T2), bc_mid(wb3, NT), ALU.mult))
                    ch(dve.tensor_tensor(T1, T1, T2, ALU.add))
                    dve.tensor_reduce(gt, v3(T1), AX_X, ALU.add).then_inc(s_gate, 1)
                    ch(dve.tensor_tensor(SK, SK, OUT, ALU.subtract))
                    dve.wait_ge(s_sig, 1)
                    ch(dve.tensor_tensor(v3(SK), v3(SK), bc_in(sg, D), ALU.mult))
                    ch(dve.tensor_tensor(OUT, OUT, SK, ALU.add))
                    dve.sem_inc(s_ske, 1)
                    bn_vector(dve, ch, "t", OUT, T1, gw, gb, (mean, var, std, bn), mean_scale=gm)
                    dve.sem_inc(s_gin, 1)
                    dve.wait_ge(s_gelu, 1)
                    ch(dve.tensor_tensor(T1, T1, H[:], ALU.add))
                    ch(dve.tensor_tensor(X[:], X[:], T1, ALU.add))

        EP, EQ = 125, E // 125

        def stage_edge_weights():
            names = ("ld", "m", "mc", "cen", "g", "gm", "r", "rc", "t", "tw", "v", "var", "std", "mr", "row", "row2",
                     "i", "col")
            (s_ld, s_m, s_mc, s_cen, s_g, s_gm, s_r, s_rc, s_t, s_tw, s_v, s_var, s_std, s_mr, s_row, s_row2, s_i,
             s_col) = (sem("e_" + x) for x in names)
            at = A[0:EP, 0:EQ * 16]
            o = EQ * 16
            w1, w1e = A[0:16, o:o + D], A[0:17, o + D:o + 2 * D]
            g1, bb1, b1 = (A[0:17, o + (2 + i) * D:o + (3 + i) * D] for i in range(3))
            mean = A[:, o + 640:o + 656]
            mcol = A[0:16, o + 656:o + 657]
            var, std = A[0:16, o + 768:o + 896], A[0:16, o + 896:o + 1024]
            row = A[0:1, o + 1024:o + 1152]
            gm, bm, selm = A[:, o + 1152:o + 1280], A[:, o + 1280:o + 1408], A[:, o + 1408:o + 1424]
            cov, tw = A[0:16, o + 1424:o + 1440], A[0:16, o + 1536:o + 1664]
            dm = A[0:16, o + 1664:o + 1680]
            ri, pi, fi = (A[:, o + 1792 + 256 * i:o + 1792 + 256 * i + P].bitcast(I32) for i in range(3))
            rf, pf, qf = (A[:, o + 2560 + 256 * i:o + 2560 + 256 * i + P] for i in range(3))
            EW = small[0:17, 0:D]
            with nc.Block() as block:
                @block.sync
                def _(sp):
                    sp.dma_start(at, t["attr"].rearrange("(p q) f -> p (q f)", p=EP)).then_inc(s_ld, 16)
                    sp.dma_start(w1, t["L3_gnn_ee_w1"]).then_inc(s_ld, 16)
                    for d, n in ((g1, "g1"), (bb1, "bb1"), (b1, "b1")):
                        sp.dma_start(d, t["L3_gnn_ee_" + n].partition_broadcast(17)).then_inc(s_ld, 16)
                    sp.wait_ge(s_row, 1)
                    sp.dma_start(small[16:17, 0:D], row).then_inc(s_row2, 16)
                    sp.wait_ge(s_row2, 16)

                @block.gpsimd
                def _(pool):
                    nc.gpsimd.iota(ri, [[1, P]], base=0, channel_multiplier=0)
                    nc.gpsimd.iota(pi, [[0, P]], base=0, channel_multiplier=1).then_inc(s_i, 1)

                @block.tensor
                def _(pe):
                    pe.wait_ge(s_ld, 80)
                    for c in range(25):
                        ins = nc.tensor.matmul(PS[:, 0:512], ones[0:EP, :], at[:, c * 512:(c + 1) * 512],
                                               start=(c == 0), stop=(c == 24))
                    ins.then_inc(s_m, 1)
                    pe.wait_ge(s_cen, 1)
                    for c in range(100):
                        a = at[:, c * P:(c + 1) * P]
                        ins = nc.tensor.matmul(PS[:, 512:512 + P], a, a, start=(c == 0), stop=(c == 99))
                    ins.then_inc(s_g, 1)
                    pe.wait_ge(s_gm, 1)
                    nc.tensor.matmul(PS[0:16, 1024:1024 + P], selm, gm, start=True, stop=True).then_inc(s_r, 1)
                    pe.wait_ge(s_rc, 1)
                    nc.tensor.matmul(PS[0:16, 1536:1536 + D], cov, w1, start=True, stop=True).then_inc(s_t, 1)
                    pe.wait_ge(s_tw, 1)
                    nc.tensor.matmul(PS[0:16, 2048:2048 + D], ones[0:16, 0:16], tw, start=True, stop=True
                                     ).then_inc(s_v, 1)
                    nc.tensor.matmul(PS[0:1, 2560:2560 + D], mcol, w1, start=True, stop=True).then_inc(s_mr, 1)

                @block.scalar
                def _(act):
                    act.wait_ge(s_var, 1)
                    nc.scalar.activation(std, var, ACT.Sqrt).then_inc(s_std, 1)

                @block.vector
                def _(dve):
                    ch = Chain("e_c", dve)
                    dve.wait_ge(s_i, 1)
                    ch(dve.tensor_scalar(fi, pi, 15, None, ALU.bitwise_and))
                    dve.tensor_copy(qf, fi)
                    ch(dve.tensor_copy(rf, ri))
                    ch(dve.tensor_tensor(selm, qf[:, 0:16], rf[:, 0:16], ALU.is_equal))
                    ch(dve.tensor_scalar(ri, ri, 4, None, ALU.arith_shift_right))
                    ch(dve.tensor_scalar(pi, pi, 4, None, ALU.arith_shift_right))
                    dve.tensor_copy(pf, pi)
                    ch(dve.tensor_copy(rf, ri))
                    ch(dve.tensor_tensor(bm, pf, rf, ALU.is_equal))
                    dve.wait_ge(s_m, 1)
                    ch(dve.tensor_reduce(mean, PS[:, 0:512].rearrange("p (q f) -> p f q", f=16), AX_X, ALU.add))
                    ch(dve.tensor_scalar(mean, mean, 1.0 / E, None, ALU.mult))
                    ch(dve.tensor_tensor(dm, mean[0:16, :], ident[0:16, 0:16], ALU.mult))
                    ch(dve.tensor_reduce(mcol, dm, AX_X, ALU.add))
                    a3 = at.rearrange("p (q f) -> p q f", f=16)
                    dve.tensor_tensor(a3, a3, bc_mid(mean[0:EP, :], EQ), ALU.subtract).then_inc(s_cen, 1)
                    dve.wait_ge(s_g, 1)
                    dve.tensor_tensor(gm, PS[:, 512:512 + P], bm, ALU.mult).then_inc(s_gm, 1)
                    dve.wait_ge(s_r, 1)
                    ch(dve.tensor_reduce(cov, PS[0:16, 1024:1024 + P].rearrange("p (b f) -> p f b", f=16), AX_X,
                                         ALU.add))
                    dve.tensor_scalar(cov, cov, 1.0 / E, None, ALU.mult).then_inc(s_rc, 1)
                    dve.wait_ge(s_t, 1)
                    dve.tensor_tensor(tw, PS[0:16, 1536:1536 + D], w1, ALU.mult).then_inc(s_tw, 1)
                    dve.wait_ge(s_v, 1)
                    dve.tensor_scalar(var, PS[0:16, 2048:2048 + D], LN_EPS, None, ALU.add).then_inc(s_var, 1)
                    dve.wait_ge(s_std, 1)
                    ch(dve.reciprocal(std, std))
                    ch(dve.tensor_tensor(std, std, g1[0:16, :], ALU.mult))
                    dve.tensor_tensor(EW[0:16, :], w1, std, ALU.mult)
                    dve.wait_ge(s_mr, 1)
                    ch(dve.tensor_tensor(row, PS[0:1, 2560:2560 + D], b1[0:1, :], ALU.add))
                    ch(dve.tensor_tensor(row, b1[0:1, :], row, ALU.subtract))
                    ch(dve.tensor_tensor(row, row, std[0:1, :], ALU.mult))
                    dve.tensor_tensor(row, row, bb1[0:1, :], ALU.add).then_inc(s_row, 1)
            return EW


        def stage_edge_end(ACC):
            s_w, s_h, s_t, s_te, s_mm, s_o = (sem("f_" + x) for x in ("w", "h", "t", "te", "mm", "o"))
            o = NT * 257
            F, FT = A[:, o:o + NW], A[:, o + NW:o + 2 * NW]
            w2, b2 = A[:, o + 2 * NW:o + 2 * NW + D], A[:, o + 2 * NW + D:o + 2 * NW + 2 * D]
            a3 = ACC.rearrange("p (t f) -> p t f", f=257)[:, :, D:257]
            with nc.Block() as block:
                @block.sync
                def _(sp):
                    sp.dma_start(w2, t["L3_gnn_ee_w2"]).then_inc(s_w, 16)
                    bcast_load(sp, b2, t["L3_gnn_ee_b2"]).then_inc(s_w, 16)
                    sp.wait_ge(s_o, 1)
                    sp.dma_start(edge_sum, F).then_inc(s_o, 16)
                    sp.wait_ge(s_o, 17)

                @block.tensor
                def _(pe):
                    pe.wait_ge(s_w, 32)
                    transpose_tiles(pe, F, s_h, s_t)
                    pe.wait_ge(s_te, 7)
                    project_tiles(pe, FT, w2, s_mm)

                @block.scalar
                def _(act):
                    for g in range(7):
                        a, b = 512 * g, min(512 * g + 512, NP)
                        act.wait_ge(s_t, g + 1)
                        nc.scalar.copy(FT[:, a:b], PS[:, a:b]).then_inc(s_te, 1)

                @block.vector
                def _(dve):
                    ch = Chain("f_c", dve)
                    dve.tensor_copy(v3(F), a3[:, :, 0:D]).then_inc(s_h, 7)
                    dve.wait_ge(s_w, 32)
                    dve.wait_ge(s_t, 7)
                    ch(dve.tensor_tensor(v3(F), bc_in(a3[:, :, D], D), bc_mid(b2, NT), ALU.mult))
                    dve.wait_ge(s_mm, 7)
                    dve.tensor_tensor(F, F, PS[:, 0:NW], ALU.add).then_inc(s_o, 1)

        def stage_gin_begin():
            s_ld, s_h, s_o = sem("i_ld"), sem("i_h"), sem("i_o")
            with nc.Block() as block:
                @block.sync
                def _(sp):
                    sp.dma_start(A[:, 0:NW], edge_sum).then_inc(s_ld, 16)
                    sp.wait_ge(s_h, 1)
                    sp.dma_start(tab_h.rearrange("(t p) f -> p t f", p=P), v3(H[:])).then_inc(s_o, 16)
                    sp.wait_ge(s_o, 16)

                @block.vector
                def _(dve):
                    dve.wait_ge(s_ld, 16)
                    dve.tensor_tensor(H[:], H[:], A[:, 0:NW], ALU.add).then_inc(s_h, 1)

        def stage_gin_layer(name, Z, w_ap, vecs, last):
            s_w, s_h, s_t, s_te, s_mm, s_out, s_st = (sem(name + x) for x in ("_w", "_h", "_t", "_te", "_mm", "_out", "_st"))
            bn = bn_sems(name)
            o = NW
            SQ = A[:, o:o + NW]
            o += NW
            w, b, gam, bet, mean, var, std = (A[:, o + D * i:o + D * (i + 1)] for i in range(7))
            with nc.Block() as block:
                @block.sync
                def _(sp):
                    sp.dma_start(w, w_ap).then_inc(s_w, 16)
                    for d, v in zip((b, gam, bet), vecs):
                        bcast_load(sp, d, v).then_inc(s_w, 16)
                    if last:
                        sp.wait_ge(s_out, 1)
                        sp.dma_start(node_view(out, True), v3(Z[:, 0:(NT - 1) * D])).then_inc(s_st, 16)
                        sp.dma_start(node_view(out, False), Z[0:NLAST, (NT - 1) * D:NW]).then_inc(s_st, 16)
                        sp.wait_ge(s_st, 32)

                @block.tensor
                def _(pe):
                    pe.wait_ge(s_w, 64)
                    transpose_tiles(pe, Z, s_h, s_t)
                    pe.wait_ge(s_te, 7)
                    project_tiles(pe, HT, w, s_mm)
                    bn_tensor(pe, Z, SQ, bn)

                @block.scalar
                def _(act):
                    for g in range(7):
                        lo, hi = 512 * g, min(512 * g + 512, NP)
                        act.wait_ge(s_t, g + 1)
                        nc.scalar.copy(HT[:, lo:hi], PS[:, lo:hi]).then_inc(s_te, 1)
                    bn_scalar(act, var, std, bn)

                @block.vector
                def _(dve):
                    ch = Chain(name + "_c", dve)
                    ch(dve.memset(mean, 0.0))
                    if not last:
                        ch(dve.tensor_tensor(Z, Z, H[:], ALU.add))
                    dve.sem_inc(s_h, 7)
                    dve.wait_ge(s_w, 64)
                    dve.wait_ge(s_mm, 7)
                    ch(dve.tensor_tensor(v3(Z), v3(PS[:, 0:NW]), bc_mid(b, NT), ALU.add))
                    bn_vector(dve, ch, name, Z, SQ, gam, bet, (mean, var, std, bn))
                    ch(dve.tensor_scalar(Z, Z, 0.0, None, ALU.max))
                    if last:
                        dve.tensor_tensor(Z, Z, X[:], ALU.add).then_inc(s_out, 1)

        stage_setup()
        end_stage()
        stage_norm("n0")
        end_stage()
        ad = stage_gat_table()
        end_stage()
        stage_scores("a0", 8, tab0, 136, ad, 8, spill0)
        end_stage()
        stage_softmax("x0", 8)
        end_stage()
        ACC = stage_aggregate("s0", (0, NT * 136), [136], heads=8, spill=spill0, width=136)
        end_stage()
        stage_gat_end(ACC)
        end_stage()
        EW = stage_edge_weights()
        end_stage()
        stage_norm("n1")
        end_stage()
        stage_rel_table("r1", t["L1_gnn_comp1"], t["L1_gnn_V1"])
        end_stage()
        ACC = stage_aggregate("s1", (0, NT * 257), [257], table=tab_rel, idx=idx_rel, edge_w=EW)
        end_stage()
        stage_rel_end("b1", ACC, t["L1_gnn_bias1"], True)
        end_stage()
        stage_edge_end(ACC)
        end_stage()
        stage_rel_table("r2", t["L1_gnn_comp2"], t["L1_gnn_V2"])
        end_stage()
        ACC = stage_aggregate("s2", (0, NW), [D], table=tab_rel, idx=idx_rel, weighted=True)
        end_stage()
        stage_rel_end("b2", ACC, t["L1_gnn_bias2"], False)
        end_stage()
        stage_norm("n2")
        end_stage()
        U = stage_queries()
        end_stage()
        stage_scores("a2", 4, tab_x, 129, U, 516, spill2)
        end_stage()
        stage_softmax("x2", 4)
        end_stage()
        ACC = stage_aggregate("s3", (0, NT * 516), [258, 258], heads=4, spill=spill2, width=129)
        end_stage()
        stage_transformer_end(ACC)
        end_stage()
        stage_norm("n3")
        end_stage()
        stage_gin_begin()
        end_stage()
        ACC = stage_aggregate("s5", (0, NW), [D], table=tab_h, idx=idx_src)
        end_stage()
        stage_gin_layer("m1", ACC, t["L3_gnn_mlp_w1"], [t["L3_gnn_mlp_" + v] for v in ("b1", "g1", "bb1")], False)
        end_stage()
        stage_gin_layer("m2", ACC, t["L3_gnn_mlp_w2"], [t["L3_gnn_mlp_" + v] for v in ("b2", "g2", "bb2")], True)
        end_stage()


def kernel(x, src, dst, edge_attr_16, edge_type_8, edge_weight, **weights):
    import numpy as np
    import concourse.bacc as bacc
    from concourse.bass_utils import run_bass_kernel_spmd

    arrays = {k: np.ascontiguousarray(v) for k, v in weights.items() if k not in (
        "L2_gnn_Wk", "L2_gnn_bq", "L2_gnn_bk")}
    pad = ST * SUPER - E

    def rows(a, fill):
        a = np.asarray(a)
        return np.concatenate([a, np.full((pad,) + a.shape[1:], fill, a.dtype)]).reshape((ST, SUPER) + a.shape[1:])

    arrays["x"] = np.ascontiguousarray(x)
    arrays["dst"] = rows(dst, NP)
    arrays["src"] = rows(src, 0)
    arrays["etype"] = rows(edge_type_8, 0)
    arrays["weight"] = rows(edge_weight, 0)
    arrays["attr"] = np.ascontiguousarray(edge_attr_16)
    arrays["attr_t"] = np.ascontiguousarray(rows(edge_attr_16, 0).reshape(2 * ST, P, 16).transpose(0, 2, 1))
    arrays["wk_t"] = np.ascontiguousarray(np.asarray(weights["L2_gnn_Wk"]).T)
    arrays["bq_t"] = np.ascontiguousarray(np.asarray(weights["L2_gnn_bq"]).reshape(4, D).T)
    arrays["bk_t"] = np.ascontiguousarray(np.asarray(weights["L2_gnn_bk"]).reshape(4, D).T)
    nc = bacc.Bacc("TRN2", target_bir_lowering=False, num_devices=1)
    t, feed = {}, {}
    for name, a in arrays.items():
        feed["in_" + name] = a
        t[name] = nc.dram_tensor("in_" + name, a.shape, mybir.dt.from_np(a.dtype), kind="ExternalInput").ap()
    out = nc.dram_tensor("out", [N, D], F32, kind="ExternalOutput").ap()
    build(nc, t, out)
    r = run_bass_kernel_spmd(nc, [feed], core_ids=[0])
    return r.results[0]["out"]
```

```python
from contextlib import ExitStack

import concourse.bass as bass
from concourse import mybir

F32 = mybir.dt.float32
I32 = mybir.dt.int32
ALU = mybir.AluOpType
ACT = mybir.ActivationFunctionType
AX_X = mybir.AxisListType.X

P = 128
N = 3125
E = 100000
D = 128
NT = -(-N // P)
NLAST = N - (NT - 1) * P
NP = NT * P
SUPER = 2 * P
ST = -(-E // SUPER)
SS = 416
K = 2 * SS
SETS = K // 8
NQ = 4
JB = 104
assert ST + NT - 1 <= SS and SS == 4 * JB and SETS % NQ == 0
BIG = 1.0e30
LN_EPS = 1e-5
CR = 16
R_REL = 8
NW = NT * D
ARENA = 30720


def build(nc, t, out):
    ctx = ExitStack()
    with ctx:
        def sb(name, shape, dt=F32):
            return ctx.enter_context(nc.sbuf_tensor(name, shape, dt))

        stage_sems = []

        def sem(name):
            stage_sems.append(nc.alloc_semaphore(name=name))
            return stage_sems[-1]

        def end_stage():
            nc.clear_and_free_semaphores(stage_sems)
            stage_sems.clear()
            nc.all_engine_barrier()

        def dram(name, shape, dt=F32):
            return nc.dram_tensor(name, shape, dt, kind="Internal").ap()

        X = sb("X", [P, NW])
        H = sb("H", [P, NW])
        HT = sb("HT", [P, NP])
        idx_src = sb("idx_src", [P, K], I32)
        idx_rel = sb("idx_rel", [P, K], I32)
        drel = sb("drel", [P, K])
        wgt = sb("wgt", [P, K])
        pen = sb("pen", [P, K])
        ntile = sb("ntile", [1, SS], I32)
        estep = sb("estep", [1, SS], I32)
        att = sb("att", [P, K * 8])
        ident = sb("ident", [P, P])
        ones = sb("ones", [P, P])
        lastmask = sb("lastmask", [P, P])
        iota_row = sb("iota_row", [P, P])
        pidx = sb("pidx", [P, 1])
        small = sb("small", [P, 192])
        A = sb("arena", [P, ARENA])
        PS = ctx.enter_context(nc.psum_tensor("PS", [P, 4096], F32))

        drel_rows = dram("drel_rows", [SS, SUPER])
        key_rows = dram("key_rows", [SS, SUPER])
        n_rows = dram("n_rows", [4, JB], I32)
        e_rows = dram("e_rows", [4, JB], I32)
        tab0 = dram("tab0", [NP, 136])
        tab_rel = dram("tab_rel", [NP * R_REL, D])
        tab_x = dram("tab_x", [NP, D])
        tab_h = dram("tab_h", [NP, D])
        spill0 = dram("spill0", [SETS, P, 8 * 136])
        spill2 = dram("spill2", [SETS, P, 8 * 129])
        score_rows = dram("score_rows", [8, K, P])
        prob_rows = dram("prob_rows", [8, K, P])
        carry_a = dram("carry_a", [P, 4])
        edge_sum = dram("edge_sum", [P, NW])
        carry_b = dram("carry_b", [P, 2])
        rel_w = dram("rel_w", [2, P, R_REL * D])
        EW = small[0:17, 0:D]

        def v3(ap, n=D):
            return ap.rearrange("p (t f) -> p t f", f=n)

        def bc_in(ap, n):
            return ap.unsqueeze(len(ap.shape)).to_broadcast(list(ap.shape) + [n])

        def bc_mid(ap, n):
            return ap.unsqueeze(1).to_broadcast([ap.shape[0], n, ap.shape[1]])

        def bcast_load(eng, dst, src):
            return eng.dma_start(dst, src.partition_broadcast(P))

        def load_tiles(eng, row, at, top):
            _, values = nc.values_load_multi_w_load_instructions(row[0:1, bass.ds(at, 4)], engines=[eng], min_val=0,
                                                                 max_val=top)
            return values

        class Chain:

            def __init__(self, name, eng):
                self.sem, self.n, self.eng = sem(name), 0, eng

            def __call__(self, ins):
                self.n += 1
                ins.then_inc(self.sem, 1)
                self.eng.wait_ge(self.sem, self.n)

        def node_view(dram_ap, full):
            if full:
                return dram_ap[0:(NT - 1) * P, :].rearrange("(t p) f -> p t f", p=P)
            return dram_ap[(NT - 1) * P:N, :]

        def stage_setup():
            s_x, s_row, s_zero = sem("s_x"), sem("s_row"), sem("s_zero")
            s_iota, s_const, s_key, s_keyb = sem("s_iota"), sem("s_const"), sem("s_key"), sem("s_keyb")
            s_step, s_gath, s_slot, s_tp, s_nw, s_rows, s_nt = (sem("s_step"), sem("s_gath"), sem("s_slot"), sem("s_tp"),
                                                          sem("s_nw"), sem("s_rows"), sem("s_nt"))
            iota_i = A[:, 0:P].bitcast(I32)
            pidx_i = A[:, P:P + 1].bitcast(I32)
            j_i = A[:, 132:136].bitcast(I32)
            s_i = A[0:1, 144:144 + ST].bitcast(I32)
            last_i = A[0:1, 544:544 + ST].bitcast(I32)
            key = A[0:1, 944:944 + ST]
            keyb = A[:, 1344:1344 + ST]
            junk = A[:, 1744:1744 + ST]
            jf, ej, nf, base, oob = (A[:, 2144 + 4 * i:2148 + 4 * i] for i in range(5))
            e_i, n_i = A[:, 2176:2180].bitcast(I32), A[:, 2180:2184].bitcast(I32)
            tile_i, sidx_f = A[0:1, 2200:2200 + ST].bitcast(I32), A[0:1, 2600:2600 + ST]
            tmp = A[:, 3072:3072 + K]
            raw = [A[:, 4096 + 1024 * i:4096 + 1024 * (i + 1)] for i in range(4)]
            sl = [A[:, 8192 + 1024 * i:8192 + 1024 * (i + 1)] for i in range(4)]
            with nc.Block() as block:
                @block.sync
                def _(sp):
                    sp.dma_start(last_i, t["dst"][:, SUPER - 1:SUPER].rearrange("s o -> o s"),
                                 allow_slow_non_contiguous=True).then_inc(s_row, 16)
                    sp.wait_ge(s_zero, 1)
                    sp.dma_start(v3(X[:, 0:(NT - 1) * D]), node_view(t["x"], True)).then_inc(s_x, 16)
                    sp.dma_start(X[0:NLAST, (NT - 1) * D:NW], node_view(t["x"], False)).then_inc(s_x, 16)
                    sp.wait_ge(s_step, 1)
                    sp.dma_start(n_rows.rearrange("b p -> p b"), n_i[0:JB, :],
                                 allow_slow_non_contiguous=True).then_inc(s_nw, 16)
                    sp.dma_start(e_rows.rearrange("b p -> p b"), e_i[0:JB, :],
                                 allow_slow_non_contiguous=True).then_inc(s_nw, 16)
                    sp.wait_ge(s_nw, 32)
                    sp.dma_start(estep[:], e_rows.rearrange("b p -> (b p)").unsqueeze(0)).then_inc(s_nt, 16)
                    sp.dma_start(ntile[:], n_rows.rearrange("b p -> (b p)").unsqueeze(0)).then_inc(s_nt, 16)
                    sp.wait_ge(s_slot, 1)
                    sp.dma_start(drel_rows.rearrange("(b p) e -> p b e", p=JB),
                                 sl[0][0:JB, :].rearrange("p (b e) -> p b e", b=4)).then_inc(s_rows, 16)
                    sp.dma_start(key_rows.rearrange("(b p) e -> p b e", p=JB),
                                 sl[3][0:JB, :].rearrange("p (b e) -> p b e", b=4)).then_inc(s_rows, 16)
                    sp.wait_ge(s_rows, 32)
                    sp.wait_ge(s_nt, 32)
                    sp.wait_ge(s_x, 32)

                @block.gpsimd
                def _(pool):
                    nc.gpsimd.iota(iota_i, [[1, P]], base=0, channel_multiplier=0)
                    nc.gpsimd.iota(pidx_i, [[1, 1]], base=0, channel_multiplier=1)
                    nc.gpsimd.iota(s_i, [[1, ST]], base=0, channel_multiplier=0)
                    nc.gpsimd.iota(j_i, [[JB, 4]], base=0, channel_multiplier=1).then_inc(s_iota, 1)
                    pool.wait_ge(s_const, 1)
                    nc.gpsimd.affine_select(out=ident[:], in_=ones[:], compare_op=ALU.is_equal, fill=0.0, base=0,
                                            pattern=[[-1, P]], channel_multiplier=1)
                    nc.gpsimd.affine_select(out=lastmask[:], in_=ones[:], compare_op=ALU.is_ge, fill=0.0,
                                            base=NLAST - 1, pattern=[[0, P]], channel_multiplier=-1).then_inc(s_const, 1)
                    pool.wait_ge(s_step, 1)
                    for n, name in enumerate(("dst", "src", "etype", "weight")):
                        for b in range(4):
                            o = raw[n][0:JB, b * SUPER:(b + 1) * SUPER]
                            pool.indirect_dma_start(
                                out=o if name == "weight" else o.bitcast(I32), out_offset=None, in_=t[name],
                                in_offset=bass.IndirectOffsetOnAxis(ap=e_i[0:JB, b:b + 1], axis=0)).then_inc(s_gath, 16)

                @block.vector
                def _(dve):
                    ch = Chain("c_setup", dve)
                    dve.memset(X[:, (NT - 1) * D:NW], 0.0).then_inc(s_zero, 1)
                    dve.memset(ones[:], 1.0).then_inc(s_const, 1)
                    dve.wait_ge(s_iota, 1)
                    dve.tensor_copy(iota_row[:], iota_i)
                    dve.tensor_copy(jf, j_i)
                    dve.tensor_copy(sidx_f, s_i)
                    ch(dve.tensor_copy(pidx[:], pidx_i))
                    dve.wait_ge(s_row, 16)
                    ch(dve.tensor_scalar(tile_i, last_i, 7, None, ALU.arith_shift_right))
                    ch(dve.tensor_copy(key, tile_i))
                    ch(dve.tensor_scalar(key, key, float(NT - 1), None, ALU.min))
                    dve.tensor_tensor(key, key, sidx_f, ALU.add).then_inc(s_key, 1)
                    dve.wait_ge(s_keyb, 1)
                    ch(dve.tensor_copy(keyb, PS[:, 0:ST]))
                    for b in range(4):
                        ch(dve.tensor_scalar(junk, keyb, jf[:, b:b + 1], None, ALU.is_lt, ALU.add,
                                             accum_out=ej[:, b:b + 1]))
                    ch(dve.tensor_tensor(nf, jf, ej, ALU.subtract))
                    ch(dve.tensor_scalar(nf, nf, float(NT - 1), None, ALU.min))
                    ch(dve.tensor_scalar(oob, ej, float(ST), 1.0e6, ALU.is_ge, ALU.mult))
                    ch(dve.tensor_scalar(ej, ej, float(ST - 1), None, ALU.min))
                    dve.tensor_copy(e_i, ej)
                    ch(dve.scalar_tensor_tensor(base, nf, float(P), oob, ALU.mult, ALU.add))
                    dve.tensor_copy(n_i, nf).then_inc(s_step, 1)
                    dve.wait_ge(s_gath, 256)
                    dve.tensor_copy(sl[3][0:JB, :], raw[0][0:JB, :].bitcast(I32))
                    dve.tensor_copy(sl[1][0:JB, :], raw[1][0:JB, :].bitcast(I32))
                    ch(dve.scalar_tensor_tensor(sl[2][0:JB, :], raw[1][0:JB, :].bitcast(I32), float(R_REL),
                                                raw[2][0:JB, :].bitcast(I32), ALU.mult, ALU.add))
                    for b in range(4):
                        c = slice(b * SUPER, (b + 1) * SUPER)
                        ins = dve.tensor_scalar(sl[0][0:JB, c], sl[3][0:JB, c], base[0:JB, b:b + 1], None,
                                                ALU.subtract)
                    ins.then_inc(s_slot, 1)
                    for i, dst in enumerate((drel, idx_src, idx_rel, wgt)):
                        for g in range(2):
                            dve.wait_ge(s_tp, 2 * i + g + 1)
                            bank = (2 * i + g) * 512
                            o = dst[:].rearrange("p (j g) -> p g j", g=2)[:, g, :]
                            ch(dve.tensor_copy(o, PS[:, bank:bank + SS]))
                    ch(dve.tensor_scalar(tmp, drel[:], 0.0, None, ALU.is_ge))
                    ch(dve.scalar_tensor_tensor(pen[:], drel[:], float(P), tmp, ALU.is_lt, ALU.mult))
                    ch(dve.tensor_scalar(pen[:], pen[:], -1.0, BIG, ALU.add, ALU.mult))

                @block.tensor
                def _(pe):
                    pe.wait_ge(s_key, 1)
                    pe.wait_ge(s_const, 2)
                    nc.tensor.matmul(PS[:, 0:ST], ones[0:1, :], key, start=True, stop=True).then_inc(s_keyb, 1)
                    pe.wait_ge(s_slot, 1)
                    for i, src in enumerate((sl[0], sl[1], sl[2], raw[3])):
                        for g in range(2):
                            for b in range(4):
                                o = (2 * i + g) * 512 + b * JB
                                ins = nc.tensor.transpose(PS[:, o:o + JB],
                                                          src[0:JB, b * SUPER + g * P:b * SUPER + (g + 1) * P],
                                                          ident[0:JB, 0:JB])
                            ins.then_inc(s_tp, 1)

        def stage_norm(name):
            s_var, s_std, s_h, s_t = sem(name + "_var"), sem(name + "_std"), sem(name + "_h"), sem(name + "_t")
            mu, var, std = A[:, 0:NT], A[:, 32:32 + NT], A[:, 64:64 + NT]
            sq = A[:, 128:128 + NW]
            with nc.Block() as block:
                @block.vector
                def _(dve):
                    ch = Chain(name + "_c", dve)
                    ch(dve.tensor_reduce(mu, v3(X[:]), AX_X, ALU.add))
                    ch(dve.tensor_scalar(mu, mu, 1.0 / D, None, ALU.mult))
                    ch(dve.tensor_tensor(v3(H[:]), v3(X[:]), bc_in(mu, D), ALU.subtract))
                    ch(dve.tensor_tensor(sq, H[:], H[:], ALU.mult))
                    ch(dve.tensor_reduce(var, v3(sq), AX_X, ALU.add))
                    dve.tensor_scalar(var, var, 1.0 / D, LN_EPS, ALU.mult, ALU.add).then_inc(s_var, 1)
                    dve.wait_ge(s_std, 1)
                    ch(dve.reciprocal(std, std))
                    for g in range(7):
                        a, b = 4 * g, min(4 * g + 4, NT)
                        ch(dve.tensor_tensor(v3(H[:, a * D:b * D]), v3(H[:, a * D:b * D]), bc_in(std[:, a:b], D),
                                             ALU.mult))
                        dve.tensor_scalar(H[:, a * D:b * D], H[:, a * D:b * D], 0.0, None, ALU.max).then_inc(s_h, 1)

                @block.scalar
                def _(act):
                    act.wait_ge(s_var, 1)
                    nc.scalar.activation(std, var, ACT.Sqrt).then_inc(s_std, 1)
                    for g in range(7):
                        a, b = 512 * g, min(512 * g + 512, NP)
                        act.wait_ge(s_t, g + 1)
                        nc.scalar.copy(HT[:, a:b], PS[:, a:b])

                @block.tensor
                def _(pe):
                    transpose_tiles(pe, H, s_h, s_t)

        def transpose_tiles(pe, src, s_in, s_out):
            for g in range(7):
                pe.wait_ge(s_in, g + 1)
                for a in range(4 * g, min(4 * g + 4, NT)):
                    ins = nc.tensor.transpose(PS[:, a * P:(a + 1) * P], src[:, a * D:(a + 1) * D], ident[:])
                ins.then_inc(s_out, 1)

        def project_tiles(pe, srcT, w, s_out):
            for g in range(7):
                for a in range(4 * g, min(4 * g + 4, NT)):
                    ins = nc.tensor.matmul(PS[:, a * P:(a + 1) * P], srcT[:, a * P:(a + 1) * P], w,
                                           start=True, stop=True)
                ins.then_inc(s_out, 1)

        def node_sum(pe, src, dst, s_in, v, s_out):
            pe.wait_ge(s_in, v)
            for a in range(NT):
                ins = nc.tensor.matmul(dst, (lastmask if a == NT - 1 else ones)[:], src[:, a * D:(a + 1) * D],
                                       start=(a == 0), stop=(a == NT - 1))
            ins.then_inc(s_out, 1)

        def gather_sets(pool, name, table, idx, G, width, idx_now, full, frees):
            row = table.shape[1]
            s_ix, s_dummy = sem(name + "_ix"), sem(name + "_pd")
            with pool.Fori(0, SETS // NQ) as i:
                for q in range(NQ):
                    for f, per in frees:
                        pool.wait_ge(f, i * (NQ * per) + ((q + 1 - NQ) * per + CR))
                        pool.sem_inc(s_dummy, 1)
                    nc.gpsimd.tensor_copy(idx_now[:, 8 * q:8 * q + 8],
                                          idx[:, bass.ds(i * (8 * NQ) + 8 * q, 8)]).then_inc(s_ix, 1)
                    pool.wait_ge(s_ix, i * NQ + q + 1)
                    pool.sem_inc(s_dummy, 1)
                    for k in range(8):
                        o = (q * 8 + k) * width
                        pool.indirect_dma_start(
                            out=G[:, o:o + row], out_offset=None, in_=table,
                            in_offset=bass.IndirectOffsetOnAxis(ap=idx_now[:, 8 * q + k:8 * q + k + 1], axis=0)
                        ).then_inc(full[q], 16)

        def each_set(eng, step, between=()):
            at = 0
            for part in tuple(between) + (None,):
                with eng.Fori(at, at + 2 if part else SETS // NQ - 1) as i:
                    for q in range(NQ):
                        step(i, q, i * NQ + q, NQ)
                if part:
                    part()
                    at += 2
            i = SETS // NQ - 1
            for q in range(NQ):
                step(i, q, i * NQ + q, NQ - 1 - q)

        def after(i, q, n=1):
            return i + (q + n) // NQ, (q + n) % NQ, i * NQ + (q + n)

        def stage_scores(name, heads, table, width, node_tab, node_w, spill, aside=None):
            o_g = NT * node_w if heads == 4 else 256
            o_db = o_g + NQ * 8 * width
            G = A[:, o_g:o_db]
            DB = [A[:, o_db + 1024 * i:o_db + 1024 * (i + 1)] for i in range(2)]
            MT = [A[:, o_db + 2048 + 1024 * i:o_db + 3072 + 1024 * i] for i in range(2)]
            o_t = o_db + 4096
            t1, t2 = A[:, o_t:o_t + 64], A[:, o_t + 64:o_t + 128]
            prod = [A[:, o_t + 128 + 516 * i:o_t + 644 + 516 * i] for i in range(4)]
            o_t += 2400 if heads == 4 else 128
            idx_now = A[:, o_t:o_t + 8 * NQ].bitcast(I32)
            assert o_t + 8 * NQ <= ARENA
            full = [sem(f"{name}_g{q}") for q in range(NQ)]
            db_full = [sem(f"{name}_db{q}") for q in range(2)]
            mt_done, mm_done, read_done, spilled, spill_free = (sem(name + x) for x in
                                                                ("_mt", "_mm", "_rd", "_sp", "_sf"))
            mul_done, act_red = sem(name + "_mul"), sem(name + "_ar")
            s_c, s_vd, s_pd = sem(name + "_c"), sem(name + "_vd"), sem(name + "_ed")
            rows = drel_rows.rearrange("j e -> (j e)").unsqueeze(0)
            with nc.Block() as block:
                @block.gpsimd
                def _(pool):
                    gather_sets(pool, name, table, idx_src, G, width, idx_now, full,
                                [(read_done, 1), (spill_free, 1)])

                if heads == 4:
                    @block.scalar
                    def _(act):
                        act.sem_inc(act_red, CR)
                        with act.Fori(0, SETS // NQ) as i:
                            for q in range(NQ):
                                act.wait_ge(read_done, i * NQ + (q + 1 - 2 + CR))
                                for k in range(8):
                                    act.wait_ge(mul_done, i * (8 * NQ) + (q * 8 + k + 1 + CR))
                                    for h in (2, 3):
                                        o = 32 * (q % 2) + 4 * k + h
                                        pr = prod[k % 4][:, h * width:(h + 1) * width]
                                        ins = nc.scalar.activation(pr, pr, ACT.Copy, accum_out=t1[:, o:o + 1])
                                    ins.then_inc(act_red, 1)

                @block.sync
                def _(sp):
                    sp.sem_inc(spill_free, CR)

                    def load_dst(i, q, s):
                        sp.dma_start(DB[q % 2], rows[0:1, bass.ds(s * 1024, 1024)].to_broadcast([P, 1024])
                                     ).then_inc(db_full[q % 2], 16)

                    def step(i, q, s, more):
                        sp.wait_ge(full[q], i * 128 + 128)
                        sp.dma_start(spill[bass.ds(s, 1), :, :].rearrange("o p f -> (o p) f"),
                                     G[:, q * 8 * width:(q + 1) * 8 * width]).then_inc(spilled, 16)
                        if more >= 2:
                            sp.wait_ge(mt_done, s + (1 + CR))
                            load_dst(*after(i, q, 2))
                        sp.wait_ge(spilled, s * 16 + 16)
                        sp.sem_inc(spill_free, 1)

                    load_dst(0, 0, 0)
                    load_dst(0, 1, 1)
                    if aside:
                        aside.loads(sp)
                    each_set(sp, step)
                    if aside:
                        aside.stores(sp)

                if aside:
                    @block.scalar
                    def _(act):
                        aside.scalar(act)

                @block.tensor
                def _(pe):
                    pe.sem_inc(mm_done, CR)

                    def step(i, q, s, more):
                        tiles = load_tiles(mybir.EngineType.PE, ntile, s * 4, NT - 1)
                        pe.wait_ge(mt_done, s + 1 + CR)
                        if heads == 8:
                            pe.wait_ge(read_done, s + (1 - 2 + CR))
                        for k in range(8):
                            n = tiles[k // 2]
                            lhsT = MT[q % 2][:, k * P:(k + 1) * P]
                            if heads == 8:
                                ins = nc.tensor.matmul(PS[:, (q % 2) * 512 + k * 8:(q % 2) * 512 + k * 8 + 8], lhsT,
                                                       node_tab[:, bass.ds(n * 8, 8)], start=True, stop=True)
                            else:
                                pe.wait_ge(mul_done, s * 8 + (k + 1 - 4 + CR))
                                for c in range(2):
                                    b = ((k % 4) * 2 + c) * 512
                                    ins = nc.tensor.matmul(PS[:, b:b + 258], lhsT,
                                                           node_tab[:, bass.ds(n * 516 + 258 * c, 258)],
                                                           start=True, stop=True)
                                ins.then_inc(s_pd, 1)
                        if heads == 8:
                            ins.then_inc(mm_done, 1)

                    each_set(pe, step, aside.tensor(pe) if aside else ())

                @block.vector
                def _(dve):
                    if heads == 4:
                        ch = Chain(name + "_c0", dve)
                        ch(dve.memset(G, 1.0))
                        dve.sem_inc(mul_done, CR)
                    dve.sem_inc(mt_done, CR)
                    dve.sem_inc(read_done, CR)

                    def onehots(i, q, s):
                        dve.wait_ge(db_full[q % 2], i * (8 * NQ) + (16 * (q // 2) + 16))
                        if heads == 8:
                            dve.wait_ge(mm_done, s + (1 - 2 + CR))
                        else:
                            dve.wait_ge(mul_done, s * 8 + (8 - 16 + CR))
                        nc.vector.tensor_scalar(MT[q % 2], DB[q % 2], pidx[:, 0:1], None,
                                                ALU.is_equal).then_inc(mt_done, 1)

                    def step(i, q, s, more):
                            if more:
                                onehots(*after(i, q))
                            g3 = G[:, q * 8 * width:(q + 1) * 8 * width].rearrange("p (k f) -> p k f", f=width)
                            dve.wait_ge(full[q], i * 128 + 128)
                            pen_b = bc_in(pen[:, bass.ds(s * 8, 8)], heads)
                            o = att[:, bass.ds(s * (8 * heads), 8 * heads)].rearrange("p (k h) -> p k h", h=heads)
                            if heads == 8:
                                dve.wait_ge(mm_done, s + 1 + CR)
                                p3 = PS[:, (q % 2) * 512:(q % 2) * 512 + 64].rearrange("p (k h) -> p k h", h=8)
                                a3 = t1.rearrange("p (k h) -> p k h", h=8)
                                nc.vector.tensor_tensor(a3, p3, g3[:, :, 128:136], ALU.add).then_inc(read_done, 1)
                                dve.wait_ge(read_done, s + 1 + CR)
                                nc.vector.scalar_tensor_tensor(t2, t1, 0.2, t1, ALU.mult, ALU.max).then_inc(s_c, 1)
                                dve.wait_ge(s_c, s + 1)
                                nc.vector.tensor_tensor(o, t2.rearrange("p (k h) -> p k h", h=8), pen_b,
                                                        ALU.add).then_inc(s_vd, 1)
                            else:
                                def reduce_slot(k):
                                    return nc.vector.tensor_reduce(
                                        t1[:, 32 * (q % 2) + 4 * k:32 * (q % 2) + 4 * k + 2],
                                        prod[k % 4][:, 0:258].rearrange("p (h f) -> p h f", h=2), AX_X,
                                        ALU.add).then_inc(s_vd, 1)

                                for k in range(8):
                                    c = s * 8 + k
                                    dve.wait_ge(s_pd, c + 1)
                                    dve.wait_ge(act_red, c + (1 - 4 + CR))
                                    b = (k % 4) * 1024
                                    p4 = PS[:, b:b + 1024].rearrange("p (b f) -> p b f", b=2)
                                    xs = g3[:, k, :].unsqueeze(1).unsqueeze(1).to_broadcast([P, 2, 2, width])
                                    nc.vector.tensor_tensor(
                                        prod[k % 4].rearrange("p (b h f) -> p b h f", b=2, h=2),
                                        p4[:, :, 0:258].rearrange("p b (h f) -> p b h f", h=2), xs,
                                        ALU.mult).then_inc(mul_done, 1)
                                    if k:
                                        dve.wait_ge(mul_done, c + CR)
                                        reduce_slot(k - 1)
                                dve.wait_ge(mul_done, s * 8 + 8 + CR)
                                reduce_slot(7)
                                dve.wait_ge(s_vd, s * 8 + 8)
                                dve.wait_ge(act_red, s * 8 + 8 + CR)
                                nc.vector.tensor_tensor(
                                    o, t1[:, 32 * (q % 2):32 * (q % 2) + 32].rearrange("p (k h) -> p k h", h=4), pen_b,
                                    ALU.add).then_inc(read_done, 1)

                    onehots(0, 0, 0)
                    each_set(dve, step, aside.vector(dve) if aside else ())

        def stage_softmax(name, heads):
            C = P // heads
            L = K * P // C
            XS, KEY, RST, SC = (A[:, i * 6656:i * 6656 + L] for i in range(4))
            stage = [A[0:JB, 26624 + 512 * i:27136 + 512 * i] for i in range(4)]
            f4, c4, c2 = A[:, 28672:28676], A[0:heads, 28704:28704 + 4 * C], A[0:heads, 28832:28832 + 2 * C]
            w = [A[0:heads, 28960 + 32 * i:28960 + 32 * i + C] for i in range(6)]
            pq = A[:, 29216:29218]
            a3 = att[:, 0:K * heads].rearrange("p (k h) -> p k h", h=heads)
            HG = heads // 4
            s_tp, s_ev, s_st, s_ld, s_key, s_f4, s_c4, s_c2, s_pq, s_exp, s_pr, s_lp, s_t2, s_sub = (
                sem(name + f"_{i}") for i in range(14))
            s_lo = [sem(f"{name}_lo{i}") for i in range(4)]
            s_lq = [sem(f"{name}_lq{i}") for i in range(4)]
            JOBS = 8 * HG

            def rows_of(d, j):
                b, g = j // HG, j % HG
                return d[4 * g:4 * g + 4, b * JB:(b + 1) * JB, :].rearrange("h k e -> k h e")
            with nc.Block() as block:
                @block.tensor
                def _(pe):
                    for j in range(JOBS):
                        if j >= 8:
                            pe.wait_ge(s_ev, j - 7)
                        for h in range(4):
                            o = (j % 8) * 512 + h * P
                            ins = nc.tensor.transpose(PS[0:JB, o:o + P],
                                                      a3[:, (j // HG) * JB:(j // HG + 1) * JB, 4 * (j % HG) + h],
                                                      ident[:])
                        ins.then_inc(s_tp, 1)
                    for j in range(JOBS):
                        pe.wait_ge(s_lo[j % 4], 16 * (j // 4 + 1))
                        if j < 8:
                            pe.wait_ge(s_ev, JOBS)
                        else:
                            pe.wait_ge(s_t2, j - 7)
                        for h in range(4):
                            o = (j % 8) * 512 + h * JB
                            ins = nc.tensor.transpose(PS[:, o:o + JB], stage[j % 4][:, h * P:(h + 1) * P],
                                                      ident[0:JB, 0:JB])
                        ins.then_inc(s_lp, 1)

                @block.scalar
                def _(act):
                    for j in range(JOBS):
                        act.wait_ge(s_tp, j + 1)
                        if j >= 4:
                            act.wait_ge(s_lq[j % 4], 16 * (j // 4))
                        nc.scalar.copy(stage[j % 4], PS[0:JB, (j % 8) * 512:(j % 8) * 512 + 512]).then_inc(s_ev, 1)
                    act.wait_ge(s_sub, 1)
                    nc.scalar.activation(XS, XS, ACT.Exp).then_inc(s_exp, 1)

                @block.sync
                def _(sp):
                    for h in range(heads):
                        sp.dma_start(KEY[h * C:(h + 1) * C, :],
                                     key_rows.rearrange("j e -> (j e)").rearrange("(c l) -> c l", c=C)
                                     ).then_inc(s_key, 16)
                    for j in range(JOBS):
                        sp.wait_ge(s_ev, j + 1)
                        sp.dma_start(rows_of(score_rows, j), stage[j % 4].rearrange("k (h e) -> k h e", h=4)
                                     ).then_inc(s_lq[j % 4], 16)
                    for i in range(4):
                        sp.wait_ge(s_lq[i], 16 * (JOBS // 4))
                    sp.dma_start(XS, score_rows[0:heads].rearrange("h k e -> (h k e)").rearrange("(q l) -> q l", q=P)
                                 ).then_inc(s_ld, 16)
                    sp.wait_ge(s_f4, 1)
                    sp.dma_start(carry_a, f4).then_inc(s_c4, 16)
                    sp.wait_ge(s_c4, 16)
                    sp.dma_start(c4, carry_a.rearrange("(h c) v -> h (c v)", h=heads)).then_inc(s_c4, 16)
                    sp.wait_ge(s_c2, 1)
                    sp.dma_start(carry_b.rearrange("(h c) v -> h (c v)", h=heads), c2).then_inc(s_pq, 16)
                    sp.wait_ge(s_pq, 16)
                    sp.dma_start(pq, carry_b).then_inc(s_pq, 16)
                    sp.wait_ge(s_exp, 1)
                    sp.dma_start(prob_rows[0:heads].rearrange("h k e -> (h k e)").rearrange("(q l) -> q l", q=P), XS
                                 ).then_inc(s_pr, 16)
                    sp.wait_ge(s_pr, 16)
                    for j in range(JOBS):
                        if j >= 4:
                            sp.wait_ge(s_lp, j - 3)
                        sp.dma_start(stage[j % 4].rearrange("k (h e) -> k h e", h=4), rows_of(prob_rows, j)
                                     ).then_inc(s_lo[j % 4], 16)

                @block.vector
                def _(dve):
                    ch = Chain(name + "_cv", dve)
                    dve.wait_ge(s_key, 16 * heads)
                    ch(dve.tensor_tensor(RST[:, 1:L], KEY[:, 1:L], KEY[:, 0:L - 1], ALU.is_equal))
                    ch(dve.tensor_scalar(RST[:, 1:L], RST[:, 1:L], -1.0, BIG, ALU.add, ALU.mult))
                    ch(dve.memset(RST[:, 0:1], -BIG))
                    dve.wait_ge(s_ld, 16)
                    ch(dve.tensor_tensor_scan(SC, RST, XS, -BIG, ALU.add, ALU.max))
                    ch(dve.tensor_tensor_scan(SC[:, 0:L - 1][:, ::-1], RST[:, 1:L][:, ::-1], SC[:, 0:L - 1][:, ::-1],
                                              SC[:, L - 1:L], ALU.add, ALU.max))
                    dve.tensor_copy(f4[:, 0:1], SC[:, 0:1])
                    dve.tensor_copy(f4[:, 1:2], SC[:, L - 1:L])
                    dve.tensor_copy(f4[:, 2:3], KEY[:, 0:1])
                    dve.tensor_copy(f4[:, 3:4], KEY[:, L - 1:L]).then_inc(s_f4, 1)
                    dve.wait_ge(s_c4, 32)
                    c43 = c4.rearrange("h (c v) -> h c v", v=4)
                    F, T, KF, KL = (c43[:, :, v] for v in range(4))
                    cont, single, link, run, tmpw, zero = w
                    ch(dve.memset(cont[:, 0:1], -BIG))
                    ch(dve.tensor_tensor(cont[:, 1:C], KF[:, 1:C], KL[:, 0:C - 1], ALU.is_equal))
                    ch(dve.tensor_scalar(cont[:, 1:C], cont[:, 1:C], -1.0, BIG, ALU.add, ALU.mult))
                    ch(dve.tensor_tensor(single, KF, KL, ALU.is_equal))
                    ch(dve.tensor_scalar(single, single, -1.0, BIG, ALU.add, ALU.mult))
                    c23 = c2.rearrange("h (c v) -> h c v", v=2)
                    ch(dve.memset(c2, -BIG))
                    ch(dve.tensor_tensor(link, cont, single, ALU.add))
                    ch(dve.tensor_tensor_scan(run, link, T, -BIG, ALU.add, ALU.max))
                    ch(dve.tensor_tensor(c23[:, 1:C, 0], run[:, 0:C - 1], cont[:, 1:C], ALU.add))
                    ch(dve.tensor_tensor(link[:, 0:C - 1], cont[:, 1:C], single[:, 0:C - 1], ALU.add))
                    ch(dve.memset(link[:, C - 1:C], -BIG))
                    ch(dve.tensor_tensor_scan(run[:, ::-1], link[:, ::-1], F[:, ::-1], -BIG, ALU.add, ALU.max))
                    dve.tensor_tensor(c23[:, 0:C - 1, 1], run[:, 1:C], cont[:, 1:C], ALU.add).then_inc(s_c2, 1)
                    dve.wait_ge(s_pq, 32)
                    for v, at in ((0, 0), (1, L - 1)):
                        ch(dve.tensor_scalar(RST, KEY, KEY[:, at:at + 1], None, ALU.is_equal))
                        ch(dve.tensor_scalar(RST, RST, -1.0, BIG, ALU.add, ALU.mult))
                        ch(dve.scalar_tensor_tensor(SC, RST, pq[:, v:v + 1], SC, ALU.add, ALU.max))
                    dve.tensor_tensor(XS, XS, SC, ALU.subtract).then_inc(s_sub, 1)
                    for j in range(JOBS):
                        dve.wait_ge(s_lp, j + 1)
                        b, g = j // HG, j % HG
                        o = a3[:, b * JB:(b + 1) * JB, 4 * g:4 * g + 4].rearrange("p k h -> p h k")
                        dve.tensor_copy(o, PS[:, (j % 8) * 512:(j % 8) * 512 + 4 * JB]
                                        .rearrange("p (h k) -> p h k", h=4)).then_inc(s_t2, 1)

        def stage_aggregate(name, acc, chunks, heads=0, spill=None, width=D, table=None, idx=None, weighted=False,
                            edge_w=None, aside=None):
            W = sum(chunks)
            o = acc[1]
            ACC = A[:, acc[0]:acc[0] + NT * W]
            G = A[:, o:o + NQ * 8 * width]
            o += NQ * 8 * width
            M = [A[:, o + 1024 * i:o + 1024 * (i + 1)] for i in range(2)]
            o += 2048
            Y = [A[:, o + 8 * W * i:o + 8 * W * (i + 1)] for i in range(2)] if heads or edge_w is not None else None
            o += 16 * W if Y else 0
            if edge_w is not None:
                GE = A[:, o:o + NQ * 1024]
                o += NQ * 1024
            dcol = A[:, o:o + 8 * NQ]
            wcol = A[:, o + 32:o + 32 + 8 * NQ]
            idx_now = A[:, o + 64:o + 64 + 8 * NQ].bitcast(I32)
            assert o + 96 <= ARENA, (name, o)
            RG = 4 if len(chunks) == 2 or edge_w is not None or aside else 8
            full = [sem(f"{name}_g{q}") for q in range(NQ)]
            attr_full = [sem(f"{name}_at{q}") for q in range(NQ)]
            m_done, y_done, sum_done, add_done, z_done, r_done = (sem(name + x) for x in
                                                                  ("_m", "_y", "_s", "_a", "_z", "_r"))
            s_v, s_dd, s_ones = sem(name + "_v"), sem(name + "_dd"), sem(name + "_one")
            ya_done = sem(name + "_ya")
            mp_done = sem(name + "_mp")
            lead = len(chunks)
            MV = 5 if heads == 8 else 8

            def region(ss, c):
                return ((ss % RG) * lead + c) * 512
            with nc.Block() as block:
                @block.sync
                def _(sp):
                    if aside:
                        aside.loads(sp)
                        aside.stores(sp)
                    if spill is not None:
                        with sp.Fori(0, SETS // NQ) as i:
                            for q in range(NQ):
                                sp.wait_ge(y_done, i * NQ + (q + 1 - NQ + CR))
                                if heads == 4:
                                    sp.wait_ge(ya_done, i * NQ + (q + 1 - NQ + CR))
                                sp.dma_start(G[:, q * 8 * width:(q + 1) * 8 * width],
                                             spill[bass.ds(i * NQ + q, 1), :, :].rearrange("o p f -> (o p) f")
                                             ).then_inc(full[q], 16)
                    if edge_w is not None:
                        sp.wait_ge(s_ones, 1)
                        with sp.Fori(0, SETS // NQ) as i:
                            for q in range(NQ):
                                s = i * NQ + q
                                sp.wait_ge(z_done, s + (1 - NQ + CR))
                                for u in range(4):
                                    e = sp.value_load(estep[0:1, bass.ds(s * 4 + u, 1)], min_val=0, max_val=ST - 1)
                                    sp.dma_start(GE[0:16, (q * 4 + u) * 256:(q * 4 + u + 1) * 256]
                                                 .rearrange("f (g e) -> f g e", g=2),
                                                 t["attr_t"][bass.ds(e * 2, 2), :, :].rearrange("g f e -> f g e")
                                                 ).then_inc(attr_full[q], 16)

                if heads:
                    @block.gpsimd
                    def _(pool):
                        pool.sem_inc(y_done, CR)
                        with pool.Fori(0, SETS // NQ) as i:
                            for q in range(NQ):
                                s = i * NQ + q
                                pool.wait_ge(sum_done, s * 4 + (4 - 8 + CR))
                                if heads == 8:
                                    pool.wait_ge(s_v, s + 1)
                                    pool.sem_inc(s_dd, 1)
                                    for k in range(MV, 8):
                                        ins = nc.gpsimd.tensor_scalar(
                                            M[q % 2][:, k * P:(k + 1) * P], iota_row[:],
                                            dcol[:, 8 * q + k:8 * q + k + 1], None, ALU.is_equal)
                                    ins.then_inc(mp_done, 1)
                                pool.wait_ge(full[q], i * 16 + 16)
                                y3 = Y[q % 2].rearrange("p (k f) -> p k f", f=W)
                                g3 = G[:, q * 8 * width:(q + 1) * 8 * width].rearrange("p (k f) -> p k f", f=width)
                                p3 = att[:, bass.ds(s * (8 * heads), 8 * heads)].rearrange("p (k h) -> p k h", h=heads)
                                if heads == 8:
                                    nc.gpsimd.tensor_copy(y3[:, :, D:D + 8], p3)
                                    nc.gpsimd.tensor_tensor(y3[:, :, 0:D].rearrange("p k (h c) -> p k h c", h=8),
                                                            g3[:, :, 0:D].rearrange("p k (h c) -> p k h c", h=8),
                                                            bc_in(p3, 16), ALU.mult).then_inc(y_done, 1)
                                else:
                                    for c in range(2):
                                        nc.gpsimd.tensor_copy(y3[:, :, c * 258 + 256:c * 258 + 258],
                                                              p3[:, :, 2 * c:2 * c + 2])
                                    for h in range(2):
                                        ins = nc.gpsimd.tensor_tensor(y3[:, :, h * D:(h + 1) * D], g3[:, :, 0:D],
                                                                      bc_in(p3[:, :, h], D), ALU.mult)
                                    ins.then_inc(y_done, 1)

                if table is not None:
                    @block.gpsimd
                    def _(pool):
                        gather_sets(pool, name, table, idx, G, width, idx_now, full,
                                    [(sum_done, 4) if edge_w is None else (r_done, 1)])

                @block.scalar
                def _(act):
                    if aside:
                        aside.scalar(act)
                    if heads == 4:
                        act.sem_inc(ya_done, CR)
                        with act.Fori(0, SETS // NQ) as i:
                            for q in range(NQ):
                                s = i * NQ + q
                                act.wait_ge(full[q], i * 16 + 16)
                                act.wait_ge(sum_done, s * 4 + (4 - 8 + CR))
                                act.sem_inc(s_ones, 1)
                                y3 = Y[q % 2].rearrange("p (k f) -> p k f", f=W)
                                for k in range(8):
                                    for h in (2, 3):
                                        o = 258 + (h - 2) * D
                                        ins = nc.scalar.activation(
                                            y3[:, k, o:o + D], G[:, (q * 8 + k) * width:(q * 8 + k) * width + D],
                                            ACT.Copy, scale=att[:, bass.ds(s * 32 + (k * 4 + h), 1)])
                                ins.then_inc(ya_done, 1)
                    if edge_w is not None:
                        act.sem_inc(r_done, CR)
                        with act.Fori(0, SETS // NQ) as i:
                            for q in range(NQ):
                                s = i * NQ + q
                                act.wait_ge(sum_done, s * 4 + (4 - 8 + CR))
                                act.wait_ge(full[q], i * 128 + 128)
                                act.sem_inc(s_dd, 1)
                                y3 = Y[q % 2].rearrange("p (k f) -> p k f", f=W)
                                for k in range(8):
                                    nc.scalar.activation(y3[:, k, 0:D], G[:, (q * 8 + k) * D:(q * 8 + k + 1) * D],
                                                         ACT.Copy, scale=wgt[:, bass.ds(s * 8 + k, 1)])
                                act.wait_ge(z_done, s + 1 + CR)
                                for v in range(2):
                                    b = 2048 + (q % 2) * 1024 + v * 512
                                    ins = nc.scalar.activation(
                                        y3[:, 4 * v:4 * v + 4, D:2 * D],
                                        PS[:, b:b + 512].rearrange("p (k f) -> p k f", f=D), ACT.Relu)
                                ins.then_inc(r_done, 1)

                @block.tensor
                def _(pe):
                    pe.sem_inc(sum_done, CR)
                    if edge_w is not None:
                        pe.sem_inc(z_done, CR)
                    def features(i, q, s):
                        pe.wait_ge(attr_full[q], i * 64 + 64)
                        pe.wait_ge(r_done, s + (1 - 2 + CR))
                        for k in range(8):
                            b = 2048 + (q % 2) * 1024 + k * P
                            ins = nc.tensor.matmul(PS[:, b:b + P], GE[0:17, (q * 8 + k) * P:(q * 8 + k + 1) * P],
                                                   edge_w, start=True, stop=True)
                        ins.then_inc(z_done, 1)

                    def step(i, q, s, more):
                            if edge_w is not None:
                                if more:
                                    features(*after(i, q))
                                pe.wait_ge(r_done, s + 1 + CR)
                            elif table is not None:
                                pe.wait_ge(full[q], i * 128 + 128)
                            if heads:
                                pe.wait_ge(y_done, s + 1 + CR)
                            if heads == 4:
                                pe.wait_ge(ya_done, s + 1 + CR)
                            pe.wait_ge(m_done, s + 1)
                            if heads == 8:
                                pe.wait_ge(mp_done, s + 1)
                            for u in range(4):
                                ss = s * 4 + u
                                pe.wait_ge(add_done, ss * 2 + (2 - 2 * RG + CR))
                                for c, wc in enumerate(chunks):
                                    b, at = region(q * 4 + u, c), sum(chunks[:c])
                                    for g in range(2):
                                        k = 2 * u + g
                                        rhs = (Y[q % 2][:, k * W + at:k * W + at + wc] if Y else
                                               G[:, (q * 8 + k) * width:(q * 8 + k) * width + wc])
                                        ins = nc.tensor.matmul(PS[:, b:b + wc], M[q % 2][:, k * P:(k + 1) * P], rhs,
                                                               start=(g == 0), stop=(g == 1))
                                ins.then_inc(sum_done, 1)

                    if edge_w is not None:
                        pe.wait_ge(s_ones, 1)
                        features(0, 0, 0)
                    each_set(pe, step, aside.tensor(pe) if aside else ())

                @block.vector
                def _(dve):
                    ch = Chain(name + "_c0", dve)
                    ch(dve.memset(ACC, 0.0))
                    if edge_w is not None:
                        ch(dve.memset(GE[0:32, :], 1.0))
                        for y in Y:
                            ch(dve.memset(y.rearrange("p (k f) -> p k f", f=W)[:, :, 2 * D:2 * D + 1], 1.0))
                        dve.sem_inc(s_ones, 1)
                    dve.sem_inc(add_done, CR)

                    def prepare(i, q, s, load=lambda: None):
                        dve.wait_ge(sum_done, s * 4 + (4 - 8 + CR))
                        nc.vector.tensor_scalar(dcol[:, 8 * q:8 * q + 8], drel[:, bass.ds(s * 8, 8)], 1.0, None,
                                                ALU.mult).then_inc(s_v, 1)
                        if weighted:
                            nc.vector.tensor_scalar(wcol[:, 8 * q:8 * q + 8], wgt[:, bass.ds(s * 8, 8)], 1.0, None,
                                                    ALU.mult).then_inc(s_v, 1)
                        dve.wait_ge(s_v, s * 2 + 2 if weighted else s + 1)
                        for k in range(MV):
                            c = 8 * q + k
                            if weighted:
                                ins = nc.vector.tensor_scalar(M[q % 2][:, k * P:(k + 1) * P], iota_row[:],
                                                              dcol[:, c:c + 1], wcol[:, c:c + 1], ALU.is_equal, ALU.mult)
                            else:
                                ins = nc.vector.tensor_scalar(M[q % 2][:, k * P:(k + 1) * P], iota_row[:],
                                                              dcol[:, c:c + 1], None, ALU.is_equal)
                        ins.then_inc(m_done, 1)
                        tiles = load()
                        return tiles

                    def add_up(q, s, tiles):
                        for u, n in enumerate(tiles):
                            ss = s * 4 + u
                            dve.wait_ge(sum_done, ss + 1 + CR)
                            if heads == 8:
                                dve.wait_ge(add_done, ss * 2 + CR)
                                a = ACC[:, bass.ds(n * W, W)]
                                b = region(q * 4 + u, 0)
                                nc.vector.tensor_tensor(a, a, PS[:, b:b + W], ALU.add).then_inc(add_done, 2)
                                continue
                            for v in range(2):
                                dve.wait_ge(add_done, ss * 2 + (v - 1 + CR))
                                lo, hi = ((0, W // 2), (W // 2, W))[v]
                                b = region(q * 4 + u, v if lead == 2 else 0) + (0 if lead == 2 else lo)
                                a = ACC[:, bass.ds(n * W + lo, hi - lo)]
                                nc.vector.tensor_tensor(a, a, PS[:, b:b + hi - lo], ALU.add).then_inc(add_done, 1)

                    def tiles_of(s):
                        return load_tiles(mybir.EngineType.DVE, ntile, s * 4, NT - 1)

                    def step(i, q, s, more):
                        if more:
                            tiles = prepare(*after(i, q), lambda: tiles_of(s))
                        else:
                            tiles = tiles_of(s)
                        add_up(q, s, tiles)

                    prepare(0, 0, 0)
                    each_set(dve, step, aside.vector(dve) if aside else ())
            return ACC

        def bn_vector(dve, ch, name, Z, SQ, gamma, beta, v, mean_scale=None):
            mean, var, std = v[0:3]
            s_z, s_sum, s_var, s_std = v[3]
            ch(dve.tensor_copy(mean, mean))
            s_z_sem = s_z
            dve.sem_inc(s_z_sem, 1)
            dve.wait_ge(s_sum, 1)
            ch(dve.tensor_scalar(mean, PS[:, 3584:3584 + D], 1.0 / N, None, ALU.mult))
            if mean_scale is not None:
                ch(dve.tensor_tensor(mean, mean, mean_scale, ALU.mult))
            ch(dve.tensor_tensor(v3(Z), v3(Z), bc_mid(mean, NT), ALU.subtract))
            dve.tensor_tensor(SQ, Z, Z, ALU.mult).then_inc(s_z, 1)
            dve.wait_ge(s_sum, 2)
            dve.tensor_scalar(var, PS[:, 3584:3584 + D], 1.0 / N, LN_EPS, ALU.mult, ALU.add).then_inc(s_var, 1)
            dve.wait_ge(s_std, 1)
            ch(dve.reciprocal(std, std))
            ch(dve.tensor_tensor(std, std, gamma, ALU.mult))
            ch(dve.tensor_tensor(v3(Z), v3(Z), bc_mid(std, NT), ALU.mult))
            ch(dve.tensor_tensor(v3(Z), v3(Z), bc_mid(beta, NT), ALU.add))

        def bn_sems(name):
            return tuple(sem(f"{name}_bn{x}") for x in ("z", "sum", "var", "std"))

        def bn_tensor(pe, Z, SQ, sems):
            s_z, s_sum, _, _ = sems
            node_sum(pe, Z, PS[:, 3584:3584 + D], s_z, 1, s_sum)
            node_sum(pe, SQ, PS[:, 3584:3584 + D], s_z, 2, s_sum)

        def bn_scalar(act, var, std, sems):
            act.wait_ge(sems[2], 1)
            nc.scalar.activation(std, var, ACT.Sqrt).then_inc(sems[3], 1)

        def stage_gat_table():
            s_w, s_mm, s_ev, s_st, s_tab = sem("g0_w"), sem("g0_mm"), sem("g0_ev"), sem("g0_st"), sem("g0_tab")
            ad = A[:, 0:NT * 8]
            tab = A[:, 256:256 + NT * 136].rearrange("p (t f) -> p t f", f=136)
            w, asb, adb = A[:, 4096:4224], A[:, 4224:4352], A[:, 4352:4480]
            tmp = A[:, 4608:4608 + NW]
            with nc.Block() as block:
                @block.sync
                def _(sp):
                    sp.dma_start(w, t["L0_gnn_W"]).then_inc(s_w, 16)
                    bcast_load(sp, asb, t["L0_gnn_att_src"].rearrange("h c -> (h c)")).then_inc(s_w, 16)
                    bcast_load(sp, adb, t["L0_gnn_att_dst"].rearrange("h c -> (h c)")).then_inc(s_w, 16)
                    sp.wait_ge(s_st, 1)
                    sp.dma_start(tab0.rearrange("(t p) f -> p t f", p=P), tab).then_inc(s_tab, 16)
                    sp.wait_ge(s_tab, 16)

                @block.tensor
                def _(pe):
                    pe.wait_ge(s_w, 48)
                    project_tiles(pe, HT, w, s_mm)

                @block.scalar
                def _(act):
                    for g in range(7):
                        a, b = 4 * g, min(4 * g + 4, NT)
                        act.wait_ge(s_mm, g + 1)
                        nc.scalar.copy(tab[:, a:b, 0:D], v3(PS[:, a * D:b * D])).then_inc(s_ev, 1)

                @block.vector
                def _(dve):
                    ch = Chain("g0_c", dve)
                    dve.wait_ge(s_w, 48)
                    dve.wait_ge(s_ev, 7)
                    ch(dve.tensor_tensor(v3(tmp), tab[:, :, 0:D], bc_mid(adb, NT), ALU.mult))
                    ch(dve.tensor_reduce(ad.rearrange("p (t h) -> p t h", h=8),
                                         tmp.rearrange("p (t h c) -> p t h c", t=NT, c=16), AX_X, ALU.add))
                    ch(dve.tensor_tensor(v3(tmp), tab[:, :, 0:D], bc_mid(asb, NT), ALU.mult))
                    dve.tensor_reduce(tab[:, :, D:D + 8], tmp.rearrange("p (t h c) -> p t h c", t=NT, c=16), AX_X,
                                      ALU.add).then_inc(s_st, 1)
            return ad

        def stage_gat_end(ACC):
            s_w = sem("g1_w")
            bn = bn_sems("g1")
            base = NT * 136
            Z, SQ = A[:, base:base + NW], A[:, base + NW:base + 2 * NW]
            rd = A[:, base + 2 * NW:base + 2 * NW + NT * 8]
            o = base + 2 * NW + 256
            bias, gam, bet, mean, var, std = (A[:, o + D * i:o + D * (i + 1)] for i in range(6))
            a3 = ACC.rearrange("p (t f) -> p t f", f=136)
            with nc.Block() as block:
                @block.sync
                def _(sp):
                    bcast_load(sp, bias, t["L0_gnn_bias"]).then_inc(s_w, 16)
                    bcast_load(sp, gam, t["L0_gnn_gamma"]).then_inc(s_w, 16)
                    bcast_load(sp, bet, t["L0_gnn_beta"]).then_inc(s_w, 16)

                @block.vector
                def _(dve):
                    ch = Chain("g1_c", dve)
                    ch(dve.memset(mean, 0.0))
                    r3 = rd.rearrange("p (t h) -> p t h", h=8)
                    ch(dve.tensor_scalar(r3, a3[:, :, D:D + 8], 1e-16, None, ALU.add))
                    ch(dve.reciprocal(rd, rd))
                    ch(dve.tensor_tensor(Z.rearrange("p (t h c) -> p t h c", t=NT, c=16),
                                         a3[:, :, 0:D].rearrange("p t (h c) -> p t h c", c=16), bc_in(r3, 16),
                                         ALU.mult))
                    dve.wait_ge(s_w, 48)
                    ch(dve.tensor_tensor(v3(Z), v3(Z), bc_mid(bias, NT), ALU.add))
                    bn_vector(dve, ch, "g1", Z, SQ, gam, bet, (mean, var, std, bn))
                    ch(dve.tensor_scalar(Z, Z, 0.0, None, ALU.max))
                    ch(dve.tensor_tensor(Z, Z, H[:], ALU.add))
                    ch(dve.tensor_tensor(X[:], X[:], Z, ALU.add))

                @block.tensor
                def _(pe):
                    bn_tensor(pe, Z, SQ, bn)

                @block.scalar
                def _(act):
                    bn_scalar(act, var, std, bn)

        def stage_rel_table(name, i, base):
            s_w, s_mm, s_ea, s_ev = (sem(name + x) for x in ("_w", "_mm", "_ea", "_ev"))
            s_out = [sem(f"{name}_o{i}") for i in range(4)]
            wr = A[:, base:base + 1024]
            tb = [A[:, base + 1024 * (i + 1):base + 1024 * (i + 2)] for i in range(4)]
            tab3 = tab_rel.rearrange("(t p r) o -> t p (r o)", p=P, r=R_REL)
            with nc.Block() as block:
                @block.sync
                def _(sp):
                    sp.dma_start(wr, rel_w[i]).then_inc(s_w, 16)
                    for a in range(NT):
                        sp.wait_ge(s_ea, a + 1)
                        sp.wait_ge(s_ev, a + 1)
                        sp.dma_start(tab3[a], tb[a % 4]).then_inc(s_out[a % 4], 16)
                    for j in range(4):
                        sp.wait_ge(s_out[j], 16 * len(range(j, NT, 4)))

                @block.vector
                def _(dve):
                    for a in range(NT):
                        dve.wait_ge(s_mm, a + 1)
                        if a >= 4:
                            dve.wait_ge(s_out[a % 4], 16 * (a // 4))
                        b = (a % 4) * 1024
                        dve.tensor_copy(tb[a % 4][:, 0:512], PS[:, b:b + 512]).then_inc(s_ev, 1)

                @block.scalar
                def _(act):
                    for a in range(NT):
                        act.wait_ge(s_mm, a + 1)
                        if a >= 4:
                            act.wait_ge(s_out[a % 4], 16 * (a // 4))
                        b = (a % 4) * 1024 + 512
                        nc.scalar.copy(tb[a % 4][:, 512:1024], PS[:, b:b + 512]).then_inc(s_ea, 1)

                @block.tensor
                def _(pe):
                    pe.wait_ge(s_w, 16)
                    for a in range(NT):
                        if a >= 4:
                            pe.wait_ge(s_ev, a - 3)
                            pe.wait_ge(s_ea, a - 3)
                        for c in range(2):
                            b = (a % 4) * 1024 + 512 * c
                            ins = nc.tensor.matmul(PS[:, b:b + 512], HT[:, a * P:(a + 1) * P],
                                                   wr[:, 512 * c:512 * (c + 1)], start=True, stop=True)
                        ins.then_inc(s_mm, 1)

        def stage_rel_end(name, ACC, bias_ap, first):
            s_w, s_h, s_t = sem(name + "_w"), sem(name + "_h"), sem(name + "_t")
            bias = A[:, ARENA - D:ARENA]
            with nc.Block() as block:
                @block.sync
                def _(sp):
                    bcast_load(sp, bias, bias_ap).then_inc(s_w, 16)

                @block.vector
                def _(dve):
                    ch = Chain(name + "_c", dve)
                    dve.wait_ge(s_w, 16)
                    a3 = ACC.rearrange("p (t f) -> p t f", t=NT)[:, :, 0:D]
                    ch(dve.tensor_tensor(a3, a3, bc_mid(bias, NT), ALU.add))
                    if first:
                        dve.tensor_scalar(v3(H[:]), a3, 0.0, None, ALU.max).then_inc(s_h, 7)
                    else:
                        ch(dve.tensor_tensor(X[:], X[:], ACC, ALU.add))
                if first:
                    @block.tensor
                    def _(pe):
                        transpose_tiles(pe, H, s_h, s_t)

                    @block.scalar
                    def _(act):
                        for g in range(7):
                            a, b = 512 * g, min(512 * g + 512, NP)
                            act.wait_ge(s_t, g + 1)
                            nc.scalar.copy(HT[:, a:b], PS[:, a:b])

        def stage_queries():
            s_w, s_tab, s_q, s_qe, s_u, s_ue = (sem("q_" + x) for x in ("w", "tab", "q", "qe", "u", "ue"))
            U = A[:, 0:NT * 516]
            o = NT * 516
            wq, wkt = A[:, o:o + 512], A[:, o + 512:o + 1024]
            bq, bk = A[:, o + 1024:o + 1028], A[:, o + 1028:o + 1032]
            qt = [A[:, o + 1040 + 512 * i:o + 1552 + 512 * i] for i in range(2)]
            with nc.Block() as block:
                @block.sync
                def _(sp):
                    sp.dma_start(wq, t["L2_gnn_Wq"]).then_inc(s_w, 16)
                    sp.dma_start(wkt.rearrange("c (h f) -> c h f", h=4), t["wk_t"].rearrange("(h c) f -> c h f", h=4)
                                 ).then_inc(s_w, 16)
                    sp.dma_start(bq, t["bq_t"]).then_inc(s_w, 16)
                    sp.dma_start(bk, t["bk_t"]).then_inc(s_w, 16)
                    sp.dma_start(tab_x.rearrange("(t p) f -> p t f", p=P), v3(H[:])).then_inc(s_tab, 16)
                    sp.wait_ge(s_tab, 16)

                @block.tensor
                def _(pe):
                    pe.wait_ge(s_w, 64)
                    for a in range(NT + 1):
                        if a < NT:
                            if a >= 2:
                                pe.wait_ge(s_qe, a - 1)
                            for h in range(4):
                                o = (a % 2) * 512 + h * P
                                ins = nc.tensor.matmul(PS[:, o:o + P], wq[:, h * P:(h + 1) * P],
                                                       HT[:, a * P:(a + 1) * P], start=True, stop=True)
                            ins.then_inc(s_q, 1)
                        if a > 0:
                            b = a - 1
                            pe.wait_ge(s_qe, b + 1)
                            if b >= 2:
                                pe.wait_ge(s_ue, b - 1)
                            for h in range(4):
                                o = 1024 + (b % 2) * 1024 + (h // 2) * 512
                                lhsT = qt[b % 2][:, h * P:(h + 1) * P]
                                nc.tensor.matmul(PS[:, o + (h % 2) * 129:o + (h % 2) * 129 + D], lhsT,
                                                 wkt[:, h * D:(h + 1) * D], start=True, stop=True)
                                ins = nc.tensor.matmul(PS[:, o + (h % 2) * 129 + D:o + (h % 2) * 129 + 129], lhsT, bk[:, h:h + 1],
                                                       start=True, stop=True)
                            ins.then_inc(s_u, 1)

                @block.vector
                def _(dve):
                    dve.wait_ge(s_w, 64)
                    for a in range(NT):
                        dve.wait_ge(s_q, a + 1)
                        if a >= 2:
                            dve.wait_ge(s_u, a - 1)
                        dve.tensor_tensor(qt[a % 2].rearrange("c (h n) -> c h n", h=4),
                                          PS[:, (a % 2) * 512:(a % 2) * 512 + 512].rearrange("c (h n) -> c h n", h=4),
                                          bc_in(bq, P), ALU.add).then_inc(s_qe, 1)

                @block.scalar
                def _(act):
                    for a in range(NT):
                        act.wait_ge(s_u, a + 1)
                        o = 1024 + (a % 2) * 1024
                        nc.scalar.activation(U[:, a * 516:(a + 1) * 516].rearrange("p (c f) -> p c f", c=2),
                                             PS[:, o:o + 1024].rearrange("p (c f) -> p c f", c=2)[:, :, 0:258],
                                             ACT.Copy, scale=float(D) ** -0.5).then_inc(s_ue, 1)
            return U

        def stage_transformer_end(ACC):
            names = ("w", "zn", "zt", "ze", "at", "ae", "o", "oe", "sk", "ske", "gate", "sig", "gelu", "g")
            s_w, s_zn, s_zt, s_ze, s_at, s_ae, s_o, s_oe, s_sk, s_ske, s_gate, s_sig, s_gin, s_gelu = (
                sem("t_" + x) for x in names)
            bn = bn_sems("t")
            o = NT * 516
            OUT, SK, T1 = (A[:, o + NW * i:o + NW * (i + 1)] for i in range(3))
            o += 3 * NW
            wv, wsk = A[:, o:o + 512], A[:, o + 512:o + 640]
            bv = A[0:4, o + 640:o + 768]
            vec = [A[:, o + 768 + D * i:o + 896 + D * i] for i in range(10)]
            bsk, wb1, wb2, wb3, gw, gb, gm, mean, var, std = vec
            o += 768 + 1280
            rd, ra = A[:, o:o + 100], A[:, o + 100:o + 200]
            gt, sg = A[:, o + 200:o + 225], A[:, o + 232:o + 257]
            zt = [A[:, o + 260 + 512 * i:o + 772 + 512 * i] for i in range(2)]
            aT = [A[0:4, o + 1284 + P * i:o + 1412 + P * i] for i in range(2)]
            assert o + 1540 <= ARENA
            a4 = ACC.rearrange("p (t c f) -> p t c f", c=2, f=258)
            r4 = rd.rearrange("p (t c h) -> p t c h", c=2, h=2)
            T2 = A[:, 0:NW]
            with nc.Block() as block:
                @block.sync
                def _(sp):
                    sp.dma_start(wv, t["L2_gnn_Wv"]).then_inc(s_w, 16)
                    sp.dma_start(wsk, t["L2_gnn_Wskip"]).then_inc(s_w, 16)
                    sp.dma_start(bv, t["L2_gnn_bv"].rearrange("(h c) -> h c", h=4)).then_inc(s_w, 16)
                    bcast_load(sp, bsk, t["L2_gnn_bskip"]).then_inc(s_w, 16)
                    for i, w in enumerate((wb1, wb2, wb3)):
                        bcast_load(sp, w, t["L2_gnn_Wbeta"][i * D:(i + 1) * D]).then_inc(s_w, 16)
                    bcast_load(sp, gw, t["L2_gnn_gn_weight"]).then_inc(s_w, 16)
                    bcast_load(sp, gb, t["L2_gnn_gn_bias"]).then_inc(s_w, 16)
                    bcast_load(sp, gm, t["L2_gnn_gn_mean_scale"]).then_inc(s_w, 16)

                @block.tensor
                def _(pe):
                    pe.wait_ge(s_w, 160)
                    pe.wait_ge(s_zn, 1)
                    for a in range(NT + 1):
                        if a < NT:
                            if a >= 2:
                                pe.wait_ge(s_ze, a - 1)
                                pe.wait_ge(s_ae, a - 1)
                            for h in range(4):
                                b = (a % 2) * 512 + h * P
                                nc.tensor.transpose(PS[:, b:b + P],
                                                    a4[:, a, h // 2, (h % 2) * D:(h % 2) * D + D], ident[:]
                                                    ).then_inc(s_zt, 1)
                            b = 1024 + (a % 2) * 512
                            nc.tensor.transpose(PS[0:4, b:b + P], ra[:, 4 * a:4 * a + 4], ident[:]).then_inc(s_at, 1)
                        if a > 0:
                            c = a - 1
                            b = 2048 + (c % 2) * 512
                            pe.wait_ge(s_ze, c + 1)
                            pe.wait_ge(s_ae, c + 1)
                            if c >= 2:
                                pe.wait_ge(s_oe, c - 1)
                            for h in range(4):
                                nc.tensor.matmul(PS[:, b:b + D], zt[c % 2][:, h * P:(h + 1) * P],
                                                 wv[:, h * D:(h + 1) * D], start=(h == 0), stop=False)
                            nc.tensor.matmul(PS[:, b:b + D], aT[c % 2], bv, start=False, stop=True).then_inc(s_o, 1)
                    pe.wait_ge(s_oe, NT)
                    project_tiles(pe, HT, wsk, s_sk)
                    pe.wait_ge(s_ske, 1)
                    bn_tensor(pe, OUT, T1, bn)

                @block.scalar
                def _(act):
                    for a in range(NT):
                        act.wait_ge(s_zt, 4 * a + 4)
                        if a >= 2:
                            act.wait_ge(s_o, a - 1)
                        nc.scalar.copy(zt[a % 2], PS[:, (a % 2) * 512:(a % 2) * 512 + 512]).then_inc(s_ze, 1)
                    act.wait_ge(s_gate, 1)
                    nc.scalar.activation(sg, gt, ACT.Sigmoid).then_inc(s_sig, 1)
                    bn_scalar(act, var, std, bn)
                    act.wait_ge(s_gin, 1)
                    nc.scalar.activation(T1, OUT, ACT.Gelu).then_inc(s_gelu, 1)

                @block.vector
                def _(dve):
                    ch = Chain("t_c", dve)
                    ch(dve.memset(mean, 0.0))
                    den = a4[:, :, :, 256:258]
                    ch(dve.tensor_scalar(r4, den, 1e-16, None, ALU.add))
                    ch(dve.reciprocal(rd, rd))
                    ch(dve.tensor_scalar(rd, rd, 0.25, None, ALU.mult))
                    dve.tensor_tensor(ra.rearrange("p (t c h) -> p t c h", c=2, h=2), den, r4, ALU.mult)
                    for c in range(2):
                        z = a4[:, :, c, 0:256].rearrange("p t (h f) -> p t h f", h=2)
                        ins = dve.tensor_tensor(z, z, bc_in(r4[:, :, c, :], D), ALU.mult)
                    ins.then_inc(s_zn, 1)
                    for a in range(NT):
                        dve.wait_ge(s_at, a + 1)
                        if a >= 2:
                            dve.wait_ge(s_o, a - 1)
                        dve.tensor_copy(aT[a % 2], PS[0:4, 1024 + (a % 2) * 512:1024 + (a % 2) * 512 + P]
                                        ).then_inc(s_ae, 1)
                        if a >= 1:
                            c = a - 1
                            dve.wait_ge(s_o, c + 1)
                            b = 2048 + (c % 2) * 512
                            dve.tensor_copy(OUT[:, c * D:(c + 1) * D], PS[:, b:b + D]).then_inc(s_oe, 1)
                    c = NT - 1
                    dve.wait_ge(s_o, NT)
                    b = 2048 + (c % 2) * 512
                    dve.tensor_copy(OUT[:, c * D:(c + 1) * D], PS[:, b:b + D]).then_inc(s_oe, 1)
                    dve.wait_ge(s_oe, NT)
                    dve.wait_ge(s_sk, 7)
                    ch(dve.tensor_tensor(v3(SK), v3(PS[:, 0:NW]), bc_mid(bsk, NT), ALU.add))
                    ch(dve.tensor_tensor(v3(T1), v3(OUT), bc_mid(wb1, NT), ALU.mult))
                    ch(dve.tensor_tensor(v3(T2), v3(SK), bc_mid(wb2, NT), ALU.mult))
                    ch(dve.tensor_tensor(T1, T1, T2, ALU.add))
                    ch(dve.tensor_tensor(T2, OUT, SK, ALU.subtract))
                    ch(dve.tensor_tensor(v3(T2), v3(T2), bc_mid(wb3, NT), ALU.mult))
                    ch(dve.tensor_tensor(T1, T1, T2, ALU.add))
                    dve.tensor_reduce(gt, v3(T1), AX_X, ALU.add).then_inc(s_gate, 1)
                    ch(dve.tensor_tensor(SK, SK, OUT, ALU.subtract))
                    dve.wait_ge(s_sig, 1)
                    ch(dve.tensor_tensor(v3(SK), v3(SK), bc_in(sg, D), ALU.mult))
                    ch(dve.tensor_tensor(OUT, OUT, SK, ALU.add))
                    dve.sem_inc(s_ske, 1)
                    bn_vector(dve, ch, "t", OUT, T1, gw, gb, (mean, var, std, bn), mean_scale=gm)
                    dve.sem_inc(s_gin, 1)
                    dve.wait_ge(s_gelu, 1)
                    ch(dve.tensor_tensor(T1, T1, H[:], ALU.add))
                    ch(dve.tensor_tensor(X[:], X[:], T1, ALU.add))

        EP, EQ = 125, E // 125

        class WeightsAside:

            def __init__(self, base):
                (self.s_ld, self.s_m, self.s_cen, self.s_gm, self.s_g, self.s_r, self.s_rc, self.s_t, self.s_tw, self.s_v,
                 self.s_var, self.s_std, self.s_mr, self.s_row, self.s_row2, self.s_wl, self.s_wr, self.s_ws) = (
                    sem("e_" + x) for x in ("ld", "m", "cen", "gm", "g", "r", "rc", "t", "tw", "v", "var", "std", "mr",
                                            "row", "row2", "wl", "wr", "ws"))
                self.at = A[0:EP, base:base + EQ * 16]
                o = base + EQ * 16
                self.w1 = A[0:16, o:o + D]
                self.g1, self.bb1, self.b1 = (A[0:17, o + (2 + i) * D:o + (3 + i) * D] for i in range(3))
                self.mean = A[:, o + 640:o + 656]
                self.mcol = A[0:16, o + 656:o + 657]
                self.var, self.std = A[0:16, o + 768:o + 896], A[0:16, o + 896:o + 1024]
                self.row = A[0:1, o + 1024:o + 1152]
                self.gm, self.bm, self.selm = A[:, o + 1152:o + 1280], A[:, o + 1280:o + 1408], A[:, o + 1408:o + 1424]
                self.cov, self.tw = A[0:16, o + 1424:o + 1440], A[0:16, o + 1536:o + 1664]
                self.dm = A[0:16, o + 1664:o + 1680]
                self.ri, self.pi, self.fi = (A[:, o + 1792 + 128 * i:o + 1920 + 128 * i].bitcast(I32) for i in range(3))
                self.rf, self.pf, self.qf = (A[:, o + 2176 + 128 * i:o + 2304 + 128 * i] for i in range(3))
                o += 2560
                self.v = [A[:, o + 2112 * i:o + 2112 * i + 1024] for i in range(2)]
                self.wr = [A[:, o + 2112 * i + 1024:o + 2112 * i + 2048] for i in range(2)]
                self.cb = [A[:, o + 2112 * i + 2048:o + 2112 * i + 2112] for i in range(2)]
                assert o + 4224 <= ARENA

            def loads(self, sp):
                sp.dma_start(self.at, t["attr"].rearrange("(p q) f -> p (q f)", p=EP)).then_inc(self.s_ld, 16)
                sp.dma_start(self.w1, t["L3_gnn_ee_w1"]).then_inc(self.s_ld, 16)
                for d, n in ((self.g1, "g1"), (self.bb1, "bb1"), (self.b1, "b1")):
                    sp.dma_start(d, t["L3_gnn_ee_" + n].partition_broadcast(17)).then_inc(self.s_ld, 16)
                for i in range(2):
                    sp.dma_start(self.v[i].rearrange("i (b o) -> i b o", b=R_REL),
                                 t[f"L1_gnn_V{i + 1}"].rearrange("b i o -> i b o")).then_inc(self.s_wl, 16)
                    bcast_load(sp, self.cb[i], t[f"L1_gnn_comp{i + 1}"].rearrange("r b -> (r b)")).then_inc(self.s_wl, 16)

            def stores(self, sp):
                sp.wait_ge(self.s_row, 1)
                sp.dma_start(small[16:17, 0:D], self.row).then_inc(self.s_row2, 16)
                for i in range(2):
                    sp.wait_ge(self.s_wr, i + 1)
                    sp.dma_start(rel_w[i], self.wr[i]).then_inc(self.s_ws, 16)
                sp.wait_ge(self.s_row2, 16)
                sp.wait_ge(self.s_ws, 32)

            def scalar(self, act):
                act.wait_ge(self.s_var, 1)
                nc.scalar.activation(self.std, self.var, ACT.Sqrt).then_inc(self.s_std, 1)

            def tensor(self, pe):
                def column_sums():
                    pe.wait_ge(self.s_ld, 80)
                    for c in range(25):
                        ins = nc.tensor.matmul(PS[:, 1024:1536], ones[0:EP, :], self.at[:, c * 512:(c + 1) * 512],
                                               start=(c == 0), stop=(c == 24))
                    ins.then_inc(self.s_m, 1)

                def gram():
                    pe.wait_ge(self.s_cen, 1)
                    for c in range(100):
                        a = self.at[:, c * P:(c + 1) * P]
                        ins = nc.tensor.matmul(PS[:, 1536:1536 + P], a, a, start=(c == 0), stop=(c == 99))
                    ins.then_inc(self.s_g, 1)

                def variances():
                    pe.wait_ge(self.s_gm, 1)
                    nc.tensor.matmul(PS[0:16, 2048:2048 + P], self.selm, self.gm, start=True, stop=True
                                     ).then_inc(self.s_r, 1)
                    pe.wait_ge(self.s_rc, 1)
                    nc.tensor.matmul(PS[0:16, 2560:2560 + D], self.cov, self.w1, start=True, stop=True
                                     ).then_inc(self.s_t, 1)
                    pe.wait_ge(self.s_tw, 1)
                    nc.tensor.matmul(PS[0:16, 3072:3072 + D], ones[0:16, 0:16], self.tw, start=True, stop=True
                                     ).then_inc(self.s_v, 1)
                    nc.tensor.matmul(PS[0:1, 3584:3584 + D], self.mcol, self.w1, start=True, stop=True
                                     ).then_inc(self.s_mr, 1)

                return column_sums, lambda: None, gram, lambda: None, variances

            def vector(self, dve):
                ch = Chain("e_c", dve)
                mean, std, row, cov = self.mean, self.std, self.row, self.cov

                def masks():
                    ch(dve.tensor_copy(self.ri, iota_row[:]))
                    ch(dve.tensor_copy(self.pi, pidx[:, 0:1].to_broadcast([P, P])))
                    ch(dve.tensor_scalar(self.fi, self.pi, 15, None, ALU.bitwise_and))
                    dve.tensor_copy(self.qf, self.fi)
                    ch(dve.tensor_copy(self.rf, self.ri))
                    ch(dve.tensor_tensor(self.selm, self.qf[:, 0:16], self.rf[:, 0:16], ALU.is_equal))
                    ch(dve.tensor_scalar(self.ri, self.ri, 4, None, ALU.arith_shift_right))
                    ch(dve.tensor_scalar(self.pi, self.pi, 4, None, ALU.arith_shift_right))
                    dve.tensor_copy(self.pf, self.pi)
                    ch(dve.tensor_copy(self.rf, self.ri))
                    ch(dve.tensor_tensor(self.bm, self.pf, self.rf, ALU.is_equal))

                def centre():
                    dve.wait_ge(self.s_m, 1)
                    ch(dve.tensor_reduce(mean, PS[:, 1024:1536].rearrange("p (q f) -> p f q", f=16), AX_X, ALU.add))
                    ch(dve.tensor_scalar(mean, mean, 1.0 / E, None, ALU.mult))
                    ch(dve.tensor_tensor(self.dm, mean[0:16, :], ident[0:16, 0:16], ALU.mult))
                    ch(dve.tensor_reduce(self.mcol, self.dm, AX_X, ALU.add))
                    a3 = self.at.rearrange("p (q f) -> p q f", f=16)
                    dve.tensor_tensor(a3, a3, bc_mid(mean[0:EP, :], EQ), ALU.subtract).then_inc(self.s_cen, 1)

                def relation_weights(i, first, last):
                    dve.wait_ge(self.s_wl, 64)
                    for b in range(first, last):
                        for r in range(R_REL):
                            o, src = self.wr[i][:, r * D:(r + 1) * D], self.v[i][:, b * D:(b + 1) * D]
                            c = self.cb[i][:, r * R_REL + b:r * R_REL + b + 1]
                            if b == 0:
                                ins = dve.tensor_scalar(o, src, c, None, ALU.mult)
                            else:
                                ins = dve.scalar_tensor_tensor(o, src, c, o, ALU.mult, ALU.add)
                        if b < R_REL - 1:
                            ch(ins)
                    if last == R_REL:
                        ins.then_inc(self.s_wr, 1)

                def fold():
                    dve.wait_ge(self.s_g, 1)
                    dve.tensor_tensor(self.gm, PS[:, 1536:1536 + P], self.bm, ALU.mult).then_inc(self.s_gm, 1)
                    dve.wait_ge(self.s_r, 1)
                    ch(dve.tensor_reduce(cov, PS[0:16, 2048:2048 + P].rearrange("p (b f) -> p f b", f=16), AX_X,
                                         ALU.add))
                    dve.tensor_scalar(cov, cov, 1.0 / E, None, ALU.mult).then_inc(self.s_rc, 1)
                    dve.wait_ge(self.s_t, 1)
                    dve.tensor_tensor(self.tw, PS[0:16, 2560:2560 + D], self.w1, ALU.mult).then_inc(self.s_tw, 1)
                    dve.wait_ge(self.s_v, 1)
                    dve.tensor_scalar(self.var, PS[0:16, 3072:3072 + D], LN_EPS, None, ALU.add).then_inc(self.s_var, 1)
                    dve.wait_ge(self.s_std, 1)
                    ch(dve.reciprocal(std, std))
                    ch(dve.tensor_tensor(std, std, self.g1[0:16, :], ALU.mult))
                    dve.tensor_tensor(EW[0:16, :], self.w1, std, ALU.mult)
                    dve.wait_ge(self.s_mr, 1)
                    ch(dve.tensor_tensor(row, PS[0:1, 3584:3584 + D], self.b1[0:1, :], ALU.add))
                    ch(dve.tensor_tensor(row, self.b1[0:1, :], row, ALU.subtract))
                    ch(dve.tensor_tensor(row, row, std[0:1, :], ALU.mult))
                    dve.tensor_tensor(row, row, self.bb1[0:1, :], ALU.add).then_inc(self.s_row, 1)

                return (masks, centre, lambda: relation_weights(0, 0, 4), lambda: relation_weights(0, 4, 8), fold,
                        lambda: relation_weights(1, 0, 4), lambda: relation_weights(1, 4, 8))

        class EdgeSumAside:

            def __init__(self, ACC, base):
                self.s_w, self.s_h, self.s_t, self.s_te, self.s_mm, self.s_me, self.s_o = (
                    sem("f_" + x) for x in ("w", "h", "t", "te", "mm", "me", "o"))
                self.a3 = ACC.rearrange("p (t f) -> p t f", f=257)[:, :, D:257]
                self.F, self.FT, self.S = (A[:, base + NW * i:base + NW * (i + 1)] for i in range(3))
                o = base + 3 * NW
                self.w2, self.b2 = A[:, o:o + D], A[:, o + D:o + 2 * D]
                assert o + 2 * D <= ARENA

            def loads(self, sp):
                sp.dma_start(self.w2, t["L3_gnn_ee_w2"]).then_inc(self.s_w, 16)
                bcast_load(sp, self.b2, t["L3_gnn_ee_b2"]).then_inc(self.s_w, 16)

            def stores(self, sp):
                sp.wait_ge(self.s_me, 7)
                sp.dma_start(edge_sum, self.S).then_inc(self.s_o, 16)
                sp.wait_ge(self.s_o, 16)

            def tensor(self, pe):
                def products():
                    pe.wait_ge(self.s_w, 32)
                    pe.wait_ge(self.s_h, 1)
                    for g in range(8):
                        if g < 7:
                            if g >= 2:
                                pe.wait_ge(self.s_te, g - 1)
                            for a in range(4 * g, min(4 * g + 4, NT)):
                                b = 2048 + (g % 2) * 512 + (a % 4) * P
                                ins = nc.tensor.transpose(PS[:, b:b + P], self.F[:, a * D:(a + 1) * D], ident[:])
                            ins.then_inc(self.s_t, 1)
                        if g > 0:
                            c = g - 1
                            pe.wait_ge(self.s_te, c + 1)
                            if c >= 2:
                                pe.wait_ge(self.s_me, c - 1)
                            for a in range(4 * c, min(4 * c + 4, NT)):
                                b = 3072 + (c % 2) * 512 + (a % 4) * P
                                ins = nc.tensor.matmul(PS[:, b:b + P], self.FT[:, a * P:(a + 1) * P], self.w2,
                                                       start=True, stop=True)
                            ins.then_inc(self.s_mm, 1)

                return (products,)

            def scalar(self, act):
                for g in range(7):
                    lo, hi = 512 * g, min(512 * g + 512, NP)
                    act.wait_ge(self.s_t, g + 1)
                    b = 2048 + (g % 2) * 512
                    nc.scalar.copy(self.FT[:, lo:hi], PS[:, b:b + hi - lo]).then_inc(self.s_te, 1)

            def vector(self, dve):
                def add_up():
                    ch = Chain("f_c", dve)
                    dve.wait_ge(self.s_w, 32)
                    dve.tensor_copy(v3(self.F), self.a3[:, :, 0:D]).then_inc(self.s_h, 1)
                    ch(dve.tensor_tensor(v3(self.S), bc_in(self.a3[:, :, D], D), bc_mid(self.b2, NT), ALU.mult))
                    for g in range(7):
                        lo, hi = 512 * g, min(512 * g + 512, NP)
                        b = 3072 + (g % 2) * 512
                        dve.wait_ge(self.s_mm, g + 1)
                        dve.tensor_tensor(self.S[:, lo:hi], self.S[:, lo:hi], PS[:, b:b + hi - lo], ALU.add
                                          ).then_inc(self.s_me, 1)

                return (add_up,)

        def stage_gin_begin():
            s_ld, s_h, s_o = sem("i_ld"), sem("i_h"), sem("i_o")
            with nc.Block() as block:
                @block.sync
                def _(sp):
                    sp.dma_start(A[:, 0:NW], edge_sum).then_inc(s_ld, 16)
                    sp.wait_ge(s_h, 1)
                    sp.dma_start(tab_h.rearrange("(t p) f -> p t f", p=P), v3(H[:])).then_inc(s_o, 16)
                    sp.wait_ge(s_o, 16)

                @block.vector
                def _(dve):
                    dve.wait_ge(s_ld, 16)
                    dve.tensor_tensor(H[:], H[:], A[:, 0:NW], ALU.add).then_inc(s_h, 1)

        def stage_gin_layer(name, Z, w_ap, vecs, last):
            s_w, s_h, s_t, s_te, s_mm, s_out, s_st = (sem(name + x) for x in ("_w", "_h", "_t", "_te", "_mm", "_out", "_st"))
            bn = bn_sems(name)
            o = NW
            SQ = A[:, o:o + NW]
            o += NW
            w, b, gam, bet, mean, var, std = (A[:, o + D * i:o + D * (i + 1)] for i in range(7))
            with nc.Block() as block:
                @block.sync
                def _(sp):
                    sp.dma_start(w, w_ap).then_inc(s_w, 16)
                    for d, v in zip((b, gam, bet), vecs):
                        bcast_load(sp, d, v).then_inc(s_w, 16)
                    if last:
                        sp.wait_ge(s_out, 1)
                        sp.dma_start(node_view(out, True), v3(Z[:, 0:(NT - 1) * D])).then_inc(s_st, 16)
                        sp.dma_start(node_view(out, False), Z[0:NLAST, (NT - 1) * D:NW]).then_inc(s_st, 16)
                        sp.wait_ge(s_st, 32)

                @block.tensor
                def _(pe):
                    pe.wait_ge(s_w, 64)
                    transpose_tiles(pe, Z, s_h, s_t)
                    pe.wait_ge(s_te, 7)
                    project_tiles(pe, HT, w, s_mm)
                    bn_tensor(pe, Z, SQ, bn)

                @block.scalar
                def _(act):
                    for g in range(7):
                        lo, hi = 512 * g, min(512 * g + 512, NP)
                        act.wait_ge(s_t, g + 1)
                        nc.scalar.copy(HT[:, lo:hi], PS[:, lo:hi]).then_inc(s_te, 1)
                    bn_scalar(act, var, std, bn)

                @block.vector
                def _(dve):
                    ch = Chain(name + "_c", dve)
                    ch(dve.memset(mean, 0.0))
                    if not last:
                        ch(dve.tensor_tensor(Z, Z, H[:], ALU.add))
                    dve.sem_inc(s_h, 7)
                    dve.wait_ge(s_w, 64)
                    dve.wait_ge(s_mm, 7)
                    ch(dve.tensor_tensor(v3(Z), v3(PS[:, 0:NW]), bc_mid(b, NT), ALU.add))
                    bn_vector(dve, ch, name, Z, SQ, gam, bet, (mean, var, std, bn))
                    ch(dve.tensor_scalar(Z, Z, 0.0, None, ALU.max))
                    if last:
                        dve.tensor_tensor(Z, Z, X[:], ALU.add).then_inc(s_out, 1)

        stage_setup()
        end_stage()
        stage_norm("n0")
        end_stage()
        ad = stage_gat_table()
        end_stage()
        stage_scores("a0", 8, tab0, 136, ad, 8, spill0, aside=WeightsAside(8896))
        end_stage()
        stage_softmax("x0", 8)
        end_stage()
        ACC = stage_aggregate("s0", (0, NT * 136), [136], heads=8, spill=spill0, width=136)
        end_stage()
        stage_gat_end(ACC)
        end_stage()
        stage_norm("n1")
        end_stage()
        stage_rel_table("r1", 0, 16384)
        end_stage()
        ACC = stage_aggregate("s1", (0, NT * 257), [257], table=tab_rel, idx=idx_rel, edge_w=EW)
        end_stage()
        stage_rel_end("b1", ACC, t["L1_gnn_bias1"], True)
        end_stage()
        stage_rel_table("r2", 1, 16384)
        end_stage()
        NS = 257 * NT
        ACC = stage_aggregate("s2", (NS, NS + NW), [D], table=tab_rel, idx=idx_rel, weighted=True,
                              aside=EdgeSumAside(ACC, 16384))
        end_stage()
        stage_rel_end("b2", ACC, t["L1_gnn_bias2"], False)
        end_stage()
        stage_norm("n2")
        end_stage()
        U = stage_queries()
        end_stage()
        stage_scores("a2", 4, tab_x, 129, U, 516, spill2)
        end_stage()
        stage_softmax("x2", 4)
        end_stage()
        ACC = stage_aggregate("s3", (0, NT * 516), [258, 258], heads=4, spill=spill2, width=129)
        end_stage()
        stage_transformer_end(ACC)
        end_stage()
        stage_norm("n3")
        end_stage()
        stage_gin_begin()
        end_stage()
        ACC = stage_aggregate("s5", (0, NW), [D], table=tab_h, idx=idx_src)
        end_stage()
        stage_gin_layer("m1", ACC, t["L3_gnn_mlp_w1"], [t["L3_gnn_mlp_" + v] for v in ("b1", "g1", "bb1")], False)
        end_stage()
        stage_gin_layer("m2", ACC, t["L3_gnn_mlp_w2"], [t["L3_gnn_mlp_" + v] for v in ("b2", "g2", "bb2")], True)
        end_stage()


def kernel(x, src, dst, edge_attr_16, edge_type_8, edge_weight, **weights):
    import numpy as np
    import concourse.bacc as bacc
    from concourse.bass_utils import run_bass_kernel_spmd

    arrays = {k: np.ascontiguousarray(v) for k, v in weights.items() if k not in (
        "L2_gnn_Wk", "L2_gnn_bq", "L2_gnn_bk")}
    pad = ST * SUPER - E

    def rows(a, fill):
        a = np.asarray(a)
        return np.concatenate([a, np.full((pad,) + a.shape[1:], fill, a.dtype)]).reshape((ST, SUPER) + a.shape[1:])

    arrays["x"] = np.ascontiguousarray(x)
    arrays["dst"] = rows(dst, NP)
    arrays["src"] = rows(src, 0)
    arrays["etype"] = rows(edge_type_8, 0)
    arrays["weight"] = rows(edge_weight, 0)
    arrays["attr"] = np.ascontiguousarray(edge_attr_16)
    arrays["attr_t"] = np.ascontiguousarray(rows(edge_attr_16, 0).reshape(2 * ST, P, 16).transpose(0, 2, 1))
    arrays["wk_t"] = np.ascontiguousarray(np.asarray(weights["L2_gnn_Wk"]).T)
    arrays["bq_t"] = np.ascontiguousarray(np.asarray(weights["L2_gnn_bq"]).reshape(4, D).T)
    arrays["bk_t"] = np.ascontiguousarray(np.asarray(weights["L2_gnn_bk"]).reshape(4, D).T)
    nc = bacc.Bacc("TRN2", target_bir_lowering=False, num_devices=1)
    t, feed = {}, {}
    for name, a in arrays.items():
        feed["in_" + name] = a
        t[name] = nc.dram_tensor("in_" + name, a.shape, mybir.dt.from_np(a.dtype), kind="ExternalInput").ap()
    out = nc.dram_tensor("out", [N, D], F32, kind="ExternalOutput").ap()
    build(nc, t, out)
    r = run_bass_kernel_spmd(nc, [feed], core_ids=[0])
    return r.results[0]["out"]
```

```python
from contextlib import ExitStack

import concourse.bass as bass
from concourse import mybir

F32 = mybir.dt.float32
I32 = mybir.dt.int32
ALU = mybir.AluOpType
ACT = mybir.ActivationFunctionType
AX_X = mybir.AxisListType.X

P = 128
N = 3125
E = 100000
D = 128
NT = -(-N // P)
NLAST = N - (NT - 1) * P
NP = NT * P
SUPER = 2 * P
ST = -(-E // SUPER)
SS = 416
K = 2 * SS
SETS = K // 8
NQ = 4
JB = 104
assert ST + NT - 1 <= SS and SS == 4 * JB and SETS % NQ == 0
BIG = 1.0e30
LN_EPS = 1e-5
CR = 16
R_REL = 8
NW = NT * D
ARENA = 30720


def build(nc, t, out):
    ctx = ExitStack()
    with ctx:
        def sb(name, shape, dt=F32):
            return ctx.enter_context(nc.sbuf_tensor(name, shape, dt))

        stage_sems = []

        def sem(name):
            stage_sems.append(nc.alloc_semaphore(name=name))
            return stage_sems[-1]

        def end_stage():
            nc.clear_and_free_semaphores(stage_sems)
            stage_sems.clear()
            nc.all_engine_barrier()

        def dram(name, shape, dt=F32):
            return nc.dram_tensor(name, shape, dt, kind="Internal").ap()

        X = sb("X", [P, NW])
        H = sb("H", [P, NW])
        HT = sb("HT", [P, NP])
        idx_src = sb("idx_src", [P, K], I32)
        idx_rel = sb("idx_rel", [P, K], I32)
        drel = sb("drel", [P, K])
        wgt = sb("wgt", [P, K])
        pen = sb("pen", [P, K])
        ntile = sb("ntile", [1, SS], I32)
        estep = sb("estep", [1, SS], I32)
        att = sb("att", [P, K * 8])
        ident = sb("ident", [P, P])
        ones = sb("ones", [P, P])
        lastmask = sb("lastmask", [P, P])
        iota_row = sb("iota_row", [P, P])
        pidx = sb("pidx", [P, 1])
        small = sb("small", [P, 192])
        A = sb("arena", [P, ARENA])
        PS = ctx.enter_context(nc.psum_tensor("PS", [P, 4096], F32))

        drel_rows = dram("drel_rows", [SS, SUPER])
        key_rows = dram("key_rows", [SS, SUPER])
        n_rows = dram("n_rows", [4, JB], I32)
        e_rows = dram("e_rows", [4, JB], I32)
        tab0 = dram("tab0", [NP, 136])
        tab_rel = dram("tab_rel", [NP * R_REL, D])
        tab_x = dram("tab_x", [NP, D])
        tab_h = dram("tab_h", [NP, D])
        spill0 = dram("spill0", [SETS, P, 8 * 136])
        spill2 = dram("spill2", [SETS, P, 8 * 129])
        score_rows = dram("score_rows", [8, K, P])
        prob_rows = dram("prob_rows", [8, K, P])
        carry_a = dram("carry_a", [P, 4])
        edge_sum = dram("edge_sum", [P, NW])
        carry_b = dram("carry_b", [P, 2])
        rel_w = dram("rel_w", [2, P, R_REL * D])
        EW = small[0:17, 0:D]

        def v3(ap, n=D):
            return ap.rearrange("p (t f) -> p t f", f=n)

        def bc_in(ap, n):
            return ap.unsqueeze(len(ap.shape)).to_broadcast(list(ap.shape) + [n])

        def bc_mid(ap, n):
            return ap.unsqueeze(1).to_broadcast([ap.shape[0], n, ap.shape[1]])

        def bcast_load(eng, dst, src):
            return eng.dma_start(dst, src.partition_broadcast(P))

        def load_tiles(eng, row, at, top):
            _, values = nc.values_load_multi_w_load_instructions(row[0:1, bass.ds(at, 4)], engines=[eng], min_val=0,
                                                                 max_val=top)
            return values

        class Chain:

            def __init__(self, name, eng):
                self.sem, self.n, self.eng = sem(name), 0, eng

            def __call__(self, ins):
                self.n += 1
                ins.then_inc(self.sem, 1)
                self.eng.wait_ge(self.sem, self.n)

        def node_view(dram_ap, full):
            if full:
                return dram_ap[0:(NT - 1) * P, :].rearrange("(t p) f -> p t f", p=P)
            return dram_ap[(NT - 1) * P:N, :]

        def stage_setup():
            s_x, s_row, s_zero = sem("s_x"), sem("s_row"), sem("s_zero")
            s_iota, s_const, s_key, s_keyb = sem("s_iota"), sem("s_const"), sem("s_key"), sem("s_keyb")
            s_step, s_gath, s_slot, s_tp, s_nw, s_rows, s_nt = (
                sem(x) for x in ("s_step", "s_gath", "s_slot", "s_tp", "s_nw", "s_rows", "s_nt"))
            iota_i = A[:, 0:P].bitcast(I32)
            pidx_i = A[:, P:P + 1].bitcast(I32)
            j_i = A[:, 132:136].bitcast(I32)
            s_i = A[0:1, 144:144 + ST].bitcast(I32)
            last_i = A[0:1, 544:544 + ST].bitcast(I32)
            key = A[0:1, 944:944 + ST]
            keyb = A[:, 1344:1344 + ST]
            junk = A[:, 1744:1744 + ST]
            jf, ej, nf, base, oob = (A[:, 2144 + 4 * i:2148 + 4 * i] for i in range(5))
            e_i, n_i = A[:, 2176:2180].bitcast(I32), A[:, 2180:2184].bitcast(I32)
            tile_i, sidx_f = A[0:1, 2200:2200 + ST].bitcast(I32), A[0:1, 2600:2600 + ST]
            tmp = A[:, 3072:3072 + K]
            raw = [A[:, 4096 + 1024 * i:4096 + 1024 * (i + 1)] for i in range(4)]
            sl = [A[:, 8192 + 1024 * i:8192 + 1024 * (i + 1)] for i in range(4)]
            with nc.Block() as block:
                @block.sync
                def _(sp):
                    sp.dma_start(last_i, t["dst"][:, SUPER - 1:SUPER].rearrange("s o -> o s"),
                                 allow_slow_non_contiguous=True).then_inc(s_row, 16)
                    sp.wait_ge(s_zero, 1)
                    sp.dma_start(v3(X[:, 0:(NT - 1) * D]), node_view(t["x"], True)).then_inc(s_x, 16)
                    sp.dma_start(X[0:NLAST, (NT - 1) * D:NW], node_view(t["x"], False)).then_inc(s_x, 16)
                    sp.wait_ge(s_step, 1)
                    sp.dma_start(n_rows.rearrange("b p -> p b"), n_i[0:JB, :],
                                 allow_slow_non_contiguous=True).then_inc(s_nw, 16)
                    sp.dma_start(e_rows.rearrange("b p -> p b"), e_i[0:JB, :],
                                 allow_slow_non_contiguous=True).then_inc(s_nw, 16)
                    sp.wait_ge(s_nw, 32)
                    sp.dma_start(estep[:], e_rows.rearrange("b p -> (b p)").unsqueeze(0)).then_inc(s_nt, 16)
                    sp.dma_start(ntile[:], n_rows.rearrange("b p -> (b p)").unsqueeze(0)).then_inc(s_nt, 16)
                    sp.wait_ge(s_slot, 1)
                    sp.dma_start(drel_rows.rearrange("(b p) e -> p b e", p=JB),
                                 sl[0][0:JB, :].rearrange("p (b e) -> p b e", b=4)).then_inc(s_rows, 16)
                    sp.dma_start(key_rows.rearrange("(b p) e -> p b e", p=JB),
                                 sl[3][0:JB, :].rearrange("p (b e) -> p b e", b=4)).then_inc(s_rows, 16)
                    sp.wait_ge(s_rows, 32)
                    sp.wait_ge(s_nt, 32)
                    sp.wait_ge(s_x, 32)

                @block.gpsimd
                def _(pool):
                    nc.gpsimd.iota(iota_i, [[1, P]], base=0, channel_multiplier=0)
                    nc.gpsimd.iota(pidx_i, [[1, 1]], base=0, channel_multiplier=1)
                    nc.gpsimd.iota(s_i, [[1, ST]], base=0, channel_multiplier=0)
                    nc.gpsimd.iota(j_i, [[JB, 4]], base=0, channel_multiplier=1).then_inc(s_iota, 1)
                    pool.wait_ge(s_const, 1)
                    nc.gpsimd.affine_select(out=ident[:], in_=ones[:], compare_op=ALU.is_equal, fill=0.0, base=0,
                                            pattern=[[-1, P]], channel_multiplier=1)
                    nc.gpsimd.affine_select(out=lastmask[:], in_=ones[:], compare_op=ALU.is_ge, fill=0.0,
                                            base=NLAST - 1, pattern=[[0, P]], channel_multiplier=-1).then_inc(s_const, 1)
                    pool.wait_ge(s_step, 1)
                    for n, name in enumerate(("dst", "src", "etype", "weight")):
                        for b in range(4):
                            o = raw[n][0:JB, b * SUPER:(b + 1) * SUPER]
                            pool.indirect_dma_start(
                                out=o if name == "weight" else o.bitcast(I32), out_offset=None, in_=t[name],
                                in_offset=bass.IndirectOffsetOnAxis(ap=e_i[0:JB, b:b + 1], axis=0)).then_inc(s_gath, 16)

                @block.vector
                def _(dve):
                    ch = Chain("c_setup", dve)
                    dve.memset(X[:, (NT - 1) * D:NW], 0.0).then_inc(s_zero, 1)
                    dve.memset(ones[:], 1.0).then_inc(s_const, 1)
                    dve.wait_ge(s_iota, 1)
                    dve.tensor_copy(iota_row[:], iota_i)
                    dve.tensor_copy(jf, j_i)
                    dve.tensor_copy(sidx_f, s_i)
                    ch(dve.tensor_copy(pidx[:], pidx_i))
                    dve.wait_ge(s_row, 16)
                    ch(dve.tensor_scalar(tile_i, last_i, 7, None, ALU.arith_shift_right))
                    ch(dve.tensor_copy(key, tile_i))
                    ch(dve.tensor_scalar(key, key, float(NT - 1), None, ALU.min))
                    dve.tensor_tensor(key, key, sidx_f, ALU.add).then_inc(s_key, 1)
                    dve.wait_ge(s_keyb, 1)
                    ch(dve.tensor_copy(keyb, PS[:, 0:ST]))
                    for b in range(4):
                        ch(dve.tensor_scalar(junk, keyb, jf[:, b:b + 1], None, ALU.is_lt, ALU.add,
                                             accum_out=ej[:, b:b + 1]))
                    ch(dve.tensor_tensor(nf, jf, ej, ALU.subtract))
                    ch(dve.tensor_scalar(nf, nf, float(NT - 1), None, ALU.min))
                    ch(dve.tensor_scalar(oob, ej, float(ST), 1.0e6, ALU.is_ge, ALU.mult))
                    ch(dve.tensor_scalar(ej, ej, float(ST - 1), None, ALU.min))
                    dve.tensor_copy(e_i, ej)
                    ch(dve.scalar_tensor_tensor(base, nf, float(P), oob, ALU.mult, ALU.add))
                    dve.tensor_copy(n_i, nf).then_inc(s_step, 1)
                    dve.wait_ge(s_gath, 256)
                    dve.tensor_copy(sl[3][0:JB, :], raw[0][0:JB, :].bitcast(I32))
                    dve.tensor_copy(sl[1][0:JB, :], raw[1][0:JB, :].bitcast(I32))
                    ch(dve.scalar_tensor_tensor(sl[2][0:JB, :], raw[1][0:JB, :].bitcast(I32), float(R_REL),
                                                raw[2][0:JB, :].bitcast(I32), ALU.mult, ALU.add))
                    for b in range(4):
                        c = slice(b * SUPER, (b + 1) * SUPER)
                        ins = dve.tensor_scalar(sl[0][0:JB, c], sl[3][0:JB, c], base[0:JB, b:b + 1], None,
                                                ALU.subtract)
                    ins.then_inc(s_slot, 1)
                    for i, dst in enumerate((drel, idx_src, idx_rel, wgt)):
                        for g in range(2):
                            dve.wait_ge(s_tp, 2 * i + g + 1)
                            bank = (2 * i + g) * 512
                            o = dst[:].rearrange("p (j g) -> p g j", g=2)[:, g, :]
                            ch(dve.tensor_copy(o, PS[:, bank:bank + SS]))
                    ch(dve.tensor_scalar(tmp, drel[:], 0.0, None, ALU.is_ge))
                    ch(dve.scalar_tensor_tensor(pen[:], drel[:], float(P), tmp, ALU.is_lt, ALU.mult))
                    ch(dve.tensor_scalar(pen[:], pen[:], -1.0, BIG, ALU.add, ALU.mult))

                @block.tensor
                def _(pe):
                    pe.wait_ge(s_key, 1)
                    pe.wait_ge(s_const, 2)
                    nc.tensor.matmul(PS[:, 0:ST], ones[0:1, :], key, start=True, stop=True).then_inc(s_keyb, 1)
                    pe.wait_ge(s_slot, 1)
                    for i, src in enumerate((sl[0], sl[1], sl[2], raw[3])):
                        for g in range(2):
                            for b in range(4):
                                o = (2 * i + g) * 512 + b * JB
                                ins = nc.tensor.transpose(PS[:, o:o + JB],
                                                          src[0:JB, b * SUPER + g * P:b * SUPER + (g + 1) * P],
                                                          ident[0:JB, 0:JB])
                            ins.then_inc(s_tp, 1)

        GROUPS = [(4 * g, min(4 * g + 4, NT)) for g in range(7)]

        def stage_norm(name, table=False):
            s_cen, s_sq, s_var, s_std, s_h, s_t = (sem(name + x) for x in ("_cen", "_sq", "_var", "_std", "_h", "_t"))
            s_e, s_o = sem(name + "_e"), sem(name + "_o")
            mu, var, std = A[:, 0:NT], A[:, 32:32 + NT], A[:, 64:64 + NT]
            sq, es = A[:, 128:128 + NW], A[:, 128 + NW:128 + 2 * NW]
            with nc.Block() as block:
                if table:
                    @block.sync
                    def _(sp):
                        sp.dma_start(es, edge_sum).then_inc(s_e, 16)
                        rows = tab_h.rearrange("(t p) f -> p t f", p=P)
                        for g, (a, b) in enumerate(GROUPS):
                            sp.wait_ge(s_h, g + 1)
                            sp.dma_start(rows[:, a:b, :], v3(H[:, a * D:b * D])).then_inc(s_o, 16)
                        sp.wait_ge(s_o, 112)

                @block.vector
                def _(dve):
                    ch = Chain(name + "_c", dve)
                    ch(dve.tensor_reduce(mu, v3(X[:]), AX_X, ALU.add))
                    ch(dve.tensor_scalar(mu, mu, 1.0 / D, None, ALU.mult))
                    for a, b in GROUPS:
                        dve.tensor_tensor(v3(H[:, a * D:b * D]), v3(X[:, a * D:b * D]), bc_in(mu[:, a:b], D),
                                          ALU.subtract).then_inc(s_cen, 1)
                    for g, (a, b) in enumerate(GROUPS):
                        dve.wait_ge(s_sq, g + 1)
                        ins = dve.tensor_reduce(var[:, a:b], v3(sq[:, a * D:b * D]), AX_X, ALU.add)
                    ch(ins)
                    dve.tensor_scalar(var, var, 1.0 / D, LN_EPS, ALU.mult, ALU.add).then_inc(s_var, 1)
                    dve.wait_ge(s_std, 1)
                    ch(dve.reciprocal(std, std))
                    if table:
                        dve.wait_ge(s_e, 16)
                    for a, b in GROUPS:
                        ins = dve.scalar_tensor_tensor(v3(H[:, a * D:b * D]), v3(H[:, a * D:b * D]), 0.0,
                                                       bc_in(std[:, a:b], D), ALU.max, ALU.mult)
                        if table:
                            ch(ins)
                            ins = dve.tensor_tensor(H[:, a * D:b * D], H[:, a * D:b * D], es[:, a * D:b * D], ALU.add)
                        ins.then_inc(s_h, 1)

                @block.scalar
                def _(act):
                    for g, (a, b) in enumerate(GROUPS):
                        act.wait_ge(s_cen, g + 1)
                        nc.scalar.activation(sq[:, a * D:b * D], H[:, a * D:b * D], ACT.Square).then_inc(s_sq, 1)
                    act.wait_ge(s_var, 1)
                    nc.scalar.activation(std, var, ACT.Sqrt).then_inc(s_std, 1)
                    if not table:
                        for g, (a, b) in enumerate(GROUPS):
                            act.wait_ge(s_t, g + 1)
                            nc.scalar.copy(HT[:, a * P:b * P], PS[:, a * P:b * P])

                if not table:
                    @block.tensor
                    def _(pe):
                        transpose_tiles(pe, H, s_h, s_t)

        def transpose_tiles(pe, src, s_in, s_out):
            for g in range(7):
                pe.wait_ge(s_in, g + 1)
                for a in range(4 * g, min(4 * g + 4, NT)):
                    ins = nc.tensor.transpose(PS[:, a * P:(a + 1) * P], src[:, a * D:(a + 1) * D], ident[:])
                ins.then_inc(s_out, 1)

        def project_tiles(pe, srcT, w, s_out, s_in=None):
            for g in range(7):
                if s_in is not None:
                    pe.wait_ge(s_in, g + 1)
                for a in range(4 * g, min(4 * g + 4, NT)):
                    ins = nc.tensor.matmul(PS[:, a * P:(a + 1) * P], srcT[:, a * P:(a + 1) * P], w,
                                           start=True, stop=True)
                ins.then_inc(s_out, 1)

        def node_sum(pe, src, dst, s_in, s_out):
            for g, (first, last) in enumerate(GROUPS):
                pe.wait_ge(s_in, g + 1)
                for a in range(first, last):
                    ins = nc.tensor.matmul(dst, (lastmask if a == NT - 1 else ones)[:], src[:, a * D:(a + 1) * D],
                                           start=(a == 0), stop=(a == NT - 1))
            ins.then_inc(s_out, 1)

        def gather_sets(pool, name, table, idx, G, width, idx_now, full, frees):
            row = table.shape[1]
            s_ix, s_dummy = sem(name + "_ix"), sem(name + "_pd")
            RW = 8 * NQ
            now = [idx_now[:, r * RW:(r + 1) * RW] for r in range(2)]

            def two_rounds(i, last):
                for r in range(2):
                    for q in range(NQ):
                        for f, per in frees:
                            pool.wait_ge(f, i * (2 * NQ * per) + ((r * NQ + q + 1 - NQ) * per + CR))
                            pool.sem_inc(s_dummy, 1)
                        if q == NQ - 1 and not (last and r == 1):
                            nc.gpsimd.tensor_copy(now[1 - r], idx[:, bass.ds(i * (2 * RW) + (r + 1) * RW, RW)]
                                                  ).then_inc(s_ix, 1)
                        if q == 0:
                            pool.wait_ge(s_ix, i * 2 + r + 1)
                            pool.sem_inc(s_dummy, 1)
                        for k in range(8 * q, 8 * q + 8):
                            pool.indirect_dma_start(
                                out=G[:, k * width:k * width + row], out_offset=None, in_=table,
                                in_offset=bass.IndirectOffsetOnAxis(ap=now[r][:, k:k + 1], axis=0)
                            ).then_inc(full[q], 16)

            nc.gpsimd.tensor_copy(now[0], idx[:, 0:RW]).then_inc(s_ix, 1)
            rounds = SETS // NQ
            assert rounds % 2 == 0
            with pool.Fori(0, rounds // 2 - 1) as i:
                two_rounds(i, False)
            two_rounds(rounds // 2 - 1, True)

        def each_set(eng, step, between=()):
            at = 0
            for part in tuple(between) + (None,):
                with eng.Fori(at, at + 2 if part else SETS // NQ - 1) as i:
                    for q in range(NQ):
                        step(i, q, i * NQ + q, NQ)
                if part:
                    part()
                    at += 2
            i = SETS // NQ - 1
            for q in range(NQ):
                step(i, q, i * NQ + q, NQ - 1 - q)

        def after(i, q, n=1):
            return i + (q + n) // NQ, (q + n) % NQ, i * NQ + (q + n)

        def stage_scores(name, heads, table, width, node_tab, node_w, spill, aside=None):
            o_g = NT * node_w if heads == 4 else 256
            o_db = o_g + NQ * 8 * width
            G = A[:, o_g:o_db]
            DB = [A[:, o_db + 1024 * i:o_db + 1024 * (i + 1)] for i in range(2)]
            MT = [A[:, o_db + 2048 + 1024 * i:o_db + 3072 + 1024 * i] for i in range(2)]
            o_t = o_db + 4096
            t1, t2 = A[:, o_t:o_t + 64], A[:, o_t + 64:o_t + 128]
            prod = [A[:, o_t + 128 + 516 * i:o_t + 644 + 516 * i] for i in range(4)]
            o_t += 2400 if heads == 4 else 128
            idx_now = A[:, o_t:o_t + 16 * NQ].bitcast(I32)
            assert o_t + 16 * NQ <= ARENA
            full = [sem(f"{name}_g{q}") for q in range(NQ)]
            db_full = [sem(f"{name}_db{q}") for q in range(2)]
            mt_done, mm_done, read_done, spilled, spill_free = (sem(name + x) for x in
                                                                ("_mt", "_mm", "_rd", "_sp", "_sf"))
            mul_done, act_red = sem(name + "_mul"), sem(name + "_ar")
            s_c, s_vd, s_pd = sem(name + "_c"), sem(name + "_vd"), sem(name + "_ed")
            rows = drel_rows.rearrange("j e -> (j e)").unsqueeze(0)
            with nc.Block() as block:
                @block.gpsimd
                def _(pool):
                    gather_sets(pool, name, table, idx_src, G, width, idx_now, full,
                                [(read_done, 1), (spill_free, 1)])

                if heads == 4:
                    @block.scalar
                    def _(act):
                        act.sem_inc(act_red, CR)
                        with act.Fori(0, SETS // NQ) as i:
                            for q in range(NQ):
                                act.wait_ge(read_done, i * NQ + (q + 1 - 2 + CR))
                                for k in range(8):
                                    act.wait_ge(mul_done, i * (8 * NQ) + (q * 8 + k + 1 + CR))
                                    for h in ((1, 2, 3) if k % 2 else (2, 3)):
                                        o = 32 * (q % 2) + 4 * k + h
                                        pr = prod[k % 4][:, h * width:(h + 1) * width]
                                        ins = nc.scalar.activation(pr, pr, ACT.Copy, accum_out=t1[:, o:o + 1])
                                    ins.then_inc(act_red, 1)

                @block.sync
                def _(sp):
                    sp.sem_inc(spill_free, CR)

                    def load_dst(i, q, s):
                        sp.dma_start(DB[q % 2], rows[0:1, bass.ds(s * 1024, 1024)].to_broadcast([P, 1024])
                                     ).then_inc(db_full[q % 2], 16)

                    def step(i, q, s, more):
                        sp.wait_ge(full[q], i * 128 + 128)
                        sp.dma_start(spill[bass.ds(s, 1), :, :].rearrange("o p f -> (o p) f"),
                                     G[:, q * 8 * width:(q + 1) * 8 * width]).then_inc(spilled, 16)
                        if more >= 2:
                            sp.wait_ge(mt_done, s + (1 + CR))
                            load_dst(*after(i, q, 2))
                        sp.wait_ge(spilled, s * 16 + 16)
                        sp.sem_inc(spill_free, 1)

                    load_dst(0, 0, 0)
                    load_dst(0, 1, 1)
                    if aside:
                        aside.loads(sp)
                    each_set(sp, step)
                    if aside:
                        aside.stores(sp)

                if aside:
                    @block.scalar
                    def _(act):
                        aside.scalar(act)

                @block.tensor
                def _(pe):
                    pe.sem_inc(mm_done, CR)

                    def step(i, q, s, more):
                        tiles = load_tiles(mybir.EngineType.PE, ntile, s * 4, NT - 1)
                        pe.wait_ge(mt_done, s + 1 + CR)
                        if heads == 8:
                            pe.wait_ge(read_done, s + (1 - 2 + CR))
                        for k in range(8):
                            n = tiles[k // 2]
                            lhsT = MT[q % 2][:, k * P:(k + 1) * P]
                            if heads == 8:
                                ins = nc.tensor.matmul(PS[:, (q % 2) * 512 + k * 8:(q % 2) * 512 + k * 8 + 8], lhsT,
                                                       node_tab[:, bass.ds(n * 8, 8)], start=True, stop=True)
                            else:
                                pe.wait_ge(mul_done, s * 8 + (k + 1 - 4 + CR))
                                for c in range(2):
                                    b = ((k % 4) * 2 + c) * 512
                                    ins = nc.tensor.matmul(PS[:, b:b + 258], lhsT,
                                                           node_tab[:, bass.ds(n * 516 + 258 * c, 258)],
                                                           start=True, stop=True)
                                ins.then_inc(s_pd, 1)
                        if heads == 8:
                            ins.then_inc(mm_done, 1)

                    each_set(pe, step, aside.tensor(pe) if aside else ())

                @block.vector
                def _(dve):
                    if heads == 4:
                        ch = Chain(name + "_c0", dve)
                        ch(dve.memset(G, 1.0))
                        dve.sem_inc(mul_done, CR)
                    dve.sem_inc(mt_done, CR)
                    dve.sem_inc(read_done, CR)

                    def onehots(i, q, s):
                        dve.wait_ge(db_full[q % 2], i * (8 * NQ) + (16 * (q // 2) + 16))
                        if heads == 8:
                            dve.wait_ge(mm_done, s + (1 - 2 + CR))
                        else:
                            dve.wait_ge(mul_done, s * 8 + (8 - 16 + CR))
                        nc.vector.tensor_scalar(MT[q % 2], DB[q % 2], pidx[:, 0:1], None,
                                                ALU.is_equal).then_inc(mt_done, 1)

                    def step(i, q, s, more):
                        if more:
                            onehots(*after(i, q))
                        g3 = G[:, q * 8 * width:(q + 1) * 8 * width].rearrange("p (k f) -> p k f", f=width)
                        dve.wait_ge(full[q], i * 128 + 128)
                        pen_b = bc_in(pen[:, bass.ds(s * 8, 8)], heads)
                        o = att[:, bass.ds(s * (8 * heads), 8 * heads)].rearrange("p (k h) -> p k h", h=heads)
                        if heads == 8:
                            dve.wait_ge(mm_done, s + 1 + CR)
                            p3 = PS[:, (q % 2) * 512:(q % 2) * 512 + 64].rearrange("p (k h) -> p k h", h=8)
                            a3 = t1.rearrange("p (k h) -> p k h", h=8)
                            nc.vector.tensor_tensor(a3, p3, g3[:, :, 128:136], ALU.add).then_inc(read_done, 1)
                            dve.wait_ge(read_done, s + 1 + CR)
                            nc.vector.scalar_tensor_tensor(t2, t1, 0.2, t1, ALU.mult, ALU.max).then_inc(s_c, 1)
                            dve.wait_ge(s_c, s + 1)
                            nc.vector.tensor_tensor(o, t2.rearrange("p (k h) -> p k h", h=8), pen_b,
                                                    ALU.add).then_inc(s_vd, 1)
                        else:
                            def reduce_slot(k):
                                n = 1 if k % 2 else 2
                                return nc.vector.tensor_reduce(
                                    t1[:, 32 * (q % 2) + 4 * k:32 * (q % 2) + 4 * k + n],
                                    prod[k % 4][:, 0:n * width].rearrange("p (h f) -> p h f", h=n), AX_X,
                                    ALU.add).then_inc(s_vd, 1)

                            for k in range(8):
                                c = s * 8 + k
                                dve.wait_ge(s_pd, c + 1)
                                dve.wait_ge(act_red, c + (1 - 4 + CR))
                                b = (k % 4) * 1024
                                p4 = PS[:, b:b + 1024].rearrange("p (b f) -> p b f", b=2)
                                xs = g3[:, k, :].unsqueeze(1).unsqueeze(1).to_broadcast([P, 2, 2, width])
                                nc.vector.tensor_tensor(
                                    prod[k % 4].rearrange("p (b h f) -> p b h f", b=2, h=2),
                                    p4[:, :, 0:258].rearrange("p b (h f) -> p b h f", h=2), xs,
                                    ALU.mult).then_inc(mul_done, 1)
                                if k:
                                    dve.wait_ge(mul_done, c + CR)
                                    reduce_slot(k - 1)
                            dve.wait_ge(mul_done, s * 8 + 8 + CR)
                            reduce_slot(7)
                            dve.wait_ge(s_vd, s * 8 + 8)
                            dve.wait_ge(act_red, s * 8 + 8 + CR)
                            nc.vector.tensor_tensor(
                                o, t1[:, 32 * (q % 2):32 * (q % 2) + 32].rearrange("p (k h) -> p k h", h=4), pen_b,
                                ALU.add).then_inc(read_done, 1)

                    onehots(0, 0, 0)
                    each_set(dve, step, aside.vector(dve) if aside else ())

        def stage_softmax(name, heads):
            C = P // heads
            L = K * P // C
            XS, KEY, RST, SC = (A[:, i * 6656:i * 6656 + L] for i in range(4))
            stage = [A[0:JB, 26624 + 512 * i:27136 + 512 * i] for i in range(4)]
            f4, c4, c2 = A[:, 28672:28676], A[0:heads, 28704:28704 + 4 * C], A[0:heads, 28832:28832 + 2 * C]
            w = [A[0:heads, 28960 + 32 * i:28960 + 32 * i + C] for i in range(4)]
            pq = A[:, 29216:29218]
            a3 = att[:, 0:K * heads].rearrange("p (k h) -> p k h", h=heads)
            HG = heads // 4
            s_tp, s_ev, s_ld, s_key, s_f4, s_c4, s_c2, s_pq, s_pr, s_lp, s_t2, s_sub = (
                sem(name + x) for x in ("_tp", "_ev", "_ld", "_key", "_f4", "_c4", "_c2", "_pq", "_pr", "_lp", "_t2",
                                        "_sub"))
            s_lo = [sem(f"{name}_lo{i}") for i in range(4)]
            s_lq = [sem(f"{name}_lq{i}") for i in range(4)]
            JOBS = 8 * HG

            def rows_of(d, j):
                b, g = j // HG, j % HG
                return d[4 * g:4 * g + 4, b * JB:(b + 1) * JB, :].rearrange("h k e -> k h e")
            with nc.Block() as block:
                @block.tensor
                def _(pe):
                    for j in range(JOBS):
                        if j >= 8:
                            pe.wait_ge(s_ev, j - 7)
                        for h in range(4):
                            o = (j % 8) * 512 + h * P
                            ins = nc.tensor.transpose(PS[0:JB, o:o + P],
                                                      a3[:, (j // HG) * JB:(j // HG + 1) * JB, 4 * (j % HG) + h],
                                                      ident[:])
                        ins.then_inc(s_tp, 1)
                    for j in range(JOBS):
                        pe.wait_ge(s_lo[j % 4], 16 * (j // 4 + 1))
                        if j < 8:
                            pe.wait_ge(s_ev, JOBS)
                        else:
                            pe.wait_ge(s_t2, j - 7)
                        for h in range(4):
                            o = (j % 8) * 512 + h * JB
                            ins = nc.tensor.transpose(PS[:, o:o + JB], stage[j % 4][:, h * P:(h + 1) * P],
                                                      ident[0:JB, 0:JB])
                        ins.then_inc(s_lp, 1)

                @block.scalar
                def _(act):
                    for j in range(JOBS):
                        act.wait_ge(s_tp, j + 1)
                        if j >= 4:
                            act.wait_ge(s_lq[j % 4], 16 * (j // 4))
                        nc.scalar.copy(stage[j % 4], PS[0:JB, (j % 8) * 512:(j % 8) * 512 + 512]).then_inc(s_ev, 1)
                    for j in range(JOBS):
                        act.wait_ge(s_lp, j + 1)
                        b, g = j // HG, j % HG
                        o = a3[:, b * JB:(b + 1) * JB, 4 * g:4 * g + 4].rearrange("p k h -> p h k")
                        nc.scalar.activation(o, PS[:, (j % 8) * 512:(j % 8) * 512 + 4 * JB]
                                             .rearrange("p (h k) -> p h k", h=4), ACT.Exp).then_inc(s_t2, 1)

                @block.sync
                def _(sp):
                    for h in range(heads):
                        sp.dma_start(KEY[h * C:(h + 1) * C, :],
                                     key_rows.rearrange("j e -> (j e)").rearrange("(c l) -> c l", c=C)
                                     ).then_inc(s_key, 16)
                    for j in range(JOBS):
                        sp.wait_ge(s_ev, j + 1)
                        sp.dma_start(rows_of(score_rows, j), stage[j % 4].rearrange("k (h e) -> k h e", h=4)
                                     ).then_inc(s_lq[j % 4], 16)
                    for i in range(4):
                        sp.wait_ge(s_lq[i], 16 * (JOBS // 4))
                    sp.dma_start(XS, score_rows[0:heads].rearrange("h k e -> (h k e)").rearrange("(q l) -> q l", q=P)
                                 ).then_inc(s_ld, 16)
                    sp.wait_ge(s_f4, 1)
                    sp.dma_start(carry_a, f4).then_inc(s_c4, 16)
                    sp.wait_ge(s_c4, 16)
                    sp.dma_start(c4, carry_a.rearrange("(h c) v -> h (c v)", h=heads)).then_inc(s_c4, 16)
                    sp.wait_ge(s_c2, 1)
                    sp.dma_start(carry_b.rearrange("(h c) v -> h (c v)", h=heads), c2).then_inc(s_pq, 16)
                    sp.wait_ge(s_pq, 16)
                    sp.dma_start(pq, carry_b).then_inc(s_pq, 16)
                    sp.wait_ge(s_sub, 1)
                    sp.dma_start(prob_rows[0:heads].rearrange("h k e -> (h k e)").rearrange("(q l) -> q l", q=P), XS
                                 ).then_inc(s_pr, 16)
                    sp.wait_ge(s_pr, 16)
                    for j in range(JOBS):
                        if j >= 4:
                            sp.wait_ge(s_lp, j - 3)
                        sp.dma_start(stage[j % 4].rearrange("k (h e) -> k h e", h=4), rows_of(prob_rows, j)
                                     ).then_inc(s_lo[j % 4], 16)

                @block.vector
                def _(dve):
                    ch = Chain(name + "_cv", dve)
                    dve.wait_ge(s_key, 16 * heads)
                    ch(dve.tensor_tensor(RST[:, 1:L], KEY[:, 1:L], KEY[:, 0:L - 1], ALU.is_equal))
                    ch(dve.tensor_scalar(RST[:, 1:L], RST[:, 1:L], -1.0, BIG, ALU.add, ALU.mult))
                    ch(dve.memset(RST[:, 0:1], -BIG))
                    dve.wait_ge(s_ld, 16)
                    ch(dve.tensor_tensor_scan(SC, RST, XS, -BIG, ALU.add, ALU.max))
                    ch(dve.tensor_tensor_scan(SC[:, 0:L - 1][:, ::-1], RST[:, 1:L][:, ::-1], SC[:, 0:L - 1][:, ::-1],
                                              SC[:, L - 1:L], ALU.add, ALU.max))
                    dve.tensor_copy(f4[:, 0:1], SC[:, 0:1])
                    dve.tensor_copy(f4[:, 1:2], SC[:, L - 1:L])
                    dve.tensor_copy(f4[:, 2:3], KEY[:, 0:1])
                    dve.tensor_copy(f4[:, 3:4], KEY[:, L - 1:L]).then_inc(s_f4, 1)
                    dve.wait_ge(s_c4, 32)
                    c43 = c4.rearrange("h (c v) -> h c v", v=4)
                    F, T, KF, KL = (c43[:, :, v] for v in range(4))
                    cont, single, link, run = w
                    ch(dve.memset(cont[:, 0:1], -BIG))
                    ch(dve.tensor_tensor(cont[:, 1:C], KF[:, 1:C], KL[:, 0:C - 1], ALU.is_equal))
                    ch(dve.tensor_scalar(cont[:, 1:C], cont[:, 1:C], -1.0, BIG, ALU.add, ALU.mult))
                    ch(dve.tensor_tensor(single, KF, KL, ALU.is_equal))
                    ch(dve.tensor_scalar(single, single, -1.0, BIG, ALU.add, ALU.mult))
                    c23 = c2.rearrange("h (c v) -> h c v", v=2)
                    ch(dve.memset(c2, -BIG))
                    ch(dve.tensor_tensor(link, cont, single, ALU.add))
                    ch(dve.tensor_tensor_scan(run, link, T, -BIG, ALU.add, ALU.max))
                    ch(dve.tensor_tensor(c23[:, 1:C, 0], run[:, 0:C - 1], cont[:, 1:C], ALU.add))
                    ch(dve.tensor_tensor(link[:, 0:C - 1], cont[:, 1:C], single[:, 0:C - 1], ALU.add))
                    ch(dve.memset(link[:, C - 1:C], -BIG))
                    ch(dve.tensor_tensor_scan(run[:, ::-1], link[:, ::-1], F[:, ::-1], -BIG, ALU.add, ALU.max))
                    dve.tensor_tensor(c23[:, 0:C - 1, 1], run[:, 1:C], cont[:, 1:C], ALU.add).then_inc(s_c2, 1)
                    dve.wait_ge(s_pq, 32)
                    for v, at in ((0, 0), (1, L - 1)):
                        ch(dve.tensor_scalar(RST, KEY, KEY[:, at:at + 1], None, ALU.is_equal))
                        ch(dve.tensor_scalar(RST, RST, -1.0, BIG, ALU.add, ALU.mult))
                        ch(dve.scalar_tensor_tensor(SC, RST, pq[:, v:v + 1], SC, ALU.add, ALU.max))
                    dve.tensor_tensor(XS, XS, SC, ALU.subtract).then_inc(s_sub, 1)

        def stage_aggregate(name, acc, chunks, heads=0, spill=None, width=D, table=None, idx=None, weighted=False,
                            edge_w=None, aside=None):
            W = sum(chunks)
            o = acc[1]
            ACC = A[:, acc[0]:acc[0] + NT * W]
            G = A[:, o:o + NQ * 8 * width]
            o += NQ * 8 * width
            M = [A[:, o + 1024 * i:o + 1024 * (i + 1)] for i in range(2)]
            o += 2048
            Y = [A[:, o + 8 * W * i:o + 8 * W * (i + 1)] for i in range(2)] if heads or edge_w is not None else None
            o += 16 * W if Y else 0
            if edge_w is not None:
                GE = A[:, o:o + NQ * 1024]
                o += NQ * 1024
            dcol = A[:, o:o + 8 * NQ]
            wcol = A[:, o + 32:o + 32 + 8 * NQ]
            idx_now = A[:, o + 64:o + 64 + 16 * NQ].bitcast(I32)
            assert o + 128 <= ARENA, (name, o)
            RG = 4 if len(chunks) == 2 or edge_w is not None or aside else 8
            full = [sem(f"{name}_g{q}") for q in range(NQ)]
            attr_full = [sem(f"{name}_at{q}") for q in range(NQ)]
            m_done, y_done, sum_done, add_done, z_done, r_done = (sem(name + x) for x in
                                                                  ("_m", "_y", "_s", "_a", "_z", "_r"))
            s_v, s_dd, s_ones = sem(name + "_v"), sem(name + "_dd"), sem(name + "_one")
            ya_done = sem(name + "_ya")
            mp_done = sem(name + "_mp")
            lead = len(chunks)
            MV = 6 if heads == 8 else 8

            def region(ss, c):
                return ((ss % RG) * lead + c) * 512
            with nc.Block() as block:
                @block.sync
                def _(sp):
                    if aside:
                        aside.loads(sp)
                        aside.stores(sp)
                    if spill is not None:
                        with sp.Fori(0, SETS // NQ) as i:
                            for q in range(NQ):
                                sp.wait_ge(y_done, i * NQ + (q + 1 - NQ + CR))
                                if heads == 4:
                                    sp.wait_ge(ya_done, i * NQ + (q + 1 - NQ + CR))
                                sp.dma_start(G[:, q * 8 * width:(q + 1) * 8 * width],
                                             spill[bass.ds(i * NQ + q, 1), :, :].rearrange("o p f -> (o p) f")
                                             ).then_inc(full[q], 16)
                    if edge_w is not None:
                        sp.wait_ge(s_ones, 1)
                        with sp.Fori(0, SETS // NQ) as i:
                            for q in range(NQ):
                                s = i * NQ + q
                                sp.wait_ge(z_done, s + (1 - NQ + CR))
                                for u in range(4):
                                    e = sp.value_load(estep[0:1, bass.ds(s * 4 + u, 1)], min_val=0, max_val=ST - 1)
                                    sp.dma_start(GE[0:16, (q * 4 + u) * 256:(q * 4 + u + 1) * 256]
                                                 .rearrange("f (g e) -> f g e", g=2),
                                                 t["attr_t"][bass.ds(e * 2, 2), :, :].rearrange("g f e -> f g e")
                                                 ).then_inc(attr_full[q], 16)

                if heads:
                    @block.gpsimd
                    def _(pool):
                        pool.sem_inc(y_done, CR)
                        with pool.Fori(0, SETS // NQ) as i:
                            for q in range(NQ):
                                s = i * NQ + q
                                pool.wait_ge(sum_done, s * 4 + (4 - 8 + CR))
                                if heads == 8:
                                    pool.wait_ge(s_v, s + 1)
                                    pool.sem_inc(s_dd, 1)
                                    for k in range(MV, 8):
                                        ins = nc.gpsimd.tensor_scalar(
                                            M[q % 2][:, k * P:(k + 1) * P], iota_row[:],
                                            dcol[:, 8 * q + k:8 * q + k + 1], None, ALU.is_equal)
                                    ins.then_inc(mp_done, 1)
                                pool.wait_ge(full[q], i * 16 + 16)
                                y3 = Y[q % 2].rearrange("p (k f) -> p k f", f=W)
                                g3 = G[:, q * 8 * width:(q + 1) * 8 * width].rearrange("p (k f) -> p k f", f=width)
                                p3 = att[:, bass.ds(s * (8 * heads), 8 * heads)].rearrange("p (k h) -> p k h", h=heads)
                                if heads == 8:
                                    nc.gpsimd.tensor_copy(y3[:, :, D:D + 8], p3)
                                    nc.gpsimd.tensor_tensor(y3[:, :, 0:D].rearrange("p k (h c) -> p k h c", h=8),
                                                            g3[:, :, 0:D].rearrange("p k (h c) -> p k h c", h=8),
                                                            bc_in(p3, 16), ALU.mult).then_inc(y_done, 1)
                                else:
                                    for c in range(2):
                                        nc.gpsimd.tensor_copy(y3[:, :, c * 258 + 256:c * 258 + 258],
                                                              p3[:, :, 2 * c:2 * c + 2])
                                    for h in range(2):
                                        ins = nc.gpsimd.tensor_tensor(y3[:, :, h * D:(h + 1) * D], g3[:, :, 0:D],
                                                                      bc_in(p3[:, :, h], D), ALU.mult)
                                    ins.then_inc(y_done, 1)

                if table is not None:
                    @block.gpsimd
                    def _(pool):
                        gather_sets(pool, name, table, idx, G, width, idx_now, full,
                                    [(sum_done, 4) if edge_w is None else (r_done, 1)])

                @block.scalar
                def _(act):
                    if aside:
                        aside.scalar(act)
                    if heads == 4:
                        act.sem_inc(ya_done, CR)
                        with act.Fori(0, SETS // NQ) as i:
                            for q in range(NQ):
                                s = i * NQ + q
                                act.wait_ge(full[q], i * 16 + 16)
                                act.wait_ge(sum_done, s * 4 + (4 - 8 + CR))
                                act.sem_inc(s_dd, 1)
                                y3 = Y[q % 2].rearrange("p (k f) -> p k f", f=W)
                                for k in range(8):
                                    for h in (2, 3):
                                        o = 258 + (h - 2) * D
                                        ins = nc.scalar.activation(
                                            y3[:, k, o:o + D], G[:, (q * 8 + k) * width:(q * 8 + k) * width + D],
                                            ACT.Copy, scale=att[:, bass.ds(s * 32 + (k * 4 + h), 1)])
                                ins.then_inc(ya_done, 1)
                    if edge_w is not None:
                        act.sem_inc(r_done, CR)
                        with act.Fori(0, SETS // NQ) as i:
                            for q in range(NQ):
                                s = i * NQ + q
                                act.wait_ge(sum_done, s * 4 + (4 - 8 + CR))
                                act.wait_ge(full[q], i * 128 + 128)
                                act.sem_inc(s_dd, 1)
                                y3 = Y[q % 2].rearrange("p (k f) -> p k f", f=W)
                                for k in range(8):
                                    nc.scalar.activation(y3[:, k, 0:D], G[:, (q * 8 + k) * D:(q * 8 + k + 1) * D],
                                                         ACT.Copy, scale=wgt[:, bass.ds(s * 8 + k, 1)])
                                act.wait_ge(z_done, s + 1 + CR)
                                for v in range(2):
                                    b = 2048 + (q % 2) * 1024 + v * 512
                                    ins = nc.scalar.activation(
                                        y3[:, 4 * v:4 * v + 4, D:2 * D],
                                        PS[:, b:b + 512].rearrange("p (k f) -> p k f", f=D), ACT.Relu)
                                ins.then_inc(r_done, 1)

                @block.tensor
                def _(pe):
                    pe.sem_inc(sum_done, CR)
                    if edge_w is not None:
                        pe.sem_inc(z_done, CR)

                    def features(i, q, s):
                        pe.wait_ge(attr_full[q], i * 64 + 64)
                        pe.wait_ge(r_done, s + (1 - 2 + CR))
                        for k in range(8):
                            b = 2048 + (q % 2) * 1024 + k * P
                            ins = nc.tensor.matmul(PS[:, b:b + P], GE[0:17, (q * 8 + k) * P:(q * 8 + k + 1) * P],
                                                   edge_w, start=True, stop=True)
                        ins.then_inc(z_done, 1)

                    def step(i, q, s, more):
                        if edge_w is not None:
                            if more:
                                features(*after(i, q))
                            pe.wait_ge(r_done, s + 1 + CR)
                        elif table is not None:
                            pe.wait_ge(full[q], i * 128 + 128)
                        if heads:
                            pe.wait_ge(y_done, s + 1 + CR)
                        if heads == 4:
                            pe.wait_ge(ya_done, s + 1 + CR)
                        pe.wait_ge(m_done, s + 1)
                        if heads == 8:
                            pe.wait_ge(mp_done, s + 1)
                        for u in range(4):
                            ss = s * 4 + u
                            pe.wait_ge(add_done, ss * 2 + (2 - 2 * RG + CR))
                            for c, wc in enumerate(chunks):
                                b, at = region(q * 4 + u, c), sum(chunks[:c])
                                for g in range(2):
                                    k = 2 * u + g
                                    rhs = (Y[q % 2][:, k * W + at:k * W + at + wc] if Y else
                                           G[:, (q * 8 + k) * width:(q * 8 + k) * width + wc])
                                    ins = nc.tensor.matmul(PS[:, b:b + wc], M[q % 2][:, k * P:(k + 1) * P], rhs,
                                                           start=(g == 0), stop=(g == 1))
                            ins.then_inc(sum_done, 1)

                    if edge_w is not None:
                        pe.wait_ge(s_ones, 1)
                        features(0, 0, 0)
                    each_set(pe, step, aside.tensor(pe) if aside else ())

                @block.vector
                def _(dve):
                    ch = Chain(name + "_c0", dve)
                    ch(dve.memset(ACC, 0.0))
                    if edge_w is not None:
                        ch(dve.memset(GE[0:32, :], 1.0))
                        for y in Y:
                            ch(dve.memset(y.rearrange("p (k f) -> p k f", f=W)[:, :, 2 * D:2 * D + 1], 1.0))
                        dve.sem_inc(s_ones, 1)
                    dve.sem_inc(add_done, CR)

                    def prepare(i, q, s, load=lambda: None):
                        dve.wait_ge(sum_done, s * 4 + (4 - 8 + CR))
                        nc.vector.tensor_scalar(dcol[:, 8 * q:8 * q + 8], drel[:, bass.ds(s * 8, 8)], 1.0, None,
                                                ALU.mult).then_inc(s_v, 1)
                        if weighted:
                            nc.vector.tensor_scalar(wcol[:, 8 * q:8 * q + 8], wgt[:, bass.ds(s * 8, 8)], 1.0, None,
                                                    ALU.mult).then_inc(s_v, 1)
                        dve.wait_ge(s_v, s * 2 + 2 if weighted else s + 1)
                        for k in range(MV):
                            c = 8 * q + k
                            if weighted:
                                ins = nc.vector.tensor_scalar(M[q % 2][:, k * P:(k + 1) * P], iota_row[:],
                                                              dcol[:, c:c + 1], wcol[:, c:c + 1], ALU.is_equal, ALU.mult)
                            else:
                                ins = nc.vector.tensor_scalar(M[q % 2][:, k * P:(k + 1) * P], iota_row[:],
                                                              dcol[:, c:c + 1], None, ALU.is_equal)
                        ins.then_inc(m_done, 1)
                        tiles = load()
                        return tiles

                    def add_up(q, s, tiles):
                        for u, n in enumerate(tiles):
                            ss = s * 4 + u
                            dve.wait_ge(sum_done, ss + 1 + CR)
                            if heads == 8:
                                dve.wait_ge(add_done, ss * 2 + CR)
                                a = ACC[:, bass.ds(n * W, W)]
                                b = region(q * 4 + u, 0)
                                nc.vector.tensor_tensor(a, a, PS[:, b:b + W], ALU.add).then_inc(add_done, 2)
                                continue
                            for v in range(2):
                                dve.wait_ge(add_done, ss * 2 + (v - 1 + CR))
                                lo, hi = ((0, W // 2), (W // 2, W))[v]
                                b = region(q * 4 + u, v if lead == 2 else 0) + (0 if lead == 2 else lo)
                                a = ACC[:, bass.ds(n * W + lo, hi - lo)]
                                nc.vector.tensor_tensor(a, a, PS[:, b:b + hi - lo], ALU.add).then_inc(add_done, 1)

                    def tiles_of(s):
                        return load_tiles(mybir.EngineType.DVE, ntile, s * 4, NT - 1)

                    def step(i, q, s, more):
                        if more:
                            tiles = prepare(*after(i, q), lambda: tiles_of(s))
                        else:
                            tiles = tiles_of(s)
                        add_up(q, s, tiles)

                    prepare(0, 0, 0)
                    each_set(dve, step, aside.vector(dve) if aside else ())
            return ACC

        def bn_vector(dve, ch, Z, gamma, beta, v, mean_scale=None, by_group=None):
            mean, var, std = v[0:3]
            _, s_cen, _, s_sum, s_var, s_std = v[3]
            dve.wait_ge(s_sum, 1)
            ch(dve.tensor_scalar(mean, PS[:, 3584:3584 + D], 1.0 / N, None, ALU.mult))
            if mean_scale is not None:
                ch(dve.tensor_tensor(mean, mean, mean_scale, ALU.mult))
            for a, b in GROUPS:
                dve.tensor_tensor(v3(Z[:, a * D:b * D]), v3(Z[:, a * D:b * D]), bc_mid(mean, b - a), ALU.subtract
                                  ).then_inc(s_cen, 1)
            dve.wait_ge(s_sum, 2)
            dve.tensor_scalar(var, PS[:, 3584:3584 + D], 1.0 / N, LN_EPS, ALU.mult, ALU.add).then_inc(s_var, 1)
            dve.wait_ge(s_std, 1)
            ch(dve.reciprocal(std, std))
            ch(dve.tensor_tensor(std, std, gamma, ALU.mult))
            dve.wait_ge(s_cen, len(GROUPS))
            ch(dve.tensor_tensor(v3(Z), v3(Z), bc_mid(std, NT), ALU.mult))
            if by_group is None:
                ch(dve.tensor_tensor(v3(Z), v3(Z), bc_mid(beta, NT), ALU.add))
                return
            for a, b in GROUPS:
                z = v3(Z[:, a * D:b * D])
                dve.tensor_tensor(z, z, bc_mid(beta, b - a), ALU.add).then_inc(by_group, 1)

        def bn_sems(name):
            return tuple(sem(f"{name}_bn{x}") for x in ("z", "cen", "sq", "sum", "var", "std"))

        def bn_tensor(pe, Z, SQ, sems):
            s_z, _, s_sq, s_sum, _, _ = sems
            node_sum(pe, Z, PS[:, 3584:3584 + D], s_z, s_sum)
            node_sum(pe, SQ, PS[:, 3584:3584 + D], s_sq, s_sum)

        def bn_scalar(act, Z, SQ, var, std, sems):
            _, s_cen, s_sq, _, s_var, s_std = sems
            for g, (a, b) in enumerate(GROUPS):
                act.wait_ge(s_cen, g + 1)
                nc.scalar.activation(SQ[:, a * D:b * D], Z[:, a * D:b * D], ACT.Square).then_inc(s_sq, 1)
            act.wait_ge(s_var, 1)
            nc.scalar.activation(std, var, ACT.Sqrt).then_inc(s_std, 1)

        def stage_gat_table():
            s_w, s_mm, s_ev, s_st, s_tab = sem("g0_w"), sem("g0_mm"), sem("g0_ev"), sem("g0_st"), sem("g0_tab")
            ad = A[:, 0:NT * 8]
            tab = A[:, 256:256 + NT * 136].rearrange("p (t f) -> p t f", f=136)
            w, asb, adb = A[:, 4096:4224], A[:, 4224:4352], A[:, 4352:4480]
            tmp = A[:, 4608:4608 + NW]
            with nc.Block() as block:
                @block.sync
                def _(sp):
                    sp.dma_start(w, t["L0_gnn_W"]).then_inc(s_w, 16)
                    bcast_load(sp, asb, t["L0_gnn_att_src"].rearrange("h c -> (h c)")).then_inc(s_w, 16)
                    bcast_load(sp, adb, t["L0_gnn_att_dst"].rearrange("h c -> (h c)")).then_inc(s_w, 16)
                    sp.wait_ge(s_st, 1)
                    sp.dma_start(tab0.rearrange("(t p) f -> p t f", p=P), tab).then_inc(s_tab, 16)
                    sp.wait_ge(s_tab, 16)

                @block.tensor
                def _(pe):
                    pe.wait_ge(s_w, 48)
                    project_tiles(pe, HT, w, s_mm)

                @block.scalar
                def _(act):
                    for g in range(7):
                        a, b = 4 * g, min(4 * g + 4, NT)
                        act.wait_ge(s_mm, g + 1)
                        nc.scalar.copy(tab[:, a:b, 0:D], v3(PS[:, a * D:b * D])).then_inc(s_ev, 1)

                @block.vector
                def _(dve):
                    ch = Chain("g0_c", dve)
                    dve.wait_ge(s_w, 48)
                    dve.wait_ge(s_ev, 7)
                    ch(dve.tensor_tensor(v3(tmp), tab[:, :, 0:D], bc_mid(adb, NT), ALU.mult))
                    ch(dve.tensor_reduce(ad.rearrange("p (t h) -> p t h", h=8),
                                         tmp.rearrange("p (t h c) -> p t h c", t=NT, c=16), AX_X, ALU.add))
                    ch(dve.tensor_tensor(v3(tmp), tab[:, :, 0:D], bc_mid(asb, NT), ALU.mult))
                    dve.tensor_reduce(tab[:, :, D:D + 8], tmp.rearrange("p (t h c) -> p t h c", t=NT, c=16), AX_X,
                                      ALU.add).then_inc(s_st, 1)
            return ad

        def stage_gat_end(ACC):
            s_w = sem("g1_w")
            bn = bn_sems("g1")
            base = NT * 136
            Z, SQ = A[:, base:base + NW], A[:, base + NW:base + 2 * NW]
            rd = A[:, base + 2 * NW:base + 2 * NW + NT * 8]
            o = base + 2 * NW + 256
            bias, gam, bet, mean, var, std = (A[:, o + D * i:o + D * (i + 1)] for i in range(6))
            a3 = ACC.rearrange("p (t f) -> p t f", f=136)
            with nc.Block() as block:
                @block.sync
                def _(sp):
                    bcast_load(sp, bias, t["L0_gnn_bias"]).then_inc(s_w, 16)
                    bcast_load(sp, gam, t["L0_gnn_gamma"]).then_inc(s_w, 16)
                    bcast_load(sp, bet, t["L0_gnn_beta"]).then_inc(s_w, 16)

                @block.vector
                def _(dve):
                    ch = Chain("g1_c", dve)
                    r3 = rd.rearrange("p (t h) -> p t h", h=8)
                    ch(dve.tensor_scalar(r3, a3[:, :, D:D + 8], 1e-16, None, ALU.add))
                    ch(dve.reciprocal(rd, rd))
                    ch(dve.tensor_tensor(Z.rearrange("p (t h c) -> p t h c", t=NT, c=16),
                                         a3[:, :, 0:D].rearrange("p t (h c) -> p t h c", c=16), bc_in(r3, 16),
                                         ALU.mult))
                    dve.wait_ge(s_w, 48)
                    for a, b in GROUPS:
                        z = v3(Z[:, a * D:b * D])
                        dve.tensor_tensor(z, z, bc_mid(bias, b - a), ALU.add).then_inc(bn[0], 1)
                    ch(dve.tensor_tensor(X[:], X[:], H[:], ALU.add))
                    dve.wait_ge(bn[0], len(GROUPS))
                    bn_vector(dve, ch, Z, gam, bet, (mean, var, std, bn))
                    ch(dve.scalar_tensor_tensor(X[:], Z, 0.0, X[:], ALU.max, ALU.add))

                @block.tensor
                def _(pe):
                    bn_tensor(pe, Z, SQ, bn)

                @block.scalar
                def _(act):
                    bn_scalar(act, Z, SQ, var, std, bn)

        def stage_rel_table(name, i, base):
            s_w, s_mm, s_ea, s_ev = (sem(name + x) for x in ("_w", "_mm", "_ea", "_ev"))
            s_out = [sem(f"{name}_o{i}") for i in range(4)]
            wr = A[:, base:base + 1024]
            tb = [A[:, base + 1024 * (i + 1):base + 1024 * (i + 2)] for i in range(4)]
            tab3 = tab_rel.rearrange("(t p r) o -> t p (r o)", p=P, r=R_REL)
            with nc.Block() as block:
                @block.sync
                def _(sp):
                    sp.dma_start(wr, rel_w[i]).then_inc(s_w, 16)
                    for a in range(NT):
                        sp.wait_ge(s_ea, a + 1)
                        sp.wait_ge(s_ev, a + 1)
                        sp.dma_start(tab3[a], tb[a % 4]).then_inc(s_out[a % 4], 16)
                    for j in range(4):
                        sp.wait_ge(s_out[j], 16 * len(range(j, NT, 4)))

                @block.vector
                def _(dve):
                    for a in range(NT):
                        dve.wait_ge(s_mm, a + 1)
                        if a >= 4:
                            dve.wait_ge(s_out[a % 4], 16 * (a // 4))
                        b = (a % 4) * 1024
                        dve.tensor_copy(tb[a % 4][:, 0:512], PS[:, b:b + 512]).then_inc(s_ev, 1)

                @block.scalar
                def _(act):
                    for a in range(NT):
                        act.wait_ge(s_mm, a + 1)
                        if a >= 4:
                            act.wait_ge(s_out[a % 4], 16 * (a // 4))
                        b = (a % 4) * 1024 + 512
                        nc.scalar.copy(tb[a % 4][:, 512:1024], PS[:, b:b + 512]).then_inc(s_ea, 1)

                @block.tensor
                def _(pe):
                    pe.wait_ge(s_w, 16)
                    for a in range(NT):
                        if a >= 4:
                            pe.wait_ge(s_ev, a - 3)
                            pe.wait_ge(s_ea, a - 3)
                        for c in range(2):
                            b = (a % 4) * 1024 + 512 * c
                            ins = nc.tensor.matmul(PS[:, b:b + 512], HT[:, a * P:(a + 1) * P],
                                                   wr[:, 512 * c:512 * (c + 1)], start=True, stop=True)
                        ins.then_inc(s_mm, 1)

        def stage_rel_end(name, ACC, bias_ap, first):
            s_w, s_h, s_t = sem(name + "_w"), sem(name + "_h"), sem(name + "_t")
            bias = A[:, ARENA - D:ARENA]
            with nc.Block() as block:
                @block.sync
                def _(sp):
                    bcast_load(sp, bias, bias_ap).then_inc(s_w, 16)

                @block.vector
                def _(dve):
                    ch = Chain(name + "_c", dve)
                    dve.wait_ge(s_w, 16)
                    a3 = ACC.rearrange("p (t f) -> p t f", t=NT)[:, :, 0:D]
                    ch(dve.tensor_tensor(a3, a3, bc_mid(bias, NT), ALU.add))
                    if first:
                        dve.tensor_scalar(v3(H[:]), a3, 0.0, None, ALU.max).then_inc(s_h, 7)
                    else:
                        ch(dve.tensor_tensor(X[:], X[:], ACC, ALU.add))
                if first:
                    @block.tensor
                    def _(pe):
                        transpose_tiles(pe, H, s_h, s_t)

                    @block.scalar
                    def _(act):
                        for g in range(7):
                            a, b = 512 * g, min(512 * g + 512, NP)
                            act.wait_ge(s_t, g + 1)
                            nc.scalar.copy(HT[:, a:b], PS[:, a:b])

        def stage_queries():
            s_w, s_tab, s_q, s_qe, s_u, s_ue = (sem("q_" + x) for x in ("w", "tab", "q", "qe", "u", "ue"))
            U = A[:, 0:NT * 516]
            o = NT * 516
            wq, wkt = A[:, o:o + 512], A[:, o + 512:o + 1028]
            bq = A[:, o + 1032:o + 1036]
            qt = [A[:, o + 1040 + 512 * i:o + 1552 + 512 * i] for i in range(2)]
            with nc.Block() as block:
                @block.sync
                def _(sp):
                    sp.dma_start(wq, t["L2_gnn_Wq"]).then_inc(s_w, 16)
                    sp.dma_start(wkt, t["wkb_t"]).then_inc(s_w, 16)
                    sp.dma_start(bq, t["bq_t"]).then_inc(s_w, 16)
                    sp.dma_start(tab_x.rearrange("(t p) f -> p t f", p=P), v3(H[:])).then_inc(s_tab, 16)
                    sp.wait_ge(s_tab, 16)

                @block.tensor
                def _(pe):
                    pe.wait_ge(s_w, 48)
                    for a in range(NT + 1):
                        if a < NT:
                            if a >= 2:
                                pe.wait_ge(s_qe, a - 1)
                            for h in range(4):
                                o = (a % 2) * 512 + h * P
                                ins = nc.tensor.matmul(PS[:, o:o + P], wq[:, h * P:(h + 1) * P],
                                                       HT[:, a * P:(a + 1) * P], start=True, stop=True)
                            ins.then_inc(s_q, 1)
                        if a > 0:
                            b = a - 1
                            pe.wait_ge(s_qe, b + 1)
                            if b >= 2:
                                pe.wait_ge(s_ue, b - 1)
                            for h in range(4):
                                o = 1024 + (b % 2) * 1024 + (h // 2) * 512
                                lhsT = qt[b % 2][:, h * P:(h + 1) * P]
                                ins = nc.tensor.matmul(PS[:, o + (h % 2) * 129:o + (h % 2) * 129 + 129], lhsT,
                                                       wkt[:, h * 129:(h + 1) * 129], start=True, stop=True)
                            ins.then_inc(s_u, 1)

                @block.vector
                def _(dve):
                    dve.wait_ge(s_w, 48)
                    for a in range(NT):
                        dve.wait_ge(s_q, a + 1)
                        if a >= 2:
                            dve.wait_ge(s_u, a - 1)
                        dve.tensor_tensor(qt[a % 2].rearrange("c (h n) -> c h n", h=4),
                                          PS[:, (a % 2) * 512:(a % 2) * 512 + 512].rearrange("c (h n) -> c h n", h=4),
                                          bc_in(bq, P), ALU.add).then_inc(s_qe, 1)

                @block.scalar
                def _(act):
                    for a in range(NT):
                        act.wait_ge(s_u, a + 1)
                        o = 1024 + (a % 2) * 1024
                        nc.scalar.activation(U[:, a * 516:(a + 1) * 516].rearrange("p (c f) -> p c f", c=2),
                                             PS[:, o:o + 1024].rearrange("p (c f) -> p c f", c=2)[:, :, 0:258],
                                             ACT.Copy, scale=float(D) ** -0.5).then_inc(s_ue, 1)
            return U

        def stage_transformer_end(ACC):
            names = ("w", "zn", "zt", "ze", "at", "ae", "o", "oe", "ske", "tm", "gr", "pk", "sig", "gin", "gelu")
            s_w, s_zn, s_zt, s_ze, s_at, s_ae, s_o, s_oe, s_ske, s_tm, s_gr, s_pk, s_sig, s_gin, s_gelu = (
                sem("t_" + x) for x in names)
            bn = bn_sems("t")
            o = NT * 516
            OUT, SK, T1 = (A[:, o + NW * i:o + NW * (i + 1)] for i in range(3))
            o += 3 * NW
            wv, wsk = A[:, o:o + 512], A[:, o + 512:o + 640]
            bv = A[0:4, o + 640:o + 768]
            vec = [A[:, o + 768 + D * i:o + 896 + D * i] for i in range(10)]
            bsk, wb1, wb2, wb3, gw, gb, gm, mean, var, std = vec
            o += 768 + 1280
            rd, ra = A[:, o:o + 100], A[:, o + 100:o + 200]
            gt, sg = A[:, o + 200:o + 225], A[:, o + 232:o + 257]
            zt = [A[:, o + 260 + 512 * i:o + 772 + 512 * i] for i in range(2)]
            aT = [A[0:4, o + 1284 + P * i:o + 1412 + P * i] for i in range(2)]
            TM = [A[:, o + 1540 + 256 * i:o + 1796 + 256 * i] for i in range(2)]
            assert o + 2052 <= ARENA
            a4 = ACC.rearrange("p (t c f) -> p t c f", c=2, f=258)
            r4 = rd.rearrange("p (t c h) -> p t c h", c=2, h=2)
            with nc.Block() as block:
                @block.sync
                def _(sp):
                    sp.dma_start(wv, t["L2_gnn_Wv"]).then_inc(s_w, 16)
                    sp.dma_start(wsk, t["L2_gnn_Wskip"]).then_inc(s_w, 16)
                    sp.dma_start(bv, t["L2_gnn_bv"].rearrange("(h c) -> h c", h=4)).then_inc(s_w, 16)
                    bcast_load(sp, bsk, t["L2_gnn_bskip"]).then_inc(s_w, 16)
                    for i, w in enumerate((wb1, wb2, wb3)):
                        bcast_load(sp, w, t["L2_gnn_Wbeta"][i * D:(i + 1) * D]).then_inc(s_w, 16)
                    bcast_load(sp, gw, t["L2_gnn_gn_weight"]).then_inc(s_w, 16)
                    bcast_load(sp, gb, t["L2_gnn_gn_bias"]).then_inc(s_w, 16)
                    bcast_load(sp, gm, t["L2_gnn_gn_mean_scale"]).then_inc(s_w, 16)

                @block.tensor
                def _(pe):
                    pe.wait_ge(s_w, 160)
                    for a in range(NT + 1):
                        if a < NT:
                            pe.wait_ge(s_zn, a // 4 + 1)
                            if a >= 2:
                                pe.wait_ge(s_ze, a - 1)
                                pe.wait_ge(s_ae, a - 1)
                            for h in range(4):
                                b = (a % 2) * 512 + h * P
                                ins = nc.tensor.transpose(PS[:, b:b + P],
                                                          a4[:, a, h // 2, (h % 2) * D:(h % 2) * D + D], ident[:])
                            ins.then_inc(s_zt, 1)
                            b = 1024 + (a % 2) * 512
                            nc.tensor.transpose(PS[0:4, b:b + P], ra[:, 4 * a:4 * a + 4], ident[:]).then_inc(s_at, 1)
                        if a > 0:
                            c = a - 1
                            if c >= 2:
                                pe.wait_ge(s_oe, c - 1)
                                pe.wait_ge(s_ske, c - 1)
                            b = 3072 + (c % 2) * 512
                            nc.tensor.matmul(PS[:, b:b + D], HT[:, c * P:(c + 1) * P], wsk, start=True, stop=True)
                            b = 2048 + (c % 2) * 512
                            pe.wait_ge(s_ze, c + 1)
                            pe.wait_ge(s_ae, c + 1)
                            for h in range(4):
                                nc.tensor.matmul(PS[:, b:b + D], zt[c % 2][:, h * P:(h + 1) * P],
                                                 wv[:, h * D:(h + 1) * D], start=(h == 0), stop=False)
                            nc.tensor.matmul(PS[:, b:b + D], aT[c % 2], bv, start=False, stop=True).then_inc(s_o, 1)
                    pe.wait_ge(s_ske, NT)
                    bn_tensor(pe, OUT, T1, bn)

                @block.scalar
                def _(act):
                    for a in range(NT):
                        act.wait_ge(s_zt, a + 1)
                        if a >= 2:
                            act.wait_ge(s_o, a - 1)
                        nc.scalar.copy(zt[a % 2], PS[:, (a % 2) * 512:(a % 2) * 512 + 512]).then_inc(s_ze, 1)
                        act.wait_ge(s_at, a + 1)
                        nc.scalar.copy(aT[a % 2], PS[0:4, 1024 + (a % 2) * 512:1024 + (a % 2) * 512 + P]
                                       ).then_inc(s_ae, 1)
                    act.wait_ge(s_gr, NT)
                    nc.scalar.activation(sg, gt, ACT.Sigmoid).then_inc(s_sig, 1)
                    bn_scalar(act, OUT, T1, var, std, bn)
                    for g, (a, b) in enumerate(GROUPS):
                        act.wait_ge(s_gin, g + 1)
                        nc.scalar.activation(T1[:, a * D:b * D], OUT[:, a * D:b * D], ACT.Gelu).then_inc(s_gelu, 1)

                @block.gpsimd
                def _(pool):
                    for c in range(NT):
                        pool.wait_ge(s_tm, 2 * c + 2)
                        sk = SK[:, c * D:(c + 1) * D]
                        nc.gpsimd.tensor_tensor(sk, sk, OUT[:, c * D:(c + 1) * D], ALU.subtract).then_inc(s_pk, 1)

                @block.vector
                def _(dve):
                    ch = Chain("t_c", dve)
                    den = a4[:, :, :, 256:258]
                    ch(dve.tensor_scalar(r4, den, 1e-16, None, ALU.add))
                    ch(dve.reciprocal(rd, rd))
                    ch(dve.tensor_scalar(rd, rd, 0.25, None, ALU.mult))
                    ch(dve.tensor_tensor(ra.rearrange("p (t c h) -> p t c h", c=2, h=2), den, r4, ALU.mult))

                    def normalise(g):
                        lo, hi = GROUPS[g]
                        for c in range(2):
                            z = a4[:, lo:hi, c, 0:256].rearrange("p t (h f) -> p t h f", h=2)
                            ins = dve.tensor_tensor(z, z, bc_in(r4[:, lo:hi, c, :], D), ALU.mult)
                        ins.then_inc(s_zn, 1)

                    normalise(0)
                    dve.wait_ge(s_w, 160)
                    dve.tensor_tensor(wb1, wb1, wb3, ALU.add)
                    ch(dve.tensor_tensor(wb2, wb2, wb3, ALU.subtract))
                    for a in range(NT + 3):
                        if a % 4 == 0 and a // 4 + 1 < len(GROUPS):
                            normalise(a // 4 + 1)
                        if 1 <= a <= NT:
                            c = a - 1
                            dve.wait_ge(s_o, c + 1)
                            b = (c % 2) * 512
                            dve.tensor_copy(OUT[:, c * D:(c + 1) * D], PS[:, 2048 + b:2048 + b + D]).then_inc(s_oe, 1)
                            dve.tensor_tensor(SK[:, c * D:(c + 1) * D], PS[:, 3072 + b:3072 + b + D], bsk, ALU.add
                                              ).then_inc(s_ske, 1)
                        if 2 <= a <= NT + 1:
                            c = a - 2
                            dve.wait_ge(s_ske, c + 1)
                            dve.wait_ge(s_oe, c + 1)
                            if c >= 2:
                                dve.wait_ge(s_gr, c - 1)
                            dve.tensor_tensor(TM[c % 2][:, 0:D], OUT[:, c * D:(c + 1) * D], wb1, ALU.mult
                                              ).then_inc(s_tm, 1)
                            dve.tensor_tensor(TM[c % 2][:, D:2 * D], SK[:, c * D:(c + 1) * D], wb2, ALU.mult
                                              ).then_inc(s_tm, 1)
                        if a >= 3:
                            c = a - 3
                            dve.wait_ge(s_tm, 2 * c + 2)
                            dve.tensor_reduce(gt[:, c:c + 1], TM[c % 2], AX_X, ALU.add).then_inc(s_gr, 1)
                    dve.wait_ge(s_sig, 1)
                    dve.wait_ge(s_pk, NT)
                    ch(dve.tensor_tensor(v3(SK), v3(SK), bc_in(sg, D), ALU.mult))
                    for a, b in GROUPS:
                        c = slice(a * D, b * D)
                        dve.tensor_tensor(OUT[:, c], OUT[:, c], SK[:, c], ALU.add).then_inc(bn[0], 1)
                    ch(dve.tensor_tensor(X[:], X[:], H[:], ALU.add))
                    dve.wait_ge(bn[0], len(GROUPS))
                    bn_vector(dve, ch, OUT, gw, gb, (mean, var, std, bn), mean_scale=gm, by_group=s_gin)
                    for g, (a, b) in enumerate(GROUPS):
                        c = slice(a * D, b * D)
                        dve.wait_ge(s_gelu, g + 1)
                        dve.tensor_tensor(X[:, c], X[:, c], T1[:, c], ALU.add)

        EP, EQ = 125, E // 125

        class WeightsAside:

            def __init__(self, base):
                (self.s_ld, self.s_m, self.s_cen, self.s_gm, self.s_g, self.s_r, self.s_rc, self.s_t, self.s_tw, self.s_v,
                 self.s_var, self.s_std, self.s_mr, self.s_row, self.s_row2, self.s_wl, self.s_wr, self.s_ws) = (
                    sem("e_" + x) for x in ("ld", "m", "cen", "gm", "g", "r", "rc", "t", "tw", "v", "var", "std", "mr",
                                            "row", "row2", "wl", "wr", "ws"))
                self.at = A[0:EP, base:base + EQ * 16]
                o = base + EQ * 16
                self.w1 = A[0:16, o:o + D]
                self.g1, self.bb1, self.b1 = (A[0:17, o + (2 + i) * D:o + (3 + i) * D] for i in range(3))
                self.mean = A[:, o + 640:o + 656]
                self.mcol = A[0:16, o + 656:o + 657]
                self.var, self.std = A[0:16, o + 768:o + 896], A[0:16, o + 896:o + 1024]
                self.row = A[0:1, o + 1024:o + 1152]
                self.gm, self.bm, self.selm = A[:, o + 1152:o + 1280], A[:, o + 1280:o + 1408], A[:, o + 1408:o + 1424]
                self.cov, self.tw = A[0:16, o + 1424:o + 1440], A[0:16, o + 1536:o + 1664]
                self.dm = A[0:16, o + 1664:o + 1680]
                self.ri, self.pi, self.fi = (A[:, o + 1792 + 128 * i:o + 1920 + 128 * i].bitcast(I32) for i in range(3))
                self.rf, self.pf, self.qf = (A[:, o + 2176 + 128 * i:o + 2304 + 128 * i] for i in range(3))
                o += 2560
                self.v = [A[:, o + 2112 * i:o + 2112 * i + 1024] for i in range(2)]
                self.wr = [A[:, o + 2112 * i + 1024:o + 2112 * i + 2048] for i in range(2)]
                self.cb = [A[:, o + 2112 * i + 2048:o + 2112 * i + 2112] for i in range(2)]
                assert o + 4224 <= ARENA

            def loads(self, sp):
                sp.dma_start(self.at, t["attr"].rearrange("(p q) f -> p (q f)", p=EP)).then_inc(self.s_ld, 16)
                sp.dma_start(self.w1, t["L3_gnn_ee_w1"]).then_inc(self.s_ld, 16)
                for d, n in ((self.g1, "g1"), (self.bb1, "bb1"), (self.b1, "b1")):
                    sp.dma_start(d, t["L3_gnn_ee_" + n].partition_broadcast(17)).then_inc(self.s_ld, 16)
                for i in range(2):
                    sp.dma_start(self.v[i].rearrange("i (b o) -> i b o", b=R_REL),
                                 t[f"L1_gnn_V{i + 1}"].rearrange("b i o -> i b o")).then_inc(self.s_wl, 16)
                    bcast_load(sp, self.cb[i], t[f"L1_gnn_comp{i + 1}"].rearrange("r b -> (r b)")).then_inc(self.s_wl, 16)

            def stores(self, sp):
                sp.wait_ge(self.s_row, 1)
                sp.dma_start(small[16:17, 0:D], self.row).then_inc(self.s_row2, 16)
                for i in range(2):
                    sp.wait_ge(self.s_wr, i + 1)
                    sp.dma_start(rel_w[i], self.wr[i]).then_inc(self.s_ws, 16)
                sp.wait_ge(self.s_row2, 16)
                sp.wait_ge(self.s_ws, 32)

            def scalar(self, act):
                act.wait_ge(self.s_var, 1)
                nc.scalar.activation(self.std, self.var, ACT.Sqrt).then_inc(self.s_std, 1)

            def tensor(self, pe):
                def column_sums():
                    pe.wait_ge(self.s_ld, 80)
                    for c in range(25):
                        ins = nc.tensor.matmul(PS[:, 1024:1536], ones[0:EP, :], self.at[:, c * 512:(c + 1) * 512],
                                               start=(c == 0), stop=(c == 24))
                    ins.then_inc(self.s_m, 1)

                def gram():
                    pe.wait_ge(self.s_cen, 1)
                    for c in range(100):
                        a = self.at[:, c * P:(c + 1) * P]
                        ins = nc.tensor.matmul(PS[:, 1536:1536 + P], a, a, start=(c == 0), stop=(c == 99))
                    ins.then_inc(self.s_g, 1)

                def variances():
                    pe.wait_ge(self.s_gm, 1)
                    nc.tensor.matmul(PS[0:16, 2048:2048 + P], self.selm, self.gm, start=True, stop=True
                                     ).then_inc(self.s_r, 1)
                    pe.wait_ge(self.s_rc, 1)
                    nc.tensor.matmul(PS[0:16, 2560:2560 + D], self.cov, self.w1, start=True, stop=True
                                     ).then_inc(self.s_t, 1)
                    pe.wait_ge(self.s_tw, 1)
                    nc.tensor.matmul(PS[0:16, 3072:3072 + D], ones[0:16, 0:16], self.tw, start=True, stop=True
                                     ).then_inc(self.s_v, 1)
                    nc.tensor.matmul(PS[0:1, 3584:3584 + D], self.mcol, self.w1, start=True, stop=True
                                     ).then_inc(self.s_mr, 1)

                return column_sums, lambda: None, gram, lambda: None, variances

            def vector(self, dve):
                ch = Chain("e_c", dve)
                mean, std, row, cov = self.mean, self.std, self.row, self.cov

                def masks():
                    ch(dve.tensor_copy(self.ri, iota_row[:]))
                    ch(dve.tensor_copy(self.pi, pidx[:, 0:1].to_broadcast([P, P])))
                    ch(dve.tensor_scalar(self.fi, self.pi, 15, None, ALU.bitwise_and))
                    dve.tensor_copy(self.qf, self.fi)
                    ch(dve.tensor_copy(self.rf, self.ri))
                    ch(dve.tensor_tensor(self.selm, self.qf[:, 0:16], self.rf[:, 0:16], ALU.is_equal))
                    ch(dve.tensor_scalar(self.ri, self.ri, 4, None, ALU.arith_shift_right))
                    ch(dve.tensor_scalar(self.pi, self.pi, 4, None, ALU.arith_shift_right))
                    dve.tensor_copy(self.pf, self.pi)
                    ch(dve.tensor_copy(self.rf, self.ri))
                    ch(dve.tensor_tensor(self.bm, self.pf, self.rf, ALU.is_equal))

                def centre():
                    dve.wait_ge(self.s_m, 1)
                    ch(dve.tensor_reduce(mean, PS[:, 1024:1536].rearrange("p (q f) -> p f q", f=16), AX_X, ALU.add))
                    ch(dve.tensor_scalar(mean, mean, 1.0 / E, None, ALU.mult))
                    ch(dve.tensor_tensor(self.dm, mean[0:16, :], ident[0:16, 0:16], ALU.mult))
                    ch(dve.tensor_reduce(self.mcol, self.dm, AX_X, ALU.add))
                    a3 = self.at.rearrange("p (q f) -> p q f", f=16)
                    dve.tensor_tensor(a3, a3, bc_mid(mean[0:EP, :], EQ), ALU.subtract).then_inc(self.s_cen, 1)

                def relation_weights(i, first, last):
                    dve.wait_ge(self.s_wl, 64)
                    for b in range(first, last):
                        for r in range(R_REL):
                            o, src = self.wr[i][:, r * D:(r + 1) * D], self.v[i][:, b * D:(b + 1) * D]
                            c = self.cb[i][:, r * R_REL + b:r * R_REL + b + 1]
                            if b == 0:
                                ins = dve.tensor_scalar(o, src, c, None, ALU.mult)
                            else:
                                ins = dve.scalar_tensor_tensor(o, src, c, o, ALU.mult, ALU.add)
                        if b < R_REL - 1:
                            ch(ins)
                    if last == R_REL:
                        ins.then_inc(self.s_wr, 1)

                def fold():
                    dve.wait_ge(self.s_g, 1)
                    dve.tensor_tensor(self.gm, PS[:, 1536:1536 + P], self.bm, ALU.mult).then_inc(self.s_gm, 1)
                    dve.wait_ge(self.s_r, 1)
                    ch(dve.tensor_reduce(cov, PS[0:16, 2048:2048 + P].rearrange("p (b f) -> p f b", f=16), AX_X,
                                         ALU.add))
                    dve.tensor_scalar(cov, cov, 1.0 / E, None, ALU.mult).then_inc(self.s_rc, 1)
                    dve.wait_ge(self.s_t, 1)
                    dve.tensor_tensor(self.tw, PS[0:16, 2560:2560 + D], self.w1, ALU.mult).then_inc(self.s_tw, 1)
                    dve.wait_ge(self.s_v, 1)
                    dve.tensor_scalar(self.var, PS[0:16, 3072:3072 + D], LN_EPS, None, ALU.add).then_inc(self.s_var, 1)
                    dve.wait_ge(self.s_std, 1)
                    ch(dve.reciprocal(std, std))
                    ch(dve.tensor_tensor(std, std, self.g1[0:16, :], ALU.mult))
                    dve.tensor_tensor(EW[0:16, :], self.w1, std, ALU.mult)
                    dve.wait_ge(self.s_mr, 1)
                    ch(dve.tensor_tensor(row, PS[0:1, 3584:3584 + D], self.b1[0:1, :], ALU.add))
                    ch(dve.tensor_tensor(row, self.b1[0:1, :], row, ALU.subtract))
                    ch(dve.tensor_tensor(row, row, std[0:1, :], ALU.mult))
                    dve.tensor_tensor(row, row, self.bb1[0:1, :], ALU.add).then_inc(self.s_row, 1)

                return (masks, centre, lambda: relation_weights(0, 0, 4), lambda: relation_weights(0, 4, 8), fold,
                        lambda: relation_weights(1, 0, 4), lambda: relation_weights(1, 4, 8))

        class EdgeSumAside:

            def __init__(self, ACC, base):
                self.s_w, self.s_h, self.s_t, self.s_te, self.s_mm, self.s_me, self.s_o = (
                    sem("f_" + x) for x in ("w", "h", "t", "te", "mm", "me", "o"))
                self.a3 = ACC.rearrange("p (t f) -> p t f", f=257)[:, :, D:257]
                self.F, self.FT, self.S = (A[:, base + NW * i:base + NW * (i + 1)] for i in range(3))
                o = base + 3 * NW
                self.w2, self.b2 = A[:, o:o + D], A[:, o + D:o + 2 * D]
                assert o + 2 * D <= ARENA

            def loads(self, sp):
                sp.dma_start(self.w2, t["L3_gnn_ee_w2"]).then_inc(self.s_w, 16)
                bcast_load(sp, self.b2, t["L3_gnn_ee_b2"]).then_inc(self.s_w, 16)

            def stores(self, sp):
                sp.wait_ge(self.s_me, 7)
                sp.dma_start(edge_sum, self.S).then_inc(self.s_o, 16)
                sp.wait_ge(self.s_o, 16)

            def tensor(self, pe):
                def products():
                    pe.wait_ge(self.s_w, 32)
                    pe.wait_ge(self.s_h, 1)
                    for g in range(8):
                        if g < 7:
                            if g >= 2:
                                pe.wait_ge(self.s_te, g - 1)
                            for a in range(4 * g, min(4 * g + 4, NT)):
                                b = 2048 + (g % 2) * 512 + (a % 4) * P
                                ins = nc.tensor.transpose(PS[:, b:b + P], self.F[:, a * D:(a + 1) * D], ident[:])
                            ins.then_inc(self.s_t, 1)
                        if g > 0:
                            c = g - 1
                            pe.wait_ge(self.s_te, c + 1)
                            if c >= 2:
                                pe.wait_ge(self.s_me, c - 1)
                            for a in range(4 * c, min(4 * c + 4, NT)):
                                b = 3072 + (c % 2) * 512 + (a % 4) * P
                                ins = nc.tensor.matmul(PS[:, b:b + P], self.FT[:, a * P:(a + 1) * P], self.w2,
                                                       start=True, stop=True)
                            ins.then_inc(self.s_mm, 1)

                return (products,)

            def scalar(self, act):
                for g in range(7):
                    lo, hi = 512 * g, min(512 * g + 512, NP)
                    act.wait_ge(self.s_t, g + 1)
                    b = 2048 + (g % 2) * 512
                    nc.scalar.copy(self.FT[:, lo:hi], PS[:, b:b + hi - lo]).then_inc(self.s_te, 1)

            def vector(self, dve):
                def add_up():
                    ch = Chain("f_c", dve)
                    dve.wait_ge(self.s_w, 32)
                    dve.tensor_copy(v3(self.F), self.a3[:, :, 0:D]).then_inc(self.s_h, 1)
                    ch(dve.tensor_tensor(v3(self.S), bc_in(self.a3[:, :, D], D), bc_mid(self.b2, NT), ALU.mult))
                    for g in range(7):
                        lo, hi = 512 * g, min(512 * g + 512, NP)
                        b = 3072 + (g % 2) * 512
                        dve.wait_ge(self.s_mm, g + 1)
                        dve.tensor_tensor(self.S[:, lo:hi], self.S[:, lo:hi], PS[:, b:b + hi - lo], ALU.add
                                          ).then_inc(self.s_me, 1)

                return (add_up,)

        def stage_gin_layer(name, Z, w_ap, vecs, last):
            s_w, s_h, s_t, s_te, s_mm, s_out, s_st = (sem(name + x) for x in ("_w", "_h", "_t", "_te", "_mm", "_out", "_st"))
            bn = bn_sems(name)
            o = NW
            SQ = A[:, o:o + NW]
            o += NW
            w, b, gam, bet, mean, var, std = (A[:, o + D * i:o + D * (i + 1)] for i in range(7))
            with nc.Block() as block:
                @block.sync
                def _(sp):
                    sp.dma_start(w, w_ap).then_inc(s_w, 16)
                    for d, v in zip((b, gam, bet), vecs):
                        bcast_load(sp, d, v).then_inc(s_w, 16)
                    if last:
                        rows = node_view(out, True)
                        for i, (lo, hi) in enumerate(((0, 12), (12, NT - 1))):
                            sp.wait_ge(s_out, i + 1)
                            sp.dma_start(rows[:, lo:hi, :], v3(Z[:, lo * D:hi * D])).then_inc(s_st, 16)
                        sp.dma_start(node_view(out, False), Z[0:NLAST, (NT - 1) * D:NW]).then_inc(s_st, 16)
                        sp.wait_ge(s_st, 48)

                @block.tensor
                def _(pe):
                    pe.wait_ge(s_w, 64)
                    transpose_tiles(pe, Z, s_h, s_t)
                    project_tiles(pe, HT, w, s_mm, s_te)
                    bn_tensor(pe, Z, SQ, bn)

                @block.scalar
                def _(act):
                    for g in range(7):
                        lo, hi = 512 * g, min(512 * g + 512, NP)
                        act.wait_ge(s_t, g + 1)
                        nc.scalar.copy(HT[:, lo:hi], PS[:, lo:hi]).then_inc(s_te, 1)
                    bn_scalar(act, Z, SQ, var, std, bn)

                @block.vector
                def _(dve):
                    ch = Chain(name + "_c", dve)
                    for lo, hi in GROUPS:
                        if last:
                            dve.sem_inc(s_h, 1)
                        else:
                            c = slice(lo * D, hi * D)
                            dve.tensor_tensor(Z[:, c], Z[:, c], H[:, c], ALU.add).then_inc(s_h, 1)
                    dve.wait_ge(s_w, 64)
                    dve.wait_ge(s_t, 7)
                    for g, (lo, hi) in enumerate(GROUPS):
                        dve.wait_ge(s_mm, g + 1)
                        c = slice(lo * D, hi * D)
                        dve.tensor_tensor(v3(Z[:, c]), v3(PS[:, c]), bc_mid(b, hi - lo), ALU.add).then_inc(bn[0], 1)
                    dve.wait_ge(bn[0], len(GROUPS))
                    bn_vector(dve, ch, Z, gam, bet, (mean, var, std, bn))
                    if last:
                        half = 12 * D
                        dve.scalar_tensor_tensor(Z[:, 0:half], Z[:, 0:half], 0.0, X[:, 0:half], ALU.max, ALU.add
                                                 ).then_inc(s_out, 1)
                        dve.scalar_tensor_tensor(Z[:, half:NW], Z[:, half:NW], 0.0, X[:, half:NW], ALU.max, ALU.add
                                                 ).then_inc(s_out, 1)
                    else:
                        ch(dve.tensor_scalar(Z, Z, 0.0, None, ALU.max))

        stage_setup()
        end_stage()
        stage_norm("n0")
        end_stage()
        ad = stage_gat_table()
        end_stage()
        stage_scores("a0", 8, tab0, 136, ad, 8, spill0, aside=WeightsAside(8896))
        end_stage()
        stage_softmax("x0", 8)
        end_stage()
        ACC = stage_aggregate("s0", (0, NT * 136), [136], heads=8, spill=spill0, width=136)
        end_stage()
        stage_gat_end(ACC)
        end_stage()
        stage_norm("n1")
        end_stage()
        stage_rel_table("r1", 0, 16384)
        end_stage()
        ACC = stage_aggregate("s1", (0, NT * 257), [257], table=tab_rel, idx=idx_rel, edge_w=EW)
        end_stage()
        stage_rel_end("b1", ACC, t["L1_gnn_bias1"], True)
        end_stage()
        stage_rel_table("r2", 1, 16384)
        end_stage()
        NS = 257 * NT
        ACC = stage_aggregate("s2", (NS, NS + NW), [D], table=tab_rel, idx=idx_rel, weighted=True,
                              aside=EdgeSumAside(ACC, 16384))
        end_stage()
        stage_rel_end("b2", ACC, t["L1_gnn_bias2"], False)
        end_stage()
        stage_norm("n2")
        end_stage()
        U = stage_queries()
        end_stage()
        stage_scores("a2", 4, tab_x, 129, U, 516, spill2)
        end_stage()
        stage_softmax("x2", 4)
        end_stage()
        ACC = stage_aggregate("s3", (0, NT * 516), [258, 258], heads=4, spill=spill2, width=129)
        end_stage()
        stage_transformer_end(ACC)
        end_stage()
        stage_norm("n3", table=True)
        end_stage()
        ACC = stage_aggregate("s5", (0, NW), [D], table=tab_h, idx=idx_src)
        end_stage()
        stage_gin_layer("m1", ACC, t["L3_gnn_mlp_w1"], [t["L3_gnn_mlp_" + v] for v in ("b1", "g1", "bb1")], False)
        end_stage()
        stage_gin_layer("m2", ACC, t["L3_gnn_mlp_w2"], [t["L3_gnn_mlp_" + v] for v in ("b2", "g2", "bb2")], True)
        end_stage()


def kernel(x, src, dst, edge_attr_16, edge_type_8, edge_weight, **weights):
    import numpy as np
    import concourse.bacc as bacc
    from concourse.bass_utils import run_bass_kernel_spmd

    arrays = {k: np.ascontiguousarray(v) for k, v in weights.items() if k not in (
        "L2_gnn_Wk", "L2_gnn_bq", "L2_gnn_bk")}
    pad = ST * SUPER - E

    def rows(a, fill):
        a = np.asarray(a)
        return np.concatenate([a, np.full((pad,) + a.shape[1:], fill, a.dtype)]).reshape((ST, SUPER) + a.shape[1:])

    arrays["x"] = np.ascontiguousarray(x)
    arrays["dst"] = rows(dst, NP)
    arrays["src"] = rows(src, 0)
    arrays["etype"] = rows(edge_type_8, 0)
    arrays["weight"] = rows(edge_weight, 0)
    arrays["attr"] = np.ascontiguousarray(edge_attr_16)
    arrays["attr_t"] = np.ascontiguousarray(rows(edge_attr_16, 0).reshape(2 * ST, P, 16).transpose(0, 2, 1))
    wk = np.asarray(weights["L2_gnn_Wk"]).reshape(D, 4, D).transpose(2, 1, 0)
    bk = np.asarray(weights["L2_gnn_bk"]).reshape(4, D).T
    arrays["wkb_t"] = np.ascontiguousarray(np.concatenate([wk, bk[:, :, None]], axis=2).reshape(D, 4 * (D + 1)))
    arrays["bq_t"] = np.ascontiguousarray(np.asarray(weights["L2_gnn_bq"]).reshape(4, D).T)
    nc = bacc.Bacc("TRN2", target_bir_lowering=False, num_devices=1)
    t, feed = {}, {}
    for name, a in arrays.items():
        feed["in_" + name] = a
        t[name] = nc.dram_tensor("in_" + name, a.shape, mybir.dt.from_np(a.dtype), kind="ExternalInput").ap()
    out = nc.dram_tensor("out", [N, D], F32, kind="ExternalOutput").ap()
    build(nc, t, out)
    r = run_bass_kernel_spmd(nc, [feed], core_ids=[0])
    return r.results[0]["out"]
```
